# Optimizing a Trainium2 kernel written in Bass

```python
import numpy as np
import jax
import jax.numpy as jnp

def _softmax(x, axis=-1):
    return jax.nn.softmax(x, axis=axis)
def _gelu(x):
    return jax.nn.gelu(x, approximate=True)
def _silu(x):
    return jax.nn.silu(x)
def _sigmoid(x):
    return jax.nn.sigmoid(x)
def _layernorm(x, axis=-1, eps=1e-5):
    m = jnp.mean(x, axis=axis, keepdims=True)
    v = jnp.var(x, axis=axis, keepdims=True)
    return (x - m) / jnp.sqrt(v + eps)
def _scatter_add(tgt, idx, src, axis=0):
    return tgt.at[idx].add(src)
def _segment_sum(src, seg, n):
    return jax.ops.segment_sum(src, seg, n)

kernel_name = 'mk_adj_resnorm_d4_adj_128_a78b43'

def setup_inputs(seed: int = 0):
    np.random.seed(seed)
    _w = jnp.asarray
    def _rec_inputs():
        import jax
        import jax.numpy as jnp
        _gk = jax.random.key(seed)
        x = -0.0002928 + 1 * jax.random.normal(jax.random.fold_in(_gk, 1), (32, 512, 128), jnp.float32)
        _w = (1.0 + jnp.arange(512, dtype=jnp.float32)) ** -0.5
        _w = _w / _w.mean()
        _pij = jnp.clip(0.015625 * _w[:, None] * _w[None, :], 0.0, 1.0)
        _a = jax.random.uniform(jax.random.fold_in(_gk, 2), (512, 512)) < _pij
        _a = jnp.logical_or(_a, jnp.eye(512, dtype=bool))
        _af = _a.astype(jnp.float32)
        adj = _af
        return x, adj
    x, adj = _rec_inputs()
    def _L0_gnn_setup():
        import jax, jax.numpy as jnp
        import numpy as np
        B, N, D = (4, 8192, 128)
        key = jax.random.key(seed)
        kx, ka, kq, kk, kv = jax.random.split(key, 5)
        x = jax.random.normal(kx, (B, N, D), dtype=jnp.float32)
        mask = (jax.random.uniform(ka, (N, N)) < 0.05).astype(jnp.float32)
        A_shape = jnp.clip(mask + jnp.eye(N, dtype=jnp.float32), 0.0, 1.0)
        q = jax.random.normal(kq, (D, D), dtype=jnp.float32)
        k = jax.random.normal(kk, (D, D), dtype=jnp.float32)
        v = jax.random.normal(kv, (D, D), dtype=jnp.float32)
        return {'x': x, 'A_shape': A_shape, 'q': q, 'k': k, 'v': v}
    _L0_gnn_all = _L0_gnn_setup()
    _L0_gnn_in = {k: v for k, v in _L0_gnn_all.items() if k in ('q', 'k', 'v', )}
    del _L0_gnn_all

    def _L1_gnn_setup():
        import jax, jax.numpy as jnp
        import numpy as np
        ALPHA = 0.005

        def _linear_init(key, fan_in, shape):
            bound = 1.0 / np.sqrt(fan_in)
            return jax.random.uniform(key, shape, jnp.float32, -bound, bound)
        key = jax.random.key(seed)
        ks = jax.random.split(key, 12)
        B, N, NI, NH, NO = (4, 512, 128, 128, 128)
        x = jax.random.normal(ks[0], (B, N, NI), jnp.float32)
        adj = (jax.random.uniform(ks[1], (N, N)) < 0.05).astype(jnp.float32)
        Wi = _linear_init(ks[2], NI, (NI, NH))
        bi = _linear_init(ks[3], NI, (NH,))
        We = _linear_init(ks[4], 2 * NH, (2 * NH, 1))
        be = _linear_init(ks[5], 2 * NH, (1,))
        Wn = _linear_init(ks[6], 2 * NH, (2 * NH, NO))
        bn = _linear_init(ks[7], 2 * NH, (NO,))
        Wm = _linear_init(ks[8], 2 * NH, (2 * NH, NO))
        bm = _linear_init(ks[9], 2 * NH, (NO,))
        return {'x': x, 'adj': adj, 'Wi': Wi, 'bi': bi, 'We': We, 'be': be, 'Wn': Wn, 'bn': bn, 'Wm': Wm, 'bm': bm}
    _L1_gnn_all = _L1_gnn_setup()
    _L1_gnn_in = {k: v for k, v in _L1_gnn_all.items() if k in ('Wi', 'bi', 'We', 'be', 'Wn', 'bn', 'Wm', 'bm', )}
    del _L1_gnn_all

    def _L2_gnn_setup():
        import jax, jax.numpy as jnp
        import numpy as np
        B, N, CIN, COUT, K = (16384, 17, 128, 128, 3)

        def _cheb_basis(adj):
            n = adj.shape[0]
            d_inv_sqrt = jnp.sum(adj, axis=-1) ** (-0.5)
            eye = jnp.eye(n, dtype=adj.dtype)
            L = eye - d_inv_sqrt[:, None] * adj * d_inv_sqrt[None, :]
            T2 = 2.0 * (L @ L) - eye
            return jnp.stack([eye, L, T2])
        key = jax.random.key(seed)
        kx, ka, kw = jax.random.split(key, 3)
        x = jax.random.normal(kx, (B, N, CIN), dtype=jnp.float32)
        adj = jax.random.uniform(ka, (N, N), dtype=jnp.float32)
        weight = jax.random.normal(kw, (K, 1, CIN, COUT), dtype=jnp.float32) * 0.05
        bias = jnp.zeros((1, 1, COUT), dtype=jnp.float32)
        return {'x': x, 'adj': adj, 'weight': weight, 'bias': bias}
    _L2_gnn_all = _L2_gnn_setup()
    _L2_gnn_in = {k: v for k, v in _L2_gnn_all.items() if k in ('weight', 'bias', )}
    del _L2_gnn_all

    def _L3_gnn_setup():
        import jax, jax.numpy as jnp
        import numpy as np
        B, N, D = (32, 1024, 128)
        TIME_STEP = 5
        key = jax.random.key(seed)
        ks = jax.random.split(key, 12)
        s2 = 1.0 / np.sqrt(2 * D)
        s1 = 1.0 / np.sqrt(D)
        return {'input': jax.random.normal(ks[0], (B, N, D), jnp.float32), 'in_matrix': jax.random.uniform(ks[1], (N, N), jnp.float32), 'out_matrix': jax.random.uniform(ks[2], (N, N), jnp.float32), 'w3_w': jax.random.normal(ks[3], (D, 2 * D), jnp.float32) * s2, 'w3_b': jnp.zeros((D,), jnp.float32), 'u3_w': jax.random.normal(ks[4], (D, D), jnp.float32) * s1, 'u3_b': jnp.zeros((D,), jnp.float32), 'w4_w': jax.random.normal(ks[5], (D, 2 * D), jnp.float32) * s2, 'w4_b': jnp.zeros((D,), jnp.float32), 'w5_w': jax.random.normal(ks[6], (D, 2 * D), jnp.float32) * s2, 'w5_b': jnp.zeros((D,), jnp.float32), 'u5_w': jax.random.normal(ks[7], (D, D), jnp.float32) * s1, 'u5_b': jnp.zeros((D,), jnp.float32), 'time_step': TIME_STEP}
    _L3_gnn_all = _L3_gnn_setup()
    _L3_gnn_in = {k: v for k, v in _L3_gnn_all.items() if k in ('w3_w', 'w3_b', 'u3_w', 'u3_b', 'w4_w', 'w4_b', 'w5_w', 'w5_b', 'u5_w', 'u5_b', )}
    del _L3_gnn_all

    return {
        "x": x,
        "adj": adj,
        "L0_gnn_q": _L0_gnn_in["q"],
        "L0_gnn_k": _L0_gnn_in["k"],
        "L0_gnn_v": _L0_gnn_in["v"],
        "L1_gnn_Wi": _L1_gnn_in["Wi"],
        "L1_gnn_bi": _L1_gnn_in["bi"],
        "L1_gnn_We": _L1_gnn_in["We"],
        "L1_gnn_be": _L1_gnn_in["be"],
        "L1_gnn_Wn": _L1_gnn_in["Wn"],
        "L1_gnn_bn": _L1_gnn_in["bn"],
        "L1_gnn_Wm": _L1_gnn_in["Wm"],
        "L1_gnn_bm": _L1_gnn_in["bm"],
        "L2_gnn_weight": _L2_gnn_in["weight"],
        "L2_gnn_bias": _L2_gnn_in["bias"],
        "L3_gnn_w3_w": _L3_gnn_in["w3_w"],
        "L3_gnn_w3_b": _L3_gnn_in["w3_b"],
        "L3_gnn_u3_w": _L3_gnn_in["u3_w"],
        "L3_gnn_u3_b": _L3_gnn_in["u3_b"],
        "L3_gnn_w4_w": _L3_gnn_in["w4_w"],
        "L3_gnn_w4_b": _L3_gnn_in["w4_b"],
        "L3_gnn_w5_w": _L3_gnn_in["w5_w"],
        "L3_gnn_w5_b": _L3_gnn_in["w5_b"],
        "L3_gnn_u5_w": _L3_gnn_in["u5_w"],
        "L3_gnn_u5_b": _L3_gnn_in["u5_b"],
    }

def reference(x, adj, L0_gnn_q, L0_gnn_k, L0_gnn_v, L1_gnn_Wi, L1_gnn_bi, L1_gnn_We, L1_gnn_be, L1_gnn_Wn, L1_gnn_bn, L1_gnn_Wm, L1_gnn_bm, L2_gnn_weight, L2_gnn_bias, L3_gnn_w3_w, L3_gnn_w3_b, L3_gnn_u3_w, L3_gnn_u3_b, L3_gnn_w4_w, L3_gnn_w4_b, L3_gnn_w5_w, L3_gnn_w5_b, L3_gnn_u5_w, L3_gnn_u5_b):
    import jax
    import jax.numpy as jnp
    def _L0_gnn_ref(x, A_shape, q, k, v):
        import jax, jax.numpy as jnp
        import numpy as np
        B, N, D = (4, 8192, 128)
        input_dimension = x.shape[-1]
        Q = x @ q
        K = x @ k
        A = jnp.einsum('bnd,bmd->bnm', Q, K)
        A = A / jnp.sqrt(jnp.float32(input_dimension))
        A = jnp.tanh(A / 8.0) * 8.0
        A = jnp.exp(A) * A_shape
        A = A / jnp.sum(A, axis=-1, keepdims=True)
        out = A @ x @ v
        return out

    def _L1_gnn_ref(x, adj, Wi, bi, We, be, Wn, bn, Wm, bm):
        import jax, jax.numpy as jnp
        import numpy as np
        ALPHA = 0.005

        def _linear_init(key, fan_in, shape):
            bound = 1.0 / np.sqrt(fan_in)
            return jax.random.uniform(key, shape, jnp.float32, -bound, bound)
        H = Wi.shape[1]
        x_h = jax.nn.elu(x @ Wi + bi)
        a_src = x_h @ We[:H, 0]
        a_tgt = x_h @ We[H:, 0]
        e = jax.nn.sigmoid(a_tgt[:, :, None] + a_src[:, None, :] + be[0])
        mask = adj + ALPHA * (1.0 - (adj != 0).astype(adj.dtype))
        e = e * mask
        agg = jnp.einsum('bij,bjh->bih', e, x_h)
        self_part = x_h * jnp.sum(e, axis=-1, keepdims=True)
        recv = jnp.concatenate([agg, self_part], axis=-1)
        recv = jax.nn.elu(recv @ Wn + bn)
        out = jnp.concatenate([recv, x_h], axis=-1) @ Wm + bm
        return out

    def _L2_gnn_ref(x, adj, weight, bias):
        import jax, jax.numpy as jnp
        import numpy as np
        B, N, CIN, COUT, K = (16384, 17, 128, 128, 3)

        def _cheb_basis(adj):
            n = adj.shape[0]
            d_inv_sqrt = jnp.sum(adj, axis=-1) ** (-0.5)
            eye = jnp.eye(n, dtype=adj.dtype)
            L = eye - d_inv_sqrt[:, None] * adj * d_inv_sqrt[None, :]
            T2 = 2.0 * (L @ L) - eye
            return jnp.stack([eye, L, T2])
        mul_L = _cheb_basis(adj)
        h = jnp.einsum('knm,bmc->kbnc', mul_L, x)
        h = jnp.einsum('kbnc,kcd->kbnd', h, weight[:, 0])
        out = jnp.sum(h, axis=0) + bias
        return jax.nn.relu(out)

    def _L3_gnn_ref(input, in_matrix, out_matrix, w3_w, w3_b, u3_w, u3_b, w4_w, w4_b, w5_w, w5_b, u5_w, u5_b, time_step):
        import jax, jax.numpy as jnp
        import numpy as np
        B, N, D = (32, 1024, 128)
        TIME_STEP = 5
        def step(h, _):
            m_in = jnp.einsum('nm,bmd->bnd', in_matrix, h)
            m_out = jnp.einsum('nm,bmd->bnd', out_matrix, h)
            av = jnp.concatenate([m_in, m_out], axis=-1)
            u3 = h @ u3_w.T + u3_b
            z = jax.nn.sigmoid(av @ w3_w.T + w3_b + u3)
            r = jax.nn.sigmoid(av @ w4_w.T + w4_b + u3)
            hv = jnp.tanh(av @ w5_w.T + w5_b + (r * h @ u5_w.T + u5_b))
            h = (1.0 - z) * h + z * hv
            return (h, None)
        h, _ = jax.lax.scan(step, input, None, length=time_step)
        return h

    x = _layernorm(x + _L0_gnn_ref(x, adj, L0_gnn_q, L0_gnn_k, L0_gnn_v), axis=-1)
    x = _layernorm(x + _L1_gnn_ref(x, adj, L1_gnn_Wi, L1_gnn_bi, L1_gnn_We, L1_gnn_be, L1_gnn_Wn, L1_gnn_bn, L1_gnn_Wm, L1_gnn_bm), axis=-1)
    x = _layernorm(x + _L2_gnn_ref(x, adj, L2_gnn_weight, L2_gnn_bias), axis=-1)
    x = _layernorm(x + _L3_gnn_ref(x, adj, adj, L3_gnn_w3_w, L3_gnn_w3_b, L3_gnn_u3_w, L3_gnn_u3_b, L3_gnn_w4_w, L3_gnn_w4_b, L3_gnn_w5_w, L3_gnn_w5_b, L3_gnn_u5_w, L3_gnn_u5_b, 5), axis=-1)
    return x


_drawn_inputs = setup_inputs


def setup_inputs(seed=0):
    import zlib

    import numpy as np

    out = dict(_drawn_inputs(seed))
    spreads = {'L2_gnn_bias': (0.0, 0.1),
     'L3_gnn_w3_b': (0.0, 0.1),
     'L3_gnn_u3_b': (0.0, 0.1),
     'L3_gnn_w4_b': (0.0, 0.8),
     'L3_gnn_w5_b': (0.0, 0.1),
     'L3_gnn_u5_b': (0.0, 0.1)}
    factors = {}
    for name, (base, spread) in spreads.items():
        noise = np.random.default_rng([zlib.crc32(name.encode()), seed]).standard_normal(out[name].shape)
        drawn = base * np.exp(spread * noise) if base else spread * noise
        out[name] = jnp.asarray(drawn.astype(out[name].dtype))
    for name, factor in factors.items():
        out[name] = (out[name] * factor).astype(out[name].dtype)
    return out
```

```python
from contextlib import ExitStack

import concourse.bass as bass
from concourse import mybir

F32 = mybir.dt.float32
F32R = mybir.dt.float32r
ALU = mybir.AluOpType
ACT = mybir.ActivationFunctionType
AX = mybir.AxisListType

P = 128
SLOTS = 4
PAIRS = SLOTS // 2
STEPS = 5
ALPHA = 0.005
EPS = 1e-5

TURNED = {"x0": 1, "x1": 2, "xh": 3, "x2": 4, "x3": 5, **{f"h{k}": 6 + k for k in range(STEPS)}}
XT = {"x0": 1, "x1": 2, "x2": 3, "x3": 4, **{f"h{k}": 5 + k for k in range(STEPS - 1)}}
GT = {"query": 1, "xh": 2, "agg": 3, **{f"m{k}": 4 + k for k in range(STEPS)}}
ST = {"self": 1, **{f"rh{k}": 2 + k for k in range(STEPS)}}
NH = {"x3": 1, **{f"h{k}": 2 + k for k in range(STEPS - 1)}}
PRODUCT = {name: n + 1 for n, name in enumerate(
    ["query", "mix", "sums0", "out0", "xh", "src", "tgt", "agg", "sums1", "recv", "out1"]
    + [f"{name}{k}" for k in range(STEPS) for name in ("m", "r", "z", "hv")])}
PRODUCTS = len(PRODUCT)
VECTOR = {name: n + 1 for n, name in enumerate(
    ["rsum", "elu_low1", "elu1", "src_bias", "self", "elu_low2", "elu2"]
    + [f"{name}{k}" for k in range(STEPS) for name in ("rh", "update", "h")])}
VECTORS = len(VECTOR)
POOL = {name: n + 1 for n, name in enumerate(
    ["half_sum0", "edge_sum0", "std0", "rstd0", "bias1", "half_sum1", "edge_sum1", "std1", "rstd1", "bias2",
     "std2", "rstd2"] + [f"diff{k}" for k in range(STEPS)] + ["std3", "rstd3"])}
POOLS = len(POOL)
NORMS = 4


def build(nc, x, adj, q, k, v, Wi, bi, We, be, Wn, bn, Wm, bm, cheb_w, cheb_b,
          w3_w, w3_b, u3_w, u3_b, w4_w, w4_b, w5_w, w5_b, u5_w, u5_b, out):
    B, N, D = x.shape
    TILES = N // P
    ROUNDS = B // SLOTS
    SCORE_SCALE = 1.0 / (float(D) ** 0.5 * 8.0)
    assert D == P and N == TILES * P and B == ROUNDS * SLOTS

    with ExitStack() as ctx:
        def sb(name, shape, dt=F32):
            return ctx.enter_context(nc.sbuf_tensor(name, shape, dt))

        def sem(name):
            return ctx.enter_context(nc.semaphore(name))

        def sems(name, n=SLOTS):
            return [sem(f"{name}{i}") for i in range(n)]

        ident = sb("ident", [P, P])
        ones = sb("ones", [P, P])
        neg_half = sb("neg_half", [P, TILES])
        eps_cols = sb("eps_cols", [P, TILES])
        adjT = sb("adjT", [P, TILES, N])
        adjT_hi = sb("adjT_hi", [P, TILES, N], F32R)
        adjT_lo = sb("adjT_lo", [P, TILES, N], F32R)
        edge_mask = sb("edge_mask", [P, TILES, N])
        degree = sb("degree", [P, TILES])
        dinv = sb("dinv", [P, TILES])
        neg_dinv = sb("neg_dinv", [P, TILES])
        v_sb = sb("v_sb", [P, D])
        qk_hi, qk_lo = sb("qk_hi", [P, D], F32R), sb("qk_lo", [P, D], F32R)
        Wi_hi, Wi_lo = sb("Wi_hi", [P, D], F32R), sb("Wi_lo", [P, D], F32R)
        We_sb = sb("We_sb", [P, 2])
        Wt_hi, Wt_lo = sb("Wt_hi", [P, P], F32R), sb("Wt_lo", [P, P], F32R)
        Wn_hi, Wn_lo = sb("Wn_hi", [P, 2, D], F32R), sb("Wn_lo", [P, 2, D], F32R)
        Wm_sb = sb("Wm_sb", [P, 2, D])
        C_hi, C_lo = sb("C_hi", [P, 3, D], F32R), sb("C_lo", [P, 3, D], F32R)
        G_W3, G_W4, G_W5, G_U3, G_U5 = range(5)
        Gw_hi, Gw_lo = sb("Gw_hi", [P, 5, D], F32R), sb("Gw_lo", [P, 5, D], F32R)
        bi_sb, bn_sb, be_sb = sb("bi_sb", [P, 1]), sb("bn_sb", [P, 1]), sb("be_sb", [P, 1])
        bm_rows, cb_rows = sb("bm_rows", [P, D]), sb("cb_rows", [P, D])
        gate_bias = sb("gate_bias", [P, 5])
        z_bias, r_bias, hv_bias = sb("z_bias", [P, 1]), sb("r_bias", [P, 1]), sb("hv_bias", [P, 1])

        def per_slot(name, shape, dt=F32):
            return [sb(f"{name}{s}", shape, dt) for s in range(SLOTS)]

        xin = per_slot("xin", [P, TILES, D])
        X_pair = [sb(f"X{i}", [P, 2, TILES, D]) for i in range(PAIRS)]
        X = [X_pair[s // 2][:, s % 2] for s in range(SLOTS)]
        xT_hi, xT_lo = per_slot("xT_hi", [P, N], F32R), per_slot("xT_lo", [P, N], F32R)
        gT_hi, gT_lo = per_slot("gT_hi", [P, N], F32R), per_slot("gT_lo", [P, N], F32R)
        sT_hi, sT_lo = per_slot("sT_hi", [P, N], F32R), per_slot("sT_lo", [P, N], F32R)
        E_pair = [sb(f"E{i}", [P, 2, TILES, N]) for i in range(PAIRS)]
        E = [E_pair[s // 2][:, s % 2] for s in range(SLOTS)]
        S = per_slot("S", [P, 2, N])
        U = per_slot("U", [P, N])
        H = per_slot("H", [P, N])
        stat = per_slot("stat", [P, TILES, 6])
        mv = per_slot("mv", [P, 3, TILES])
        rstd = per_slot("rstd", [P, TILES])
        rsum = per_slot("rsum", [P, TILES])
        src_bias = per_slot("src_bias", [P, TILES])
        nh_hi = [sb(f"nh_hi{i}", [P, TILES, 2, D], F32R) for i in range(PAIRS)]
        nh_lo = [sb(f"nh_lo{i}", [P, TILES, 2, D], F32R) for i in range(PAIRS)]

        psA = [ctx.enter_context(nc.psum_tensor(f"psA{s}", [P, N], F32)) for s in range(SLOTS)]
        psB = [ctx.enter_context(nc.psum_tensor(f"psB{s}", [P, N], F32)) for s in range(SLOTS)]

        adj_in = E[0]
        stage_w3 = E[1][:, :, :].rearrange("p t n -> p (t n)")
        w_in = stage_w3[:, 0:6 * D].rearrange("p (g h d) -> p g h d", g=3, h=2)
        w_sum = stage_w3[:, 6 * D:9 * D].rearrange("p (g d) -> p g d", g=3)
        u_in = stage_w3[:, 9 * D:11 * D].rearrange("p (g d) -> p g d", g=2)
        qk_in = stage_w3[:, 11 * D:13 * D].rearrange("p (g d) -> p g d", g=2)
        qkT = stage_w3[:, 13 * D:15 * D].rearrange("p (g d) -> p g d", g=2)
        stage_c = E[2][:, :, :].rearrange("p t n -> p (t n)")
        c_in = stage_c[:, 0:3 * D].rearrange("p (g d) -> p g d", g=3)
        c_sum = stage_c[:, 3 * D:6 * D].rearrange("p (g d) -> p g d", g=3)
        Wi_in = stage_c[:, 6 * D:7 * D]
        Wn_in = stage_c[:, 7 * D:9 * D].rearrange("p (g d) -> p g d", g=2)
        tgt_cols = stage_c[:, 9 * D:10 * D]
        five = stage_c[:, 10 * D:15 * D].rearrange("p (g d) -> p g d", g=5)

        keep_pair = [E_pair[i][:, :, 0:2, :].rearrange("p o a (t c) -> p o (a t) c", c=2 * D) for i in range(PAIRS)]
        cheb_keep = [keep_pair[s // 2][:, s % 2] for s in range(SLOTS)]
        r_gate = [E[s][:, 0, :] for s in range(SLOTS)]
        z_gate = [E[s][:, 1, :] for s in range(SLOTS)]
        h_new = [E[s][:, 2, :] for s in range(SLOTS)]
        rh = [E[s][:, 3, :] for s in range(SLOTS)]

        s_adj, s_qk, s_gru, s_cheb, s_small = sem("s_adj"), sem("s_qk"), sem("s_gru"), sem("s_cheb"), sem("s_small")
        s_const, s_ident0, s_ident = sem("s_const"), sem("s_ident0"), sem("s_ident")
        s_setup_turned, s_setup_qkT, s_setup_qk = sem("s_setup_turned"), sem("s_setup_qkT"), sem("s_setup_qk")
        s_sum, s_degree, s_dinv, s_setup, dve_step = sem("s_sum"), sem("s_degree"), sem("s_dinv"), sem("s_setup"), sem("dve_step")
        loaded, stored = sems("loaded"), sems("stored")
        turned = sems("turned")
        scores_ready = sems("scores_ready")
        product = sems("product")
        cheb_ready = sems("cheb_ready")
        lap_ready = sems("lap_ready", PAIRS)
        xT_hi_ready, gT_hi_ready, sT_hi_ready, nh_hi_ready = sems("xT_hi_ready"), sems("gT_hi_ready"), sems("sT_hi_ready"), sems("nh_hi_ready")
        tanh_done = sems("tanh_done")
        exp_done = sems("exp_done")
        gate_done = sems("gate_done")
        copied = sems("copied")
        cheb_kept = sems("cheb_kept")
        cheb_hi_ready = sems("cheb_hi_ready")
        lap_hi_ready = sems("lap_hi_ready", PAIRS)
        r_done, z_done, hv_done = sems("r_done"), sems("z_done"), sems("hv_done")
        xT_lo_ready, gT_lo_ready, sT_lo_ready, nh_lo_ready = sems("xT_lo_ready"), sems("gT_lo_ready"), sems("sT_lo_ready"), sems("nh_lo_ready")
        cheb_lo_ready = sems("cheb_lo_ready")
        lap_lo_ready = sems("lap_lo_ready", PAIRS)
        edges_ready = sems("edges_ready")
        residual = sems("residual")
        var_ready = sems("var_ready")
        vector_done = sems("vector_done")
        normed = sems("normed")
        stats_ready = sems("stats_ready")
        lap_sum = sems("lap_sum", PAIRS)
        cheb_out = sems("cheb_out", PAIRS)
        pool_done = sems("pool_done")

        def col(w):
            return w.rearrange("(p a) -> p a", a=1)

        def rows(w):
            return w.rearrange("(a n) -> a n", a=1).partition_broadcast(P)

        xg = x.rearrange("b (p t) d -> b p t d", t=TILES)
        og = out.rearrange("b (p t) d -> b p t d", t=TILES)

        block = ctx.enter_context(nc.Block())

        @block.sync
        def _(sp):
            for s in range(SLOTS):
                sp.sem_inc(stored[s], 16)
                sp.sem_inc(residual[s], 1)
            sp.dma_start(adj_in[:, :, :], adj.rearrange("(p t) m -> p t m", t=TILES)).then_inc(s_adj, 16)
            sp.dma_start(qk_in[:, 0, :], q).then_inc(s_qk, 16)
            sp.dma_start(qk_in[:, 1, :], k).then_inc(s_qk, 16)
            for s in range(SLOTS):
                sp.dma_start(xin[s][:, :, :], xg[s]).then_inc(loaded[s], 16)
            for g, w in enumerate((w3_w, w4_w, w5_w)):
                sp.dma_start(w_in[:, g, :, :], w.rearrange("p (h d) -> p h d", h=2)).then_inc(s_gru, 16)
            sp.dma_start(u_in[:, 0, :], u3_w).then_inc(s_gru, 16)
            sp.dma_start(u_in[:, 1, :], u5_w).then_inc(s_gru, 16)
            sp.dma_start(c_in[:, :, :], cheb_w.rearrange("k a c d -> c (k a) d")).then_inc(s_cheb, 16)

            def load(r, s):
                sp.wait_ge(residual[s], NORMS * (r - 1) + 2)
                sp.dma_start(xin[s][:, :, :], xg[bass.ds(r * SLOTS + s, 1)].rearrange("a p t d -> p (a t) d")).then_inc(loaded[s], 16)

            def store(r, s):
                sp.wait_ge(normed[s], NORMS * (r + 1))
                sp.dma_start(og[bass.ds(r * SLOTS + s, 1)].rearrange("a p t d -> p (a t) d"), X[s]).then_inc(stored[s], 16)

            with sp.Fori(0, ROUNDS - 1) as r:
                for s in range(SLOTS):
                    load(r + 1, s)
                for s in range(SLOTS):
                    store(r, s)
            for s in range(SLOTS):
                store(ROUNDS - 1, s)
            for s in range(SLOTS):
                sp.wait_ge(stored[s], 16 * (ROUNDS + 1))

        @block.gpsimd
        def _(pool):
            nc.gpsimd.memset(ident[:, :], 0.0).then_inc(s_ident0, 1)
            nc.gpsimd.memset(ones[:, :], 1.0).then_inc(s_const, 1)
            nc.gpsimd.memset(neg_half[:, :], -0.5).then_inc(s_const, 1)
            nc.gpsimd.memset(eps_cols[:, :], EPS).then_inc(s_const, 1)
            pool.wait_ge(s_ident0, 1)
            nc.gpsimd.affine_select(out=ident[:, :], in_=ident[:, :], compare_op=ALU.not_equal, fill=1.0,
                                    base=0, pattern=[[-1, P]], channel_multiplier=1).then_inc(s_ident, 1)
            pool.wait_ge(s_degree, 1)
            pool.wait_ge(s_const, 3)
            nc.gpsimd.tensor_tensor(dinv[:, :], degree[:, :], neg_half[:, :], ALU.pow).then_inc(s_dinv, 1)
            pool.wait_ge(s_small, 16 * 14)
            pool.wait_ge(s_setup, 1)

            def edge_sums(s, r, layer):
                pool.wait_ge(edges_ready[s], 2 * TILES * r + TILES * (layer + 1))
                if layer == 1:
                    pool.wait_ge(product[s], PRODUCTS * r + PRODUCT["sums0"])
                nc.gpsimd.tensor_tensor(S[s][:, :, :], E[s][:, 0:2, :], E[s][:, 2:4, :], ALU.add).then_inc(pool_done[s], 1)
                pool.wait_ge(pool_done[s], POOLS * r + POOL[f"half_sum{layer}"])
                nc.gpsimd.tensor_tensor(S[s][:, 0, :], S[s][:, 0, :], S[s][:, 1, :], ALU.add).then_inc(pool_done[s], 1)

            def norm(s, r, layer):
                pool.wait_ge(var_ready[s], NORMS * r + layer + 1)
                nc.gpsimd.tensor_tensor(rstd[s][:, :], mv[s][:, 1, :], eps_cols[:, :], ALU.add).then_inc(pool_done[s], 1)
                pool.wait_ge(pool_done[s], POOLS * r + POOL[f"std{layer}"])
                nc.gpsimd.tensor_tensor(rstd[s][:, :], rstd[s][:, :], neg_half[:, :], ALU.pow).then_inc(pool_done[s], 1)

            def stage_edges(s, r):
                edge_sums(s, r, 0)

            def stage_att_out(s, r):
                norm(s, r, 0)

            def stage_x1(s, r):
                pool.wait_ge(normed[s], NORMS * r + 1)
                pool.wait_ge(turned[s], 10 * r + TURNED["x1"])
                nc.gpsimd.tensor_tensor(X[s], X[s],
                                        bm_rows[:, :].unsqueeze(1).to_broadcast([P, TILES, D]), ALU.add).then_inc(pool_done[s], 1)

            def stage_gates(s, r):
                edge_sums(s, r, 1)

            def stage_recv_out(s, r):
                norm(s, r, 1)

            def stage_cheb(s, r):
                pool.wait_ge(cheb_kept[s], TILES * (r + 1))
                nc.gpsimd.tensor_tensor(cheb_keep[s][:, :, 0:D], cheb_keep[s][:, :, 0:D],
                                        cb_rows[:, :].unsqueeze(1).to_broadcast([P, TILES, D]), ALU.add).then_inc(pool_done[s], 1)

            def stage_lap2(i, r):
                for s in (2 * i, 2 * i + 1):
                    norm(s, r, 2)

            def stage_v(s, r, k):
                pool.wait_ge(hv_done[s], STEPS * r + k + 1)
                nc.gpsimd.tensor_tensor(h_new[s], h_new[s], H[s][:, :], ALU.subtract).then_inc(pool_done[s], 1)

            def stage_last(s, r):
                norm(s, r, 3)

            with pool.Fori(0, ROUNDS) as r:
                for s in range(SLOTS):
                    stage_edges(s, r)
                for s in range(SLOTS):
                    stage_att_out(s, r)
                for s in range(SLOTS):
                    stage_x1(s, r)
                for s in range(SLOTS):
                    stage_gates(s, r)
                for s in range(SLOTS):
                    stage_recv_out(s, r)
                for s in range(SLOTS):
                    stage_cheb(s, r)
                for i in range(PAIRS):
                    stage_lap2(i, r)
                for k in range(STEPS):
                    for s in range(SLOTS):
                        stage_v(s, r, k)
                for s in range(SLOTS):
                    stage_last(s, r)

        @block.scalar
        def _(act):
            for g, b in enumerate((w3_b, w4_b, w5_b, u3_b, u5_b)):
                act.dma_start(gate_bias[:, g:g + 1], col(b)).then_inc(s_small, 16)
            act.dma_start(bi_sb[:, :], col(bi)).then_inc(s_small, 16)
            act.dma_start(bn_sb[:, :], col(bn)).then_inc(s_small, 16)
            for h in range(2):
                act.dma_start(We_sb[:, h:h + 1], We[h * P:(h + 1) * P, :]).then_inc(s_small, 16)
            act.dma_start(be_sb[:, :], rows(be)).then_inc(s_small, 16)
            act.dma_start(bm_rows[:, :], rows(bm)).then_inc(s_small, 16)
            act.dma_start(cb_rows[:, :], cheb_b.rearrange("a b d -> (a b) d").partition_broadcast(P)).then_inc(s_small, 16)
            act.dma_start(v_sb[:, :], v).then_inc(s_small, 16)
            act.dma_start(Wm_sb[:, :, :], Wm.rearrange("(h p) d -> p h d", h=2)).then_inc(s_small, 16)
            act.dma_start(Wi_in, Wi).then_inc(s_cheb, 16)
            act.dma_start(Wn_in[:, :, :], Wn.rearrange("(h p) d -> p h d", h=2)).then_inc(s_cheb, 16)
            act.wait_ge(s_small, 16 * 14)
            act.wait_ge(s_setup, 1)

            def turn(s, r, name):
                act.wait_ge(turned[s], 10 * r + TURNED[name])
                nc.scalar.copy(xT_hi[s][:, :], psA[s][:, :]).then_inc(xT_hi_ready[s], 1)

            def stage_x0(s, r):
                turn(s, r, "x0")

            def stage_query(s, r):
                act.wait_ge(product[s], PRODUCTS * r + PRODUCT["query"])
                nc.scalar.copy(gT_hi[s][:, :], psB[s][:, :]).then_inc(gT_hi_ready[s], 1)

            def stage_scores(s, r):
                for t in range(TILES):
                    ps = (psA, psB)[t % 2][s]
                    act.wait_ge(scores_ready[s], TILES * r + t + 1)
                    nc.scalar.activation(E[s][:, t, :], ps[:, :], ACT.Tanh, scale=SCORE_SCALE).then_inc(tanh_done[s], 1)
                    act.wait_ge(tanh_done[s], TILES * r + t + 1)
                    nc.scalar.activation(E[s][:, t, :], E[s][:, t, :], ACT.Exp, scale=8.0).then_inc(exp_done[s], 1)

            def stage_mix(s, r):
                act.wait_ge(product[s], PRODUCTS * r + PRODUCT["mix"])
                nc.scalar.copy(U[s][:, :], psA[s][:, :]).then_inc(copied[s], 1)

            def stage_x1(s, r):
                turn(s, r, "x1")

            def stage_xh(s, r):
                act.wait_ge(product[s], PRODUCTS * r + PRODUCT["xh"])
                nc.scalar.activation(U[s][:, :], psB[s][:, :], ACT.Exp, bias=bi_sb[:, :]).then_inc(exp_done[s], 1)
                act.wait_ge(vector_done[s], VECTORS * r + VECTOR["elu1"])
                nc.scalar.copy(gT_hi[s][:, :], H[s][:, :]).then_inc(gT_hi_ready[s], 1)

            def stage_gates(s, r):
                act.wait_ge(vector_done[s], VECTORS * r + VECTOR["src_bias"])
                act.wait_ge(product[s], PRODUCTS * r + PRODUCT["tgt"])
                for t in range(TILES):
                    nc.scalar.activation(E[s][:, t, :], psA[s][:, :], ACT.Tanh, scale=0.5,
                                         bias=src_bias[s][:, t:t + 1]).then_inc(gate_done[s], 1)
                act.wait_ge(turned[s], 10 * r + TURNED["xh"])
                nc.scalar.copy(U[s][:, :], psB[s][:, :]).then_inc(copied[s], 1)

            def stage_agg(s, r):
                act.wait_ge(product[s], PRODUCTS * r + PRODUCT["agg"])
                nc.scalar.copy(gT_hi[s][:, :], psA[s][:, :]).then_inc(gT_hi_ready[s], 1)
                act.wait_ge(vector_done[s], VECTORS * r + VECTOR["self"])
                nc.scalar.copy(sT_hi[s][:, :], S[s][:, 1, :]).then_inc(sT_hi_ready[s], 1)

            def stage_recv(s, r):
                act.wait_ge(product[s], PRODUCTS * r + PRODUCT["recv"])
                nc.scalar.activation(U[s][:, :], psA[s][:, :], ACT.Exp, bias=bn_sb[:, :]).then_inc(exp_done[s], 1)

            def stage_x2(s, r):
                turn(s, r, "x2")

            def stage_cheb(s, r):
                i, o = s // 2, s % 2
                for t in range(TILES):
                    ps = (psA, psB)[t % 2][s]
                    act.wait_ge(cheb_ready[s], TILES * r + t + 1)
                    nc.scalar.copy(cheb_keep[s][:, t, :], ps[:, 0:2 * D]).then_inc(cheb_kept[s], 1)
                    nc.scalar.activation(nh_hi[i][:, t, o, :], ps[:, 2 * D:3 * D], ACT.Copy,
                                         scale=dinv[:, t:t + 1]).then_inc(cheb_hi_ready[s], 1)

            def stage_lap1(i, r):
                act.wait_ge(lap_ready[i], 4 * r + 2)
                for t in range(TILES):
                    act.wait_ge(lap_sum[i], TILES * r + t + 1)
                    nc.scalar.activation(nh_hi[i][:, t, :, :], keep_pair[i][:, :, t, D:2 * D], ACT.Copy,
                                         scale=dinv[:, t:t + 1]).then_inc(lap_hi_ready[i], 1)

            def stage_x3(s, r):
                i, o = s // 2, s % 2
                act.wait_ge(normed[s], NORMS * r + 3)
                nc.scalar.copy(nh_hi[i][:, :, o, :], X[s]).then_inc(nh_hi_ready[s], 1)
                act.wait_ge(turned[s], 10 * r + TURNED["x3"])
                nc.scalar.copy(xT_hi[s][:, :], psA[s][:, :]).then_inc(xT_hi_ready[s], 1)
                nc.scalar.copy(H[s][:, :], psA[s][:, :]).then_inc(copied[s], 1)

            def stage_m(s, r, k):
                act.wait_ge(product[s], PRODUCTS * r + PRODUCT[f"m{k}"])
                nc.scalar.copy(gT_hi[s][:, :], psA[s][:, :]).then_inc(gT_hi_ready[s], 1)

            def stage_rz(s, r, k):
                act.wait_ge(product[s], PRODUCTS * r + PRODUCT[f"r{k}"])
                nc.scalar.activation(r_gate[s], psB[s][:, :], ACT.Tanh, scale=0.5, bias=r_bias[:, :]).then_inc(r_done[s], 1)
                act.wait_ge(vector_done[s], VECTORS * r + VECTOR[f"rh{k}"])
                nc.scalar.copy(sT_hi[s][:, :], rh[s]).then_inc(sT_hi_ready[s], 1)
                act.wait_ge(product[s], PRODUCTS * r + PRODUCT[f"z{k}"])
                nc.scalar.activation(z_gate[s], psA[s][:, :], ACT.Tanh, scale=0.5, bias=z_bias[:, :]).then_inc(z_done[s], 1)

            def stage_v(s, r, k):
                act.wait_ge(product[s], PRODUCTS * r + PRODUCT[f"hv{k}"])
                nc.scalar.activation(h_new[s], psB[s][:, :], ACT.Tanh, bias=hv_bias[:, :]).then_inc(hv_done[s], 1)
                if k < STEPS - 1:
                    act.wait_ge(vector_done[s], VECTORS * r + VECTOR[f"h{k}"])
                    nc.scalar.copy(xT_hi[s][:, :], H[s][:, :]).then_inc(xT_hi_ready[s], 1)

            def stage_t(s, r, k):
                i, o = s // 2, s % 2
                act.wait_ge(turned[s], 10 * r + TURNED[f"h{k}"])
                nc.scalar.copy(nh_hi[i][:, :, o, :], psA[s][:, :].rearrange("p (t d) -> p t d", t=TILES)).then_inc(nh_hi_ready[s], 1)

            with act.Fori(0, ROUNDS) as r:
                for stage in (stage_x0, stage_query, stage_scores, stage_mix, stage_x1, stage_xh, stage_gates,
                              stage_agg, stage_recv, stage_x2, stage_cheb):
                    for s in range(SLOTS):
                        stage(s, r)
                for i in range(PAIRS):
                    stage_lap1(i, r)
                for s in range(SLOTS):
                    stage_x3(s, r)
                for k in range(STEPS):
                    for stage in (stage_m, stage_rz, stage_v):
                        for s in range(SLOTS):
                            stage(s, r, k)
                    if k < STEPS - 1:
                        for s in range(SLOTS):
                            stage_t(s, r, k)

        @block.vector
        def _(dve):
            steps = [0]

            def link(instruction):
                steps[0] += 1
                instruction.then_inc(dve_step, 1)
                dve.wait_ge(dve_step, steps[0])

            def split_const(hi, lo, src):
                link(nc.vector.tensor_copy(hi, src))
                nc.vector.tensor_tensor(lo, src, hi.bitcast(F32), ALU.subtract)

            dve.wait_ge(s_adj, 16)
            nc.vector.tensor_reduce(degree[:, :], adj_in, AX.X, ALU.add).then_inc(s_degree, 1)
            dve.wait_ge(s_gru, 16 * 5)
            nc.vector.tensor_tensor(w_sum, w_in[:, :, 0, :], w_in[:, :, 1, :], ALU.add).then_inc(s_sum, 1)
            dve.wait_ge(s_setup_turned, 1)
            nc.vector.tensor_copy(qkT, psA[0][:, 0:2 * D].rearrange("p (g d) -> p g d", g=2)).then_inc(s_setup_qkT, 1)
            dve.wait_ge(s_setup_turned, 2)
            nc.vector.tensor_copy(five[:, 0:3, :], psA[1][:, 0:3 * D].rearrange("p (g d) -> p g d", g=3))
            nc.vector.tensor_copy(five[:, 3, :], psA[2][:, 0:D])
            link(nc.vector.tensor_scalar(five[:, 4, :], psA[2][:, D:2 * D], 0.5, None, ALU.mult))
            split_const(Gw_hi[:, :, :], Gw_lo[:, :, :], five)
            dve.wait_ge(s_cheb, 16 * 3)
            nc.vector.tensor_tensor(c_sum[:, 0, :], c_in[:, 0, :], c_in[:, 1, :], ALU.add)
            nc.vector.scalar_tensor_tensor(out=c_sum[:, 1, :], in0=c_in[:, 2, :], scalar=4.0, in1=c_in[:, 1, :],
                                           op0=ALU.mult, op1=ALU.add)
            link(nc.vector.tensor_scalar(c_sum[:, 2, :], c_in[:, 2, :], 2.0, None, ALU.mult))
            link(nc.vector.tensor_tensor(c_sum[:, 0, :], c_sum[:, 0, :], c_in[:, 2, :], ALU.add))
            split_const(C_hi[:, :, :], C_lo[:, :, :], c_sum)
            split_const(Wi_hi[:, :], Wi_lo[:, :], Wi_in)
            split_const(Wn_hi[:, :, :], Wn_lo[:, :, :], Wn_in)
            dve.wait_ge(s_small, 16 * 14)
            dve.wait_ge(s_const, 3)
            link(nc.vector.tensor_scalar(tgt_cols, ones[:, :], We_sb[:, 1:2], None, ALU.mult))
            split_const(Wt_hi[:, :], Wt_lo[:, :], tgt_cols)
            nc.vector.tensor_tensor(hv_bias[:, :], gate_bias[:, 2:3], gate_bias[:, 4:5], ALU.add)
            nc.vector.tensor_tensor(z_bias[:, :], gate_bias[:, 0:1], gate_bias[:, 3:4], ALU.add)
            link(nc.vector.tensor_tensor(r_bias[:, :], gate_bias[:, 1:2], gate_bias[:, 3:4], ALU.add))
            nc.vector.tensor_scalar(z_bias[:, :], z_bias[:, :], 0.5, None, ALU.mult)
            nc.vector.tensor_scalar(r_bias[:, :], r_bias[:, :], 0.5, None, ALU.mult)
            dve.wait_ge(s_dinv, 1)
            nc.vector.tensor_scalar(neg_dinv[:, :], dinv[:, :], -1.0, None, ALU.mult)
            for t in range(TILES):
                dve.wait_ge(s_setup_turned, 3 + t)
                link(nc.vector.tensor_copy(adjT[:, t, :], psB[t][:, :]))
            split_const(adjT_hi[:, :, :], adjT_lo[:, :, :], adjT[:, :, :])
            link(nc.vector.tensor_scalar(edge_mask[:, :, :], adjT[:, :, :], 0.0, 0.5 * ALPHA, ALU.is_equal, ALU.mult))
            for t in range(TILES):
                nc.vector.scalar_tensor_tensor(out=edge_mask[:, t, :], in0=adjT[:, t, :], scalar=0.5,
                                               in1=edge_mask[:, t, :], op0=ALU.mult, op1=ALU.add)
            dve.wait_ge(s_setup_qk, 1)
            link(nc.vector.tensor_copy(five[:, 0, :], psA[3][:, 0:D]))
            link(nc.vector.tensor_copy(qk_hi[:, :], five[:, 0, :]))
            nc.vector.tensor_tensor(qk_lo[:, :], five[:, 0, :], qk_hi[:, :].bitcast(F32), ALU.subtract).then_inc(s_setup, 1)
            dve.wait_ge(s_setup, 1)

            def lo_part(lo, src, hi):
                return nc.vector.tensor_tensor(lo, src, hi.bitcast(F32), ALU.subtract)

            def turn(s, r, name):
                dve.wait_ge(xT_hi_ready[s], 8 * r + XT[name])
                lo_part(xT_lo[s][:, :], psA[s][:, :], xT_hi[s][:, :]).then_inc(xT_lo_ready[s], 1)

            def norm(s, r, layer):
                dve.wait_ge(residual[s], NORMS * r + layer + 2)
                for t in range(TILES):
                    last = nc.vector.bn_stats(out=stat[s][:, t, :], in_=X[s][:, t, :])
                last.then_inc(stats_ready[s], 1)
                dve.wait_ge(stats_ready[s], 3 * (NORMS * r + layer) + 1)
                mean_e, m2_e, mean_o, m2_o = (stat[s][:, :, n] for n in (1, 2, 4, 5))
                nc.vector.tensor_tensor(mv[s][:, 0, :], mean_e, mean_o, ALU.add)
                nc.vector.tensor_tensor(mv[s][:, 1, :], m2_e, m2_o, ALU.add)
                nc.vector.tensor_tensor(mv[s][:, 2, :], mean_e, mean_o, ALU.subtract).then_inc(stats_ready[s], 1)
                dve.wait_ge(stats_ready[s], 3 * (NORMS * r + layer) + 2)
                nc.vector.tensor_scalar(mv[s][:, 0, :], mv[s][:, 0, :], 0.5, None, ALU.mult)
                nc.vector.scalar_tensor_tensor(out=mv[s][:, 2, :], in0=mv[s][:, 2, :], scalar=0.25, in1=mv[s][:, 2, :],
                                               op0=ALU.mult, op1=ALU.mult).then_inc(stats_ready[s], 1)
                dve.wait_ge(stats_ready[s], 3 * (NORMS * r + layer) + 3)
                nc.vector.scalar_tensor_tensor(out=mv[s][:, 1, :], in0=mv[s][:, 1, :], scalar=1.0 / D, in1=mv[s][:, 2, :],
                                               op0=ALU.mult, op1=ALU.add).then_inc(var_ready[s], 1)
                dve.wait_ge(pool_done[s], POOLS * r + POOL[f"rstd{layer}"])
                for t in range(TILES):
                    last = nc.vector.tensor_scalar(X[s][:, t, :], X[s][:, t, :], mv[s][:, 0, t:t + 1], rstd[s][:, t:t + 1],
                                                   ALU.subtract, ALU.mult)
                last.then_inc(normed[s], 1)

            def stage_x0(s, r):
                turn(s, r, "x0")

            def stage_query(s, r):
                dve.wait_ge(gT_hi_ready[s], 8 * r + GT["query"])
                lo_part(gT_lo[s][:, :], psB[s][:, :], gT_hi[s][:, :]).then_inc(gT_lo_ready[s], 1)

            def stage_scores(s, r):
                for t in range(TILES):
                    dve.wait_ge(exp_done[s], (TILES + 2) * r + t + 1)
                    nc.vector.tensor_tensor(E[s][:, t, :], E[s][:, t, :], adjT[:, t, :], ALU.mult).then_inc(edges_ready[s], 1)

            def stage_out0(s, r):
                dve.wait_ge(product[s], PRODUCTS * r + PRODUCT["sums0"])
                nc.vector.reciprocal(rsum[s][:, :], psB[s][:, 0:TILES]).then_inc(vector_done[s], 1)
                dve.wait_ge(vector_done[s], VECTORS * r + VECTOR["rsum"])
                dve.wait_ge(product[s], PRODUCTS * r + PRODUCT["out0"])
                dve.wait_ge(stored[s], 16 * (r + 1))
                for t in range(TILES):
                    last = nc.vector.scalar_tensor_tensor(out=X[s][:, t, :], in0=psA[s][:, t * D:(t + 1) * D],
                                                          scalar=rsum[s][:, t:t + 1], in1=xin[s][:, t, :],
                                                          op0=ALU.mult, op1=ALU.add)
                last.then_inc(residual[s], 1)
                norm(s, r, 0)

            def stage_x1(s, r):
                turn(s, r, "x1")

            def elu(s, r, n, ps, bias, dst):
                dve.wait_ge(exp_done[s], (TILES + 2) * r + TILES + n)
                nc.vector.tensor_scalar(U[s][:, :], U[s][:, :], 1.0, -1.0, ALU.min, ALU.add).then_inc(vector_done[s], 1)
                dve.wait_ge(vector_done[s], VECTORS * r + VECTOR[f"elu_low{n}"])
                nc.vector.scalar_tensor_tensor(out=dst, in0=ps, scalar=bias, in1=U[s][:, :],
                                               op0=ALU.add, op1=ALU.max).then_inc(vector_done[s], 1)

            def stage_xh(s, r):
                elu(s, r, 1, psB[s][:, :], bi_sb[:, :], H[s][:, :])
                dve.wait_ge(vector_done[s], VECTORS * r + VECTOR["elu1"])
                dve.wait_ge(gT_hi_ready[s], 8 * r + GT["xh"])
                lo_part(gT_lo[s][:, :], H[s][:, :], gT_hi[s][:, :]).then_inc(gT_lo_ready[s], 1)

            def stage_gates(s, r):
                dve.wait_ge(product[s], PRODUCTS * r + PRODUCT["src"])
                nc.vector.tensor_scalar(src_bias[s][:, :], psB[s][:, 0:TILES], be_sb[:, :], 0.5,
                                        ALU.add, ALU.mult).then_inc(vector_done[s], 1)
                for t in range(TILES):
                    dve.wait_ge(gate_done[s], TILES * r + t + 1)
                    nc.vector.scalar_tensor_tensor(out=E[s][:, t, :], in0=E[s][:, t, :], scalar=1.0, in1=edge_mask[:, t, :],
                                                   op0=ALU.add, op1=ALU.mult).then_inc(edges_ready[s], 1)

            def stage_agg(s, r):
                dve.wait_ge(gT_hi_ready[s], 8 * r + GT["agg"])
                lo_part(gT_lo[s][:, :], psA[s][:, :], gT_hi[s][:, :]).then_inc(gT_lo_ready[s], 1)
                dve.wait_ge(product[s], PRODUCTS * r + PRODUCT["sums1"])
                nc.vector.tensor_tensor(S[s][:, 1, :], psB[s][:, :], H[s][:, :], ALU.mult).then_inc(vector_done[s], 1)
                dve.wait_ge(vector_done[s], VECTORS * r + VECTOR["self"])
                dve.wait_ge(sT_hi_ready[s], 6 * r + ST["self"])
                lo_part(sT_lo[s][:, :], S[s][:, 1, :], sT_hi[s][:, :]).then_inc(sT_lo_ready[s], 1)

            def stage_recv(s, r):
                elu(s, r, 2, psA[s][:, :], bn_sb[:, :], U[s][:, :])

            def stage_out1(s, r):
                dve.wait_ge(product[s], PRODUCTS * r + PRODUCT["out1"])
                dve.wait_ge(pool_done[s], POOLS * r + POOL["bias1"])
                nc.vector.tensor_tensor(X[s], psB[s][:, :].rearrange("p (t d) -> p t d", t=TILES), X[s],
                                        ALU.add).then_inc(residual[s], 1)
                norm(s, r, 1)

            def stage_x2(s, r):
                turn(s, r, "x2")

            def stage_cheb(s, r):
                i, o = s // 2, s % 2
                for t in range(TILES):
                    ps = (psA, psB)[t % 2][s]
                    dve.wait_ge(cheb_hi_ready[s], TILES * r + t + 1)
                    nc.vector.scalar_tensor_tensor(out=nh_lo[i][:, t, o, :], in0=ps[:, 2 * D:3 * D], scalar=dinv[:, t:t + 1],
                                                   in1=nh_hi[i][:, t, o, :].bitcast(F32),
                                                   op0=ALU.mult, op1=ALU.subtract).then_inc(cheb_lo_ready[s], 1)

            def half_bank(ps, t):
                return ps[:, (t % 2) * 2 * D:(t % 2 + 1) * 2 * D].rearrange("p (o d) -> p o d", o=2)

            def stage_lap1(i, r):
                for t in range(TILES):
                    dve.wait_ge(lap_ready[i], 4 * r + t // 2 + 1)
                    keep = keep_pair[i][:, :, t, D:2 * D]
                    nc.vector.scalar_tensor_tensor(out=keep, in0=half_bank(psA[2 * i + t // 2], t), scalar=neg_dinv[:, t:t + 1],
                                                   in1=keep, op0=ALU.mult, op1=ALU.add).then_inc(lap_sum[i], 1)
                for t in range(TILES):
                    dve.wait_ge(lap_hi_ready[i], TILES * r + t + 1)
                    nc.vector.scalar_tensor_tensor(out=nh_lo[i][:, t, :, :], in0=keep_pair[i][:, :, t, D:2 * D],
                                                   scalar=dinv[:, t:t + 1], in1=nh_hi[i][:, t, :, :].bitcast(F32),
                                                   op0=ALU.mult, op1=ALU.subtract).then_inc(lap_lo_ready[i], 1)

            def stage_lap2(i, r):
                for s in (2 * i, 2 * i + 1):
                    dve.wait_ge(pool_done[s], POOLS * r + POOL["bias2"])
                for t in range(TILES):
                    dve.wait_ge(lap_ready[i], 4 * r + 2 + t // 2 + 1)
                    keep = keep_pair[i][:, :, t, 0:D]
                    nc.vector.scalar_tensor_tensor(out=keep, in0=half_bank(psB[2 * i + t // 2], t), scalar=neg_dinv[:, t:t + 1],
                                                   in1=keep, op0=ALU.mult, op1=ALU.add).then_inc(cheb_out[i], 1)
                for o in range(2):
                    s = 2 * i + o
                    dve.wait_ge(cheb_out[i], TILES * (r + 1))
                    nc.vector.scalar_tensor_tensor(out=X[s], in0=cheb_keep[s][:, :, 0:D], scalar=0.0,
                                                   in1=X[s], op0=ALU.max, op1=ALU.add).then_inc(residual[s], 1)
                for o in range(2):
                    norm(2 * i + o, r, 2)

            def stage_x3(s, r):
                i, o = s // 2, s % 2
                dve.wait_ge(normed[s], NORMS * r + 3)
                dve.wait_ge(nh_hi_ready[s], 5 * r + NH["x3"])
                lo_part(nh_lo[i][:, :, o, :], X[s], nh_hi[i][:, :, o, :]).then_inc(nh_lo_ready[s], 1)
                dve.wait_ge(copied[s], 3 * r + 3)
                turn(s, r, "x3")

            def stage_m(s, r, k):
                dve.wait_ge(gT_hi_ready[s], 8 * r + GT[f"m{k}"])
                lo_part(gT_lo[s][:, :], psA[s][:, :], gT_hi[s][:, :]).then_inc(gT_lo_ready[s], 1)

            def stage_rz(s, r, k):
                dve.wait_ge(r_done[s], STEPS * r + k + 1)
                nc.vector.scalar_tensor_tensor(out=rh[s], in0=r_gate[s], scalar=1.0, in1=H[s][:, :],
                                               op0=ALU.add, op1=ALU.mult).then_inc(vector_done[s], 1)
                dve.wait_ge(vector_done[s], VECTORS * r + VECTOR[f"rh{k}"])
                dve.wait_ge(sT_hi_ready[s], 6 * r + ST[f"rh{k}"])
                lo_part(sT_lo[s][:, :], rh[s], sT_hi[s][:, :]).then_inc(sT_lo_ready[s], 1)

            def stage_v(s, r, k):
                dve.wait_ge(pool_done[s], POOLS * r + POOL[f"diff{k}"])
                dve.wait_ge(z_done[s], STEPS * r + k + 1)
                nc.vector.scalar_tensor_tensor(out=h_new[s], in0=z_gate[s], scalar=1.0, in1=h_new[s],
                                               op0=ALU.add, op1=ALU.mult).then_inc(vector_done[s], 1)
                dve.wait_ge(vector_done[s], VECTORS * r + VECTOR[f"update{k}"])
                nc.vector.scalar_tensor_tensor(out=H[s][:, :], in0=h_new[s], scalar=0.5, in1=H[s][:, :],
                                               op0=ALU.mult, op1=ALU.add).then_inc(vector_done[s], 1)
                if k < STEPS - 1:
                    dve.wait_ge(vector_done[s], VECTORS * r + VECTOR[f"h{k}"])
                    dve.wait_ge(xT_hi_ready[s], 8 * r + XT[f"h{k}"])
                    lo_part(xT_lo[s][:, :], H[s][:, :], xT_hi[s][:, :]).then_inc(xT_lo_ready[s], 1)

            def stage_t(s, r, k):
                i, o = s // 2, s % 2
                dve.wait_ge(nh_hi_ready[s], 5 * r + NH[f"h{k}"])
                lo_part(nh_lo[i][:, :, o, :], psA[s][:, :].rearrange("p (t d) -> p t d", t=TILES),
                        nh_hi[i][:, :, o, :]).then_inc(nh_lo_ready[s], 1)

            def stage_last(s, r):
                dve.wait_ge(turned[s], 10 * r + TURNED[f"h{STEPS - 1}"])
                nc.vector.tensor_tensor(X[s], psA[s][:, :].rearrange("p (t d) -> p t d", t=TILES), X[s],
                                        ALU.add).then_inc(residual[s], 1)
                norm(s, r, 3)

            with dve.Fori(0, ROUNDS) as r:
                for stage in (stage_x0, stage_query, stage_scores, stage_out0, stage_x1, stage_xh, stage_gates,
                              stage_agg, stage_recv, stage_out1, stage_x2, stage_cheb):
                    for s in range(SLOTS):
                        stage(s, r)
                for i in range(PAIRS):
                    stage_lap1(i, r)
                for i in range(PAIRS):
                    stage_lap2(i, r)
                for s in range(SLOTS):
                    stage_x3(s, r)
                for k in range(STEPS):
                    for stage in (stage_m, stage_rz, stage_v):
                        for s in range(SLOTS):
                            stage(s, r, k)
                    for s in range(SLOTS):
                        if k < STEPS - 1:
                            stage_t(s, r, k)
                        else:
                            stage_last(s, r)

        @block.tensor
        def _(pe):
            def transpose_tiles(dst, src):
                for t in range(TILES):
                    last = nc.tensor.transpose(dst[:, t * P:(t + 1) * P], src(t), ident[:, :])
                return last

            def three_pass(dst, w_hi, w_lo, m_hi, m_lo, start=True, stop=True):
                nc.tensor.matmul(dst, w_hi, m_hi, start=start, stop=False)
                nc.tensor.matmul(dst, w_hi, m_lo, start=False, stop=False)
                return nc.tensor.matmul(dst, w_lo, m_hi, start=False, stop=stop)

            pe.wait_ge(s_ident, 1)
            pe.wait_ge(s_qk, 32)
            for g in range(2):
                last = nc.tensor.transpose(psA[0][:, g * D:(g + 1) * D], qk_in[:, g, :], ident[:, :])
            last.then_inc(s_setup_turned, 1)
            pe.wait_ge(s_sum, 1)
            for g in range(3):
                nc.tensor.transpose(psA[1][:, g * D:(g + 1) * D], w_sum[:, g, :], ident[:, :])
            pe.wait_ge(s_gru, 16 * 5)
            for g in range(2):
                last = nc.tensor.transpose(psA[2][:, g * D:(g + 1) * D], u_in[:, g, :], ident[:, :])
            last.then_inc(s_setup_turned, 1)
            pe.wait_ge(s_adj, 16)
            for m in range(TILES):
                transpose_tiles(psB[m], lambda t: adj_in[:, t, m:N:TILES]).then_inc(s_setup_turned, 1)
            pe.wait_ge(s_setup_qkT, 1)
            nc.tensor.matmul(psA[3][:, 0:D], qkT[:, 0, :], qkT[:, 1, :], start=True, stop=True).then_inc(s_setup_qk, 1)
            pe.wait_ge(s_small, 16 * 14)
            pe.wait_ge(s_setup, 1)

            def stage_x0(s, r):
                pe.wait_ge(loaded[s], 16 * r + 16)
                pe.wait_ge(residual[s], NORMS * r + 1)
                transpose_tiles(psA[s], lambda t: xin[s][:, t, :]).then_inc(turned[s], 1)

            def stage_query(s, r):
                pe.wait_ge(xT_lo_ready[s], 8 * r + XT["x0"])
                three_pass(psB[s][:, :], qk_hi[:, :], qk_lo[:, :], xT_hi[s][:, :], xT_lo[s][:, :]).then_inc(product[s], 1)

            def stage_scores(s, r):
                pe.wait_ge(gT_lo_ready[s], 8 * r + GT["query"])
                for t in range(TILES):
                    c = slice(t * P, (t + 1) * P)
                    if t >= 2:
                        pe.wait_ge(tanh_done[s], TILES * r + t - 1)
                    three_pass((psA, psB)[t % 2][s][:, :], xT_hi[s][:, c], xT_lo[s][:, c],
                               gT_hi[s][:, :], gT_lo[s][:, :]).then_inc(scores_ready[s], 1)

            def stage_mix(s, r):
                pe.wait_ge(edges_ready[s], 2 * TILES * r + TILES)
                for t in range(TILES):
                    last = nc.tensor.matmul(psA[s][:, :], xin[s][:, t, :], E[s][:, t, :], start=(t == 0), stop=(t == TILES - 1))
                last.then_inc(product[s], 1)
                pe.wait_ge(pool_done[s], POOLS * r + POOL["edge_sum0"])
                for t in range(TILES):
                    last = nc.tensor.matmul(psB[s][:, t:t + 1], S[s][:, 0, t * P:(t + 1) * P], ones[:, 0:1], start=True, stop=True)
                last.then_inc(product[s], 1)

            def stage_out0(s, r):
                pe.wait_ge(copied[s], 3 * r + 1)
                for t in range(TILES):
                    last = nc.tensor.matmul(psA[s][:, t * D:(t + 1) * D], U[s][:, t * P:(t + 1) * P], v_sb[:, :], start=True, stop=True)
                last.then_inc(product[s], 1)

            def stage_x1(s, r):
                pe.wait_ge(normed[s], NORMS * r + 1)
                transpose_tiles(psA[s], lambda t: X[s][:, t, :]).then_inc(turned[s], 1)

            def stage_xh(s, r):
                pe.wait_ge(xT_lo_ready[s], 8 * r + XT["x1"])
                three_pass(psB[s][:, :], Wi_hi[:, :], Wi_lo[:, :], xT_hi[s][:, :], xT_lo[s][:, :]).then_inc(product[s], 1)

            def stage_gates(s, r):
                pe.wait_ge(vector_done[s], VECTORS * r + VECTOR["elu1"])
                for t in range(TILES):
                    last = nc.tensor.matmul(psB[s][:, t:t + 1], H[s][:, t * P:(t + 1) * P], We_sb[:, 0:1], start=True, stop=True)
                last.then_inc(product[s], 1)
                pe.wait_ge(gT_lo_ready[s], 8 * r + GT["xh"])
                three_pass(psA[s][:, :], Wt_hi[:, :], Wt_lo[:, :], gT_hi[s][:, :], gT_lo[s][:, :]).then_inc(product[s], 1)
                pe.wait_ge(vector_done[s], VECTORS * r + VECTOR["src_bias"])
                transpose_tiles(psB[s], lambda t: H[s][:, t * P:(t + 1) * P]).then_inc(turned[s], 1)

            def stage_agg(s, r):
                pe.wait_ge(copied[s], 3 * r + 2)
                pe.wait_ge(edges_ready[s], 2 * TILES * r + 2 * TILES)
                for t in range(TILES):
                    last = nc.tensor.matmul(psA[s][:, :], U[s][:, t * P:(t + 1) * P], E[s][:, t, :], start=(t == 0), stop=(t == TILES - 1))
                last.then_inc(product[s], 1)
                pe.wait_ge(pool_done[s], POOLS * r + POOL["edge_sum1"])
                nc.tensor.matmul(psB[s][:, :], ones[:, :], S[s][:, 0, :], start=True, stop=True).then_inc(product[s], 1)

            def stage_recv(s, r):
                pe.wait_ge(gT_lo_ready[s], 8 * r + GT["agg"])
                three_pass(psA[s][:, :], Wn_hi[:, 0, :], Wn_lo[:, 0, :], gT_hi[s][:, :], gT_lo[s][:, :], stop=False)
                pe.wait_ge(sT_lo_ready[s], 6 * r + ST["self"])
                three_pass(psA[s][:, :], Wn_hi[:, 1, :], Wn_lo[:, 1, :], sT_hi[s][:, :], sT_lo[s][:, :], start=False).then_inc(product[s], 1)

            def stage_out1(s, r):
                pe.wait_ge(vector_done[s], VECTORS * r + VECTOR["elu2"])
                for t in range(TILES):
                    dst, c = psB[s][:, t * D:(t + 1) * D], slice(t * P, (t + 1) * P)
                    nc.tensor.matmul(dst, U[s][:, c], Wm_sb[:, 0, :], start=True, stop=False)
                    last = nc.tensor.matmul(dst, H[s][:, c], Wm_sb[:, 1, :], start=False, stop=True)
                last.then_inc(product[s], 1)

            def stage_x2(s, r):
                pe.wait_ge(normed[s], NORMS * r + 2)
                transpose_tiles(psA[s], lambda t: X[s][:, t, :]).then_inc(turned[s], 1)

            def stage_cheb(s, r):
                pe.wait_ge(xT_lo_ready[s], 8 * r + XT["x2"])
                for t in range(TILES):
                    c = slice(t * P, (t + 1) * P)
                    if t >= 2:
                        pe.wait_ge(cheb_lo_ready[s], TILES * r + t - 1)
                    three_pass((psA, psB)[t % 2][s][:, 0:3 * D], xT_hi[s][:, c], xT_lo[s][:, c],
                               C_hi[:, :, :].rearrange("p g d -> p (g d)"), C_lo[:, :, :].rearrange("p g d -> p (g d)")).then_inc(cheb_ready[s], 1)

            def lap(i, ps):
                for t in range(TILES):
                    dst = ps[2 * i + t // 2][:, (t % 2) * 2 * D:(t % 2 + 1) * 2 * D]
                    c = slice(t * P, (t + 1) * P)
                    for m in range(TILES):
                        hi = nh_hi[i][:, m, :, :].rearrange("p o d -> p (o d)")
                        lo = nh_lo[i][:, m, :, :].rearrange("p o d -> p (o d)")
                        last = three_pass(dst, adjT_hi[:, m, c], adjT_lo[:, m, c], hi, lo, start=(m == 0), stop=(m == TILES - 1))
                    if t % 2:
                        last.then_inc(lap_ready[i], 1)

            def stage_lap1(i, r):
                for s in (2 * i, 2 * i + 1):
                    pe.wait_ge(cheb_lo_ready[s], TILES * (r + 1))
                lap(i, psA)

            def stage_lap2(i, r):
                pe.wait_ge(lap_lo_ready[i], TILES * (r + 1))
                lap(i, psB)

            def stage_x3(s, r):
                pe.wait_ge(normed[s], NORMS * r + 3)
                transpose_tiles(psA[s], lambda t: X[s][:, t, :]).then_inc(turned[s], 1)

            def stage_m(s, r, k):
                i, o = s // 2, s % 2
                if k == 0:
                    pe.wait_ge(nh_lo_ready[s], 5 * r + NH["x3"])
                    pe.wait_ge(xT_lo_ready[s], 8 * r + XT["x3"])
                    pe.wait_ge(copied[s], 3 * r + 3)
                else:
                    pe.wait_ge(nh_lo_ready[s], 5 * r + NH[f"h{k - 1}"])
                for m in range(TILES):
                    hi, lo = nh_hi[i][:, m, o, :], nh_lo[i][:, m, o, :]
                    last = three_pass(psA[s][:, :], hi, lo, adjT_hi[:, m, :], adjT_lo[:, m, :], start=(m == 0), stop=(m == TILES - 1))
                last.then_inc(product[s], 1)

            def stage_rz(s, r, k):
                pe.wait_ge(xT_lo_ready[s], 8 * r + XT["x3" if k == 0 else f"h{k - 1}"])
                three_pass(psB[s][:, :], Gw_hi[:, G_U3, :], Gw_lo[:, G_U3, :], xT_hi[s][:, :], xT_lo[s][:, :], stop=False)
                pe.wait_ge(gT_lo_ready[s], 8 * r + GT[f"m{k}"])
                three_pass(psB[s][:, :], Gw_hi[:, G_W4, :], Gw_lo[:, G_W4, :], gT_hi[s][:, :], gT_lo[s][:, :], start=False).then_inc(product[s], 1)
                three_pass(psA[s][:, :], Gw_hi[:, G_U3, :], Gw_lo[:, G_U3, :], xT_hi[s][:, :], xT_lo[s][:, :], stop=False)
                three_pass(psA[s][:, :], Gw_hi[:, G_W3, :], Gw_lo[:, G_W3, :], gT_hi[s][:, :], gT_lo[s][:, :], start=False).then_inc(product[s], 1)

            def stage_v(s, r, k):
                pe.wait_ge(r_done[s], STEPS * r + k + 1)
                three_pass(psB[s][:, :], Gw_hi[:, G_W5, :], Gw_lo[:, G_W5, :], gT_hi[s][:, :], gT_lo[s][:, :], stop=False)
                pe.wait_ge(sT_lo_ready[s], 6 * r + ST[f"rh{k}"])
                three_pass(psB[s][:, :], Gw_hi[:, G_U5, :], Gw_lo[:, G_U5, :], sT_hi[s][:, :], sT_lo[s][:, :], start=False).then_inc(product[s], 1)

            def stage_t(s, r, k):
                pe.wait_ge(z_done[s], STEPS * r + k + 1)
                pe.wait_ge(vector_done[s], VECTORS * r + VECTOR[f"h{k}"])
                transpose_tiles(psA[s], lambda t: H[s][:, t * P:(t + 1) * P]).then_inc(turned[s], 1)

            with pe.Fori(0, ROUNDS) as r:
                for stage in (stage_x0, stage_query, stage_scores, stage_mix, stage_out0, stage_x1, stage_xh, stage_gates,
                              stage_agg, stage_recv, stage_out1, stage_x2, stage_cheb):
                    for s in range(SLOTS):
                        stage(s, r)
                for i in range(PAIRS):
                    stage_lap1(i, r)
                for i in range(PAIRS):
                    stage_lap2(i, r)
                for s in range(SLOTS):
                    stage_x3(s, r)
                for k in range(STEPS):
                    for stage in (stage_m, stage_rz, stage_v, stage_t):
                        for s in range(SLOTS):
                            stage(s, r, k)


_INS = ["x", "adj", "L0_gnn_q", "L0_gnn_k", "L0_gnn_v", "L1_gnn_Wi", "L1_gnn_bi", "L1_gnn_We", "L1_gnn_be",
        "L1_gnn_Wn", "L1_gnn_bn", "L1_gnn_Wm", "L1_gnn_bm", "L2_gnn_weight", "L2_gnn_bias",
        "L3_gnn_w3_w", "L3_gnn_w3_b", "L3_gnn_u3_w", "L3_gnn_u3_b", "L3_gnn_w4_w", "L3_gnn_w4_b",
        "L3_gnn_w5_w", "L3_gnn_w5_b", "L3_gnn_u5_w", "L3_gnn_u5_b"]


def kernel(**inputs):
    import numpy as _np
    import concourse.bacc as _bacc
    from concourse import mybir as _mybir
    from concourse.bass_utils import run_bass_kernel_spmd as _run

    nc = _bacc.Bacc("TRN2", target_bir_lowering=False, num_devices=1)
    arrays, args = {}, []
    for name in _INS:
        a = _np.ascontiguousarray(inputs[name])
        arrays[f"in_{name}"] = a
        args.append(nc.dram_tensor(f"in_{name}", a.shape, _mybir.dt.from_np(a.dtype), kind="ExternalInput").ap())
    shape = _np.shape(inputs["x"])
    args.append(nc.dram_tensor("out_0", shape, _mybir.dt.float32, kind="ExternalOutput").ap())
    build(nc, *args)
    r = _run(nc, [arrays], core_ids=[0])
    return r.results[0]["out_0"]
```

```python
from contextlib import ExitStack

import concourse.bass as bass
from concourse import mybir

F32 = mybir.dt.float32
F32R = mybir.dt.float32r
ALU = mybir.AluOpType
ACT = mybir.ActivationFunctionType
AX = mybir.AxisListType

P = 128
SLOTS = 4
PAIRS = SLOTS // 2
STEPS = 5
ALPHA = 0.005
EPS = 1e-5

SCHEDULE = [
    ("load", 1.1, 1.8, 9.7, 0.0),
    ("x0", 4.5, 1.8, 11.5, 2.0),
    ("query", 2.8, 1.8, 11.9, 0.9),
    ("scores01", 6.3, 1.8, 12.4, 0.0),
    ("scores23", 3.8, 1.8, 12.3, 2.5),
    ("mix", 5.5, 1.8, 10.7, 9.4),
    ("out0", 4.1, 1.8, 12.7, 3.3),
    ("norm0", 2.7, 5.6, 10.8, 2.1),
    ("x1", 2.7, 1.8, 12.2, 4.6),
    ("xh", 1.2, 1.8, 11.5, 9.6),
    ("gates", 2.4, 1.8, 11.7, 1.2),
    ("turn_xh", 3.3, 1.8, 12.1, 0.2),
    ("agg", 5.2, 1.8, 13.3, 0.0),
    ("recv", 6.1, 1.8, 13.3, 4.7),
    ("out1", 6.8, 5.9, 13.3, 2.9),
    ("norm1", 5.2, 1.8, 11.8, 1.4),
    ("x2", 4.3, 2.2, 12.1, 0.0),
    ("cheb01", 10.2, 1.8, 13.5, 1.2),
    ("cheb23", 2.8, 1.8, 14.2, 7.7),
    ("lap1", 12.2, 1.8, 13.5, 6.2),
    ("lap2", 6.4, 1.8, 12.8, 4.2),
    ("norm2", 1.1, 6.6, 6.8, 0.0),
    ("x3", 6.0, 1.8, 13.1, 4.7),
    ("m0", 3.4, 1.8, 12.3, 4.3),
    ("r0", 2.0, 1.8, 11.7, 3.7),
    ("v0", 4.7, 1.8, 11.9, 0.5),
    ("t0", 4.2, 1.8, 11.5, 6.0),
    ("m1", 3.1, 1.8, 12.3, 4.3),
    ("r1", 1.8, 1.8, 11.7, 3.7),
    ("v1", 3.2, 1.8, 11.9, 0.5),
    ("t1", 1.4, 1.8, 11.5, 6.0),
    ("m2", 2.3, 1.8, 12.3, 4.3),
    ("r2", 3.8, 1.8, 11.7, 3.7),
    ("v2", 5.0, 1.8, 11.9, 0.5),
    ("t2", 2.9, 1.8, 11.5, 6.0),
    ("m3", 2.6, 1.8, 12.3, 4.3),
    ("r3", 2.2, 1.8, 11.7, 3.7),
    ("v3", 3.4, 1.8, 11.9, 0.5),
    ("t3", 4.9, 1.8, 11.5, 6.0),
    ("m4", 2.8, 1.8, 12.3, 4.3),
    ("r4", 3.3, 1.8, 11.7, 3.7),
    ("v4", 3.7, 1.8, 11.9, 0.5),
    ("t4", 0.0, 1.8, 11.5, 6.0),
    ("last", 3.1, 1.8, 11.8, 7.1),
    ("norm3", 0.0, 1.8, 12.6, 1.5),
    ("store", 0.0, 1.8, 6.0, 0.0),
]
STAGES = [(name, length) for name, length, *_ in SCHEDULE]
LAGS = {"scalar": 2, "vector": 3, "gpsimd": 4}
SLOT_LAG = 6.44
PAIR_LAG = 12.81


def elag(engine, n):
    return SCHEDULE[n][LAGS[engine]] if engine in LAGS else 0.0


def body(engine):
    period = sum(length for _, length in STAGES) + SLOT_LAG
    at = []
    for s in range(SLOTS):
        time = (s // 2) * PAIR_LAG + (s % 2) * SLOT_LAG
        for n, (name, length) in enumerate(STAGES):
            if name == "lap1" and s % 2 == 0 or name == "norm2" and s % 2 == 1:
                time += SLOT_LAG
            if name not in ("lap1", "lap2") or s % 2:
                t = time + elag(engine, n)
                at.append((t % period, s, n, name, int(t // period)))
            time += length
    assert all(behind in (0, 1) for *_, behind in at)
    return [(name, s, behind) for _, s, _, name, behind in sorted(at)]


def run(engine, stages, r, first=False, last=False):
    for name, s, behind in body(engine):
        if name in stages and not (first and behind) and not (last and not behind):
            stages[name](s, r - behind)


TURNED = {"x0": 1, "x1": 2, "xh": 3, "x2": 4, "x3": 5, **{f"h{k}": 6 + k for k in range(STEPS)}}
XT = {"x0": 1, "x1": 2, "x2": 3}
GT = {"query": 1, "agg": 2, **{f"m{k}": 3 + k for k in range(STEPS)}}
NH = {"x3": 1, **{f"h{k}": 2 + k for k in range(STEPS - 1)}}
PRODUCT = {name: n + 1 for n, name in enumerate(
    ["query", "mix", "out0", "sums0", "xh", "src", "tgt", "agg", "sums1", "recv", "out1"]
    + [f"{name}{k}" for k in range(STEPS) for name in ("m", "r", "z", "hv")])}
VECTOR = {name: n + 1 for n, name in enumerate(
    ["rsum", "elu_low1", "elu1", "src_bias", "self", "elu_low2", "elu2"]
    + [f"{name}{k}" for k in range(STEPS) for name in ("rh", "update", "h")])}
POOL = {name: n + 1 for n, name in enumerate(
    ["half_sum0", "edge_sum0", "std0", "rstd0", "bias1", "half_sum1", "edge_sum1", "std1", "rstd1", "bias2",
     "std2", "rstd2"] + [f"kept{k}" for k in range(STEPS)] + ["std3", "rstd3"])}
TURNS, XTS, GTS, NHS, PRODUCTS, VECTORS, POOLS = map(len, (TURNED, XT, GT, NH, PRODUCT, VECTOR, POOL))
NORMS = 4


def build(nc, x, adj, q, k, v, Wi, bi, We, be, Wn, bn, Wm, bm, cheb_w, cheb_b,
          w3_w, w3_b, u3_w, u3_b, w4_w, w4_b, w5_w, w5_b, u5_w, u5_b, out):
    B, N, D = x.shape
    TILES = N // P
    ROUNDS = B // SLOTS
    SCORE_SCALE = 1.0 / (float(D) ** 0.5 * 8.0)
    assert D == P and N == TILES * P and B == ROUNDS * SLOTS

    with ExitStack() as ctx:
        def sb(name, shape, dt=F32):
            return ctx.enter_context(nc.sbuf_tensor(name, shape, dt))

        def sem(name):
            return ctx.enter_context(nc.semaphore(name))

        def sems(name, n=SLOTS):
            return [sem(f"{name}{i}") for i in range(n)]

        ident = sb("ident", [P, P])
        ones = sb("ones", [P, P])
        neg_half = sb("neg_half", [P, TILES])
        eps_cols = sb("eps_cols", [P, TILES])
        adjT = sb("adjT", [P, TILES, N])
        adjT_hi = sb("adjT_hi", [P, TILES, N], F32R)
        adjT_lo = sb("adjT_lo", [P, TILES, N], F32R)
        edge_mask = sb("edge_mask", [P, TILES, N])
        degree = sb("degree", [P, TILES])
        dinv = sb("dinv", [P, TILES])
        neg_dinv = sb("neg_dinv", [P, TILES])
        v_sb = sb("v_sb", [P, D])
        qk_hi, qk_lo = sb("qk_hi", [P, D], F32R), sb("qk_lo", [P, D], F32R)
        Wi_hi, Wi_lo = sb("Wi_hi", [P, D], F32R), sb("Wi_lo", [P, D], F32R)
        We_sb = sb("We_sb", [P, 2])
        tgt_rows = sb("tgt_rows", [P, P])
        Wn_hi, Wn_lo = sb("Wn_hi", [P, D], F32R), sb("Wn_lo", [P, D], F32R)
        Wn2 = sb("Wn2", [P, D])
        Wm_sb = sb("Wm_sb", [P, 2, D])
        C_hi, C_lo = sb("C_hi", [P, 3, D], F32R), sb("C_lo", [P, 3, D], F32R)
        G_R, G_ZR, G_HV = range(3)
        Gw_hi, Gw_lo = sb("Gw_hi", [P, 3, D], F32R), sb("Gw_lo", [P, 3, D], F32R)
        U3, U5 = sb("u3T", [P, D]), sb("u5T", [P, D])
        flag_cols, flag = sb("flag_cols", [P, 1]), sb("flag", [1, 1], mybir.dt.int32)
        bi_sb, bn_sb, be_sb = sb("bi_sb", [P, 1]), sb("bn_sb", [P, 1]), sb("be_sb", [P, 1])
        bm_rows, cb_rows = sb("bm_rows", [P, D]), sb("cb_rows", [P, D])
        gate_bias = sb("gate_bias", [P, 5])
        z_bias, r_bias, hv_bias = sb("z_bias", [P, 1]), sb("r_bias", [P, 1]), sb("hv_bias", [P, 1])

        def per_slot(name, shape, dt=F32):
            return [sb(f"{name}{s}", shape, dt) for s in range(SLOTS)]

        xin = per_slot("xin", [P, TILES, D])
        X_pair = [sb(f"X{i}", [P, 2, TILES, D]) for i in range(PAIRS)]
        X = [X_pair[s // 2][:, s % 2] for s in range(SLOTS)]
        xT_hi, xT_lo = per_slot("xT_hi", [P, N], F32R), per_slot("xT_lo", [P, N], F32R)
        gT_hi, gT_lo = per_slot("gT_hi", [P, N], F32R), per_slot("gT_lo", [P, N], F32R)
        E_pair = [sb(f"E{i}", [P, 2, TILES, N]) for i in range(PAIRS)]
        E = [E_pair[s // 2][:, s % 2] for s in range(SLOTS)]
        S = per_slot("S", [P, 2, N])
        U = per_slot("U", [P, N])
        H = per_slot("H", [P, N])
        stat = per_slot("stat", [P, TILES, 6])
        mv = per_slot("mv", [P, 3, TILES])
        rstd = per_slot("rstd", [P, TILES])
        rsum = per_slot("rsum", [P, TILES])
        src_bias = per_slot("src_bias", [P, TILES])
        nh_hi = [sb(f"nh_hi{i}", [P, TILES, 2, D], F32R) for i in range(PAIRS)]
        nh_lo = [sb(f"nh_lo{i}", [P, TILES, 2, D], F32R) for i in range(PAIRS)]

        psA = [ctx.enter_context(nc.psum_tensor(f"psA{s}", [P, N], F32)) for s in range(SLOTS)]
        psB = [ctx.enter_context(nc.psum_tensor(f"psB{s}", [P, N], F32)) for s in range(SLOTS)]

        adj_in = E[0]
        stage_w3 = E[1][:, :, :].rearrange("p t n -> p (t n)")
        w_in = stage_w3[:, 0:6 * D].rearrange("p (g h d) -> p g h d", g=3, h=2)
        w_sum = stage_w3[:, 6 * D:9 * D].rearrange("p (g d) -> p g d", g=3)
        u_in = stage_w3[:, 9 * D:11 * D].rearrange("p (g d) -> p g d", g=2)
        qk_in = stage_w3[:, 11 * D:13 * D].rearrange("p (g d) -> p g d", g=2)
        qkT = stage_w3[:, 13 * D:15 * D].rearrange("p (g d) -> p g d", g=2)
        stage_c = E[2][:, :, :].rearrange("p t n -> p (t n)")
        c_in = stage_c[:, 0:3 * D].rearrange("p (g d) -> p g d", g=3)
        c_sum = stage_c[:, 3 * D:6 * D].rearrange("p (g d) -> p g d", g=3)
        Wi_in = stage_c[:, 6 * D:7 * D]
        Wn_in = stage_c[:, 7 * D:8 * D]
        five = stage_c[:, 10 * D:15 * D].rearrange("p (g d) -> p g d", g=5)

        keep_pair = [E_pair[i][:, :, 0:2, :].rearrange("p o a (t c) -> p o (a t) c", c=2 * D) for i in range(PAIRS)]
        cheb_keep = [keep_pair[s // 2][:, s % 2] for s in range(SLOTS)]
        r_gate = [E[s][:, 0, :] for s in range(SLOTS)]
        z_gate = [E[s][:, 1, :] for s in range(SLOTS)]
        h_new = [E[s][:, 2, :] for s in range(SLOTS)]
        rh = [E[s][:, 3, :] for s in range(SLOTS)]
        kept = [S[s][:, 1, :] for s in range(SLOTS)]

        s_adj, s_qk, s_gru, s_cheb, s_small = sem("s_adj"), sem("s_qk"), sem("s_gru"), sem("s_cheb"), sem("s_small")
        s_const, s_ident0, s_ident = sem("s_const"), sem("s_ident0"), sem("s_ident")
        s_setup_turned, s_setup_qkT, s_setup_qk = sem("s_setup_turned"), sem("s_setup_qkT"), sem("s_setup_qk")
        s_flag_cols, s_flag_sum, s_flag = sem("s_flag_cols"), sem("s_flag_sum"), sem("s_flag")
        s_sum, s_degree, s_dinv, s_setup, dve_step = sem("s_sum"), sem("s_degree"), sem("s_dinv"), sem("s_setup"), sem("dve_step")
        loaded, stored = sems("loaded"), sems("stored")
        turned = sems("turned")
        scores_ready = sems("scores_ready")
        product = sems("product")
        cheb_ready = sems("cheb_ready")
        lap_ready = sems("lap_ready", PAIRS)
        xT_hi_ready, gT_hi_ready, nh_hi_ready = sems("xT_hi_ready"), sems("gT_hi_ready"), sems("nh_hi_ready")
        tanh_done = sems("tanh_done")
        exp_done = sems("exp_done")
        gate_done = sems("gate_done")
        copied = sems("copied")
        cheb_kept = sems("cheb_kept")
        cheb_hi_ready = sems("cheb_hi_ready")
        lap_hi_ready = sems("lap_hi_ready", PAIRS)
        r_done, z_done, hv_done = sems("r_done"), sems("z_done"), sems("hv_done")
        keep_done = sems("keep_done")
        xT_lo_ready, gT_lo_ready, nh_lo_ready = sems("xT_lo_ready"), sems("gT_lo_ready"), sems("nh_lo_ready")
        cheb_lo_ready = sems("cheb_lo_ready")
        lap_lo_ready = sems("lap_lo_ready", PAIRS)
        edges_ready = sems("edges_ready")
        residual = sems("residual")
        var_ready = sems("var_ready")
        vector_done = sems("vector_done")
        normed = sems("normed")
        stats_ready = sems("stats_ready")
        lap_sum = sems("lap_sum", PAIRS)
        cheb_out = sems("cheb_out", PAIRS)
        pool_done = sems("pool_done")

        def col(w):
            return w.rearrange("(p a) -> p a", a=1)

        def rows(w):
            return w.rearrange("(a n) -> a n", a=1).partition_broadcast(P)

        xg = x.rearrange("b (p t) d -> b p t d", t=TILES)
        og = out.rearrange("b (p t) d -> b p t d", t=TILES)

        block = ctx.enter_context(nc.Block())

        @block.sync
        def _(sp):
            for s in range(SLOTS):
                sp.sem_inc(stored[s], 16)
                sp.sem_inc(residual[s], 1)
            sp.dma_start(adj_in[:, :, :], adj.rearrange("(p t) m -> p t m", t=TILES)).then_inc(s_adj, 16)
            sp.dma_start(qk_in[:, 0, :], q).then_inc(s_qk, 16)
            sp.dma_start(qk_in[:, 1, :], k).then_inc(s_qk, 16)
            for s in range(SLOTS):
                sp.dma_start(xin[s][:, :, :], xg[s]).then_inc(loaded[s], 16)
            for g, w in enumerate((w3_w, w4_w, w5_w)):
                sp.dma_start(w_in[:, g, :, :], w.rearrange("p (h d) -> p h d", h=2)).then_inc(s_gru, 16)
            sp.dma_start(u_in[:, 0, :], u3_w).then_inc(s_gru, 16)
            sp.dma_start(u_in[:, 1, :], u5_w).then_inc(s_gru, 16)
            sp.dma_start(c_in[:, :, :], cheb_w.rearrange("k a c d -> c (k a) d")).then_inc(s_cheb, 16)

            def stage_load(s, r):
                if isinstance(r, int):
                    return
                sp.wait_ge(residual[s], NORMS * (r - 1) + 2)
                sp.dma_start(xin[s][:, :, :], xg[bass.ds(r * SLOTS + s, 1)].rearrange("a p t d -> p (a t) d")).then_inc(loaded[s], 16)

            def stage_store(s, r):
                sp.wait_ge(normed[s], NORMS * (r + 1))
                sp.dma_start(og[bass.ds(r * SLOTS + s, 1)].rearrange("a p t d -> p (a t) d"), X[s]).then_inc(stored[s], 16)

            stages = {"load": stage_load, "store": stage_store}
            run("sync", stages, 0, first=True)
            with sp.Fori(1, ROUNDS) as r:
                run("sync", stages, r)
            run("sync", stages, ROUNDS, last=True)
            for s in range(SLOTS):
                sp.wait_ge(stored[s], 16 * (ROUNDS + 1))

        @block.gpsimd
        def _(pool):
            nc.gpsimd.memset(ident[:, :], 0.0).then_inc(s_ident0, 1)
            nc.gpsimd.memset(ones[:, :], 1.0).then_inc(s_const, 1)
            nc.gpsimd.memset(neg_half[:, :], -0.5).then_inc(s_const, 1)
            nc.gpsimd.memset(eps_cols[:, :], EPS).then_inc(s_const, 1)
            pool.wait_ge(s_ident0, 1)
            nc.gpsimd.affine_select(out=ident[:, :], in_=ident[:, :], compare_op=ALU.not_equal, fill=1.0,
                                    base=0, pattern=[[-1, P]], channel_multiplier=1).then_inc(s_ident, 1)
            pool.wait_ge(s_degree, 1)
            pool.wait_ge(s_const, 3)
            nc.gpsimd.tensor_tensor(dinv[:, :], degree[:, :], neg_half[:, :], ALU.pow).then_inc(s_dinv, 1)
            pool.wait_ge(s_small, 16 * 15)
            pool.wait_ge(s_setup, 1)

            def edge_sums(s, r, layer):
                pool.wait_ge(edges_ready[s], 2 * TILES * r + TILES * (layer + 1))
                if layer == 1:
                    pool.wait_ge(product[s], PRODUCTS * r + PRODUCT["sums0"])
                nc.gpsimd.tensor_tensor(S[s][:, :, :], E[s][:, 0:2, :], E[s][:, 2:4, :], ALU.add).then_inc(pool_done[s], 1)
                pool.wait_ge(pool_done[s], POOLS * r + POOL[f"half_sum{layer}"])
                nc.gpsimd.tensor_tensor(S[s][:, 0, :], S[s][:, 0, :], S[s][:, 1, :], ALU.add).then_inc(pool_done[s], 1)

            def norm(s, r, layer):
                pool.wait_ge(var_ready[s], NORMS * r + layer + 1)
                nc.gpsimd.tensor_tensor(rstd[s][:, :], mv[s][:, 1, :], eps_cols[:, :], ALU.add).then_inc(pool_done[s], 1)
                pool.wait_ge(pool_done[s], POOLS * r + POOL[f"std{layer}"])
                nc.gpsimd.tensor_tensor(rstd[s][:, :], rstd[s][:, :], neg_half[:, :], ALU.pow).then_inc(pool_done[s], 1)

            def stage_scores23(s, r):
                edge_sums(s, r, 0)

            def stage_out0(s, r):
                norm(s, r, 0)

            def stage_x1(s, r):
                pool.wait_ge(normed[s], NORMS * r + 1)
                pool.wait_ge(turned[s], TURNS * r + TURNED["x1"])
                nc.gpsimd.tensor_tensor(X[s], X[s],
                                        bm_rows[:, :].unsqueeze(1).to_broadcast([P, TILES, D]), ALU.add).then_inc(pool_done[s], 1)

            def stage_turn_xh(s, r):
                edge_sums(s, r, 1)

            def stage_out1(s, r):
                norm(s, r, 1)

            def stage_cheb23(s, r):
                pool.wait_ge(cheb_kept[s], TILES * (r + 1))
                nc.gpsimd.tensor_tensor(cheb_keep[s][:, :, 0:D], cheb_keep[s][:, :, 0:D],
                                        cb_rows[:, :].unsqueeze(1).to_broadcast([P, TILES, D]), ALU.add).then_inc(pool_done[s], 1)

            def stage_lap2(s, r):
                norm(s - 1, r, 2)
                norm(s, r, 2)

            def stage_v(s, r, k):
                pool.wait_ge(keep_done[s], STEPS * r + k + 1)
                nc.gpsimd.tensor_tensor(kept[s], kept[s], H[s][:, :], ALU.mult).then_inc(pool_done[s], 1)

            def stage_last(s, r):
                norm(s, r, 3)

            stages = {"scores23": stage_scores23, "out0": stage_out0, "x1": stage_x1, "turn_xh": stage_turn_xh,
                      "out1": stage_out1, "cheb23": stage_cheb23, "lap2": stage_lap2, "last": stage_last}
            for k in range(STEPS):
                stages[f"v{k}"] = lambda s, r, k=k: stage_v(s, r, k)
            run("gpsimd", stages, 0, first=True)
            with pool.Fori(1, ROUNDS) as r:
                run("gpsimd", stages, r)
            run("gpsimd", stages, ROUNDS, last=True)

        @block.scalar
        def _(act):
            for g, b in enumerate((w3_b, w4_b, w5_b, u3_b, u5_b)):
                act.dma_start(gate_bias[:, g:g + 1], col(b)).then_inc(s_small, 16)
            act.dma_start(bi_sb[:, :], col(bi)).then_inc(s_small, 16)
            act.dma_start(bn_sb[:, :], col(bn)).then_inc(s_small, 16)
            for h in range(2):
                act.dma_start(We_sb[:, h:h + 1], We[h * P:(h + 1) * P, :]).then_inc(s_small, 16)
            act.dma_start(be_sb[:, :], rows(be)).then_inc(s_small, 16)
            act.dma_start(bm_rows[:, :], rows(bm)).then_inc(s_small, 16)
            act.dma_start(cb_rows[:, :], cheb_b.rearrange("a b d -> (a b) d").partition_broadcast(P)).then_inc(s_small, 16)
            act.dma_start(v_sb[:, :], v).then_inc(s_small, 16)
            act.dma_start(Wm_sb[:, :, :], Wm.rearrange("(h p) d -> p h d", h=2)).then_inc(s_small, 16)
            act.dma_start(Wi_in, Wi).then_inc(s_cheb, 16)
            act.dma_start(Wn_in, Wn[0:P, :]).then_inc(s_cheb, 16)
            act.dma_start(Wn2[:, :], Wn[P:2 * P, :]).then_inc(s_small, 16)
            act.wait_ge(s_small, 16 * 15)
            act.wait_ge(s_setup, 1)

            def turn(s, r, name):
                act.wait_ge(turned[s], TURNS * r + TURNED[name])
                nc.scalar.copy(xT_hi[s][:, :], psA[s][:, :]).then_inc(xT_hi_ready[s], 1)

            def stage_x0(s, r):
                turn(s, r, "x0")

            def stage_query(s, r):
                act.wait_ge(product[s], PRODUCTS * r + PRODUCT["query"])
                nc.scalar.copy(gT_hi[s][:, :], psB[s][:, :]).then_inc(gT_hi_ready[s], 1)

            def scores(s, r, tiles):
                for t in tiles:
                    ps = (psA, psB)[t % 2][s]
                    act.wait_ge(scores_ready[s], TILES * r + t + 1)
                    nc.scalar.activation(E[s][:, t, :], ps[:, :], ACT.Tanh, scale=SCORE_SCALE).then_inc(tanh_done[s], 1)
                for t in tiles:
                    act.wait_ge(tanh_done[s], TILES * r + t + 1)
                    nc.scalar.activation(E[s][:, t, :], E[s][:, t, :], ACT.Exp, scale=8.0).then_inc(exp_done[s], 1)

            def stage_scores01(s, r):
                scores(s, r, (0, 1))

            def stage_scores23(s, r):
                scores(s, r, (2, 3))

            def stage_mix(s, r):
                act.wait_ge(product[s], PRODUCTS * r + PRODUCT["mix"])
                nc.scalar.copy(U[s][:, :], psA[s][:, :]).then_inc(copied[s], 1)

            def stage_x1(s, r):
                turn(s, r, "x1")

            def stage_xh(s, r):
                act.wait_ge(product[s], PRODUCTS * r + PRODUCT["xh"])
                nc.scalar.activation(U[s][:, :], psB[s][:, :], ACT.Exp, bias=bi_sb[:, :]).then_inc(exp_done[s], 1)

            def stage_turn_xh(s, r):
                act.wait_ge(vector_done[s], VECTORS * r + VECTOR["src_bias"])
                act.wait_ge(product[s], PRODUCTS * r + PRODUCT["tgt"])
                for t in range(TILES):
                    nc.scalar.activation(E[s][:, t, :], psA[s][:, :], ACT.Tanh, scale=0.5,
                                         bias=src_bias[s][:, t:t + 1]).then_inc(gate_done[s], 1)
                act.wait_ge(turned[s], TURNS * r + TURNED["xh"])
                nc.scalar.copy(U[s][:, :], psB[s][:, :]).then_inc(copied[s], 1)

            def stage_agg(s, r):
                act.wait_ge(product[s], PRODUCTS * r + PRODUCT["agg"])
                nc.scalar.copy(gT_hi[s][:, :], psA[s][:, :]).then_inc(gT_hi_ready[s], 1)

            def stage_recv(s, r):
                act.wait_ge(product[s], PRODUCTS * r + PRODUCT["recv"])
                nc.scalar.activation(U[s][:, :], psA[s][:, :], ACT.Exp, bias=bn_sb[:, :]).then_inc(exp_done[s], 1)

            def stage_x2(s, r):
                turn(s, r, "x2")

            def cheb(s, r, tiles):
                i, o = s // 2, s % 2
                for t in tiles:
                    ps = (psA, psB)[t % 2][s]
                    act.wait_ge(cheb_ready[s], TILES * r + t + 1)
                    nc.scalar.activation(nh_hi[i][:, t, o, :], ps[:, 2 * D:3 * D], ACT.Copy,
                                         scale=dinv[:, t:t + 1]).then_inc(cheb_hi_ready[s], 1)
                    nc.scalar.copy(cheb_keep[s][:, t, :], ps[:, 0:2 * D]).then_inc(cheb_kept[s], 1)

            def stage_cheb01(s, r):
                cheb(s, r, (0, 1))

            def stage_cheb23(s, r):
                cheb(s, r, (2, 3))

            def stage_lap1(s, r):
                i = s // 2
                act.wait_ge(lap_ready[i], 4 * r + 2)
                for t in range(TILES):
                    act.wait_ge(lap_sum[i], TILES * r + t + 1)
                    nc.scalar.activation(nh_hi[i][:, t, :, :], keep_pair[i][:, :, t, D:2 * D], ACT.Copy,
                                         scale=dinv[:, t:t + 1]).then_inc(lap_hi_ready[i], 1)

            def stage_x3(s, r):
                i, o = s // 2, s % 2
                act.wait_ge(normed[s], NORMS * r + 3)
                nc.scalar.copy(nh_hi[i][:, :, o, :], X[s]).then_inc(nh_hi_ready[s], 1)
                act.wait_ge(turned[s], TURNS * r + TURNED["x3"])
                nc.scalar.copy(H[s][:, :], psA[s][:, :]).then_inc(copied[s], 1)

            def stage_m(s, r, k):
                act.wait_ge(product[s], PRODUCTS * r + PRODUCT[f"m{k}"])
                nc.scalar.copy(gT_hi[s][:, :], psA[s][:, :]).then_inc(gT_hi_ready[s], 1)

            def stage_r(s, r, k):
                act.wait_ge(product[s], PRODUCTS * r + PRODUCT[f"r{k}"])
                nc.scalar.activation(r_gate[s], psB[s][:, :], ACT.Tanh, scale=0.5, bias=r_bias[:, :]).then_inc(r_done[s], 1)

            def stage_v(s, r, k):
                act.wait_ge(product[s], PRODUCTS * r + PRODUCT[f"z{k}"])
                nc.scalar.activation(z_gate[s], psB[s][:, :], ACT.Tanh, scale=0.5, bias=z_bias[:, :]).then_inc(z_done[s], 1)
                act.wait_ge(z_done[s], STEPS * r + k + 1)
                nc.scalar.activation(kept[s], z_gate[s], ACT.Copy, scale=-0.5, bias=0.5).then_inc(keep_done[s], 1)
                act.wait_ge(product[s], PRODUCTS * r + PRODUCT[f"hv{k}"])
                nc.scalar.activation(h_new[s], psA[s][:, :], ACT.Tanh, bias=hv_bias[:, :]).then_inc(hv_done[s], 1)

            def stage_t(s, r, k):
                i, o = s // 2, s % 2
                act.wait_ge(turned[s], TURNS * r + TURNED[f"h{k}"])
                nc.scalar.copy(nh_hi[i][:, :, o, :], psA[s][:, :].rearrange("p (t d) -> p t d", t=TILES)).then_inc(nh_hi_ready[s], 1)

            stages = {"x0": stage_x0, "query": stage_query, "scores01": stage_scores01, "scores23": stage_scores23,
                      "mix": stage_mix, "x1": stage_x1, "xh": stage_xh, "turn_xh": stage_turn_xh, "agg": stage_agg,
                      "recv": stage_recv, "x2": stage_x2, "cheb01": stage_cheb01, "cheb23": stage_cheb23,
                      "lap1": stage_lap1, "x3": stage_x3}
            for k in range(STEPS):
                stages[f"m{k}"] = lambda s, r, k=k: stage_m(s, r, k)
                stages[f"r{k}"] = lambda s, r, k=k: stage_r(s, r, k)
                stages[f"v{k}"] = lambda s, r, k=k: stage_v(s, r, k)
                if k < STEPS - 1:
                    stages[f"t{k}"] = lambda s, r, k=k: stage_t(s, r, k)
            run("scalar", stages, 0, first=True)
            with act.Fori(1, ROUNDS) as r:
                run("scalar", stages, r)
            run("scalar", stages, ROUNDS, last=True)

        @block.vector
        def _(dve):
            steps = [0]

            def link(instruction):
                steps[0] += 1
                instruction.then_inc(dve_step, 1)
                dve.wait_ge(dve_step, steps[0])

            def split_const(hi, lo, src):
                link(nc.vector.tensor_copy(hi, src))
                nc.vector.tensor_tensor(lo, src, hi.bitcast(F32), ALU.subtract)

            dve.wait_ge(s_adj, 16)
            nc.vector.tensor_reduce(degree[:, :], adj_in, AX.X, ALU.add).then_inc(s_degree, 1)
            dve.wait_ge(s_gru, 16 * 5)
            nc.vector.tensor_tensor(w_sum, w_in[:, :, 0, :], w_in[:, :, 1, :], ALU.add).then_inc(s_sum, 1)
            dve.wait_ge(s_setup_turned, 1)
            nc.vector.tensor_copy(qkT, psA[0][:, 0:2 * D].rearrange("p (g d) -> p g d", g=2)).then_inc(s_setup_qkT, 1)
            dve.wait_ge(s_setup_turned, 2)
            nc.vector.tensor_copy(five[:, 3, :], psA[1][:, 0:D])
            nc.vector.tensor_copy(five[:, G_R, :], psA[1][:, D:2 * D])
            link(nc.vector.tensor_copy(five[:, G_HV, :], psA[1][:, 2 * D:3 * D]))
            nc.vector.tensor_copy(U3[:, :], psA[2][:, 0:D])
            nc.vector.tensor_scalar(U5[:, :], psA[2][:, D:2 * D], 0.5, None, ALU.mult)
            link(nc.vector.tensor_tensor(five[:, G_ZR, :], five[:, 3, :], five[:, G_R, :], ALU.subtract))
            split_const(Gw_hi[:, :, :], Gw_lo[:, :, :], five[:, 0:3, :])
            dve.wait_ge(s_cheb, 16 * 3)
            nc.vector.tensor_tensor(c_sum[:, 0, :], c_in[:, 0, :], c_in[:, 1, :], ALU.add)
            nc.vector.scalar_tensor_tensor(out=c_sum[:, 1, :], in0=c_in[:, 2, :], scalar=4.0, in1=c_in[:, 1, :],
                                           op0=ALU.mult, op1=ALU.add)
            link(nc.vector.tensor_scalar(c_sum[:, 2, :], c_in[:, 2, :], 2.0, None, ALU.mult))
            link(nc.vector.tensor_tensor(c_sum[:, 0, :], c_sum[:, 0, :], c_in[:, 2, :], ALU.add))
            split_const(C_hi[:, :, :], C_lo[:, :, :], c_sum)
            split_const(Wi_hi[:, :], Wi_lo[:, :], Wi_in)
            split_const(Wn_hi[:, :], Wn_lo[:, :], Wn_in)
            dve.wait_ge(s_small, 16 * 15)
            dve.wait_ge(s_const, 3)
            nc.vector.tensor_scalar(tgt_rows[:, :], ones[:, :], We_sb[:, 1:2], None, ALU.mult)
            nc.vector.tensor_tensor(hv_bias[:, :], gate_bias[:, 2:3], gate_bias[:, 4:5], ALU.add)
            nc.vector.tensor_tensor(z_bias[:, :], gate_bias[:, 0:1], gate_bias[:, 3:4], ALU.add)
            link(nc.vector.tensor_tensor(r_bias[:, :], gate_bias[:, 1:2], gate_bias[:, 3:4], ALU.add))
            nc.vector.tensor_scalar(z_bias[:, :], z_bias[:, :], 0.5, None, ALU.mult)
            nc.vector.tensor_scalar(r_bias[:, :], r_bias[:, :], 0.5, None, ALU.mult)
            dve.wait_ge(s_dinv, 1)
            nc.vector.tensor_scalar(neg_dinv[:, :], dinv[:, :], -1.0, None, ALU.mult)
            for t in range(TILES):
                dve.wait_ge(s_setup_turned, 3 + t)
                link(nc.vector.tensor_copy(adjT[:, t, :], psB[t][:, :]))
            link(nc.vector.tensor_copy(adjT_hi[:, :, :], adjT[:, :, :]))
            link(nc.vector.tensor_tensor(adjT_lo[:, :, :], adjT[:, :, :], adjT_hi[:, :, :].bitcast(F32), ALU.subtract))
            link(nc.vector.tensor_scalar(edge_mask[:, :, :], adjT_lo[:, :, :].bitcast(F32), 0.0, None, ALU.not_equal))
            nc.vector.tensor_reduce(flag_cols[:, :], edge_mask[:, :, :], AX.XY, ALU.max).then_inc(s_flag_cols, 1)
            dve.wait_ge(s_flag_cols, 1)
            link(nc.vector.tensor_scalar(edge_mask[:, :, :], adjT[:, :, :], 0.0, 0.5 * ALPHA, ALU.is_equal, ALU.mult))
            for t in range(TILES):
                nc.vector.scalar_tensor_tensor(out=edge_mask[:, t, :], in0=adjT[:, t, :], scalar=0.5,
                                               in1=edge_mask[:, t, :], op0=ALU.mult, op1=ALU.add)
            dve.wait_ge(s_flag_sum, 1)
            nc.vector.tensor_copy(flag[:, :], psA[3][0:1, D:D + 1]).then_inc(s_flag, 1)
            dve.wait_ge(s_setup_qk, 1)
            link(nc.vector.tensor_copy(five[:, 0, :], psA[3][:, 0:D]))
            link(nc.vector.tensor_copy(qk_hi[:, :], five[:, 0, :]))
            nc.vector.tensor_tensor(qk_lo[:, :], five[:, 0, :], qk_hi[:, :].bitcast(F32), ALU.subtract).then_inc(s_setup, 1)
            dve.wait_ge(s_setup, 1)

            def lo_part(lo, src, hi):
                return nc.vector.tensor_tensor(lo, src, hi.bitcast(F32), ALU.subtract)

            def turn(s, r, name):
                dve.wait_ge(xT_hi_ready[s], XTS * r + XT[name])
                lo_part(xT_lo[s][:, :], psA[s][:, :], xT_hi[s][:, :]).then_inc(xT_lo_ready[s], 1)

            def spread(s, r, layer):
                dve.wait_ge(residual[s], NORMS * r + layer + 2)
                for t in range(TILES):
                    last = nc.vector.bn_stats(out=stat[s][:, t, :], in_=X[s][:, t, :])
                last.then_inc(stats_ready[s], 1)
                dve.wait_ge(stats_ready[s], 3 * (NORMS * r + layer) + 1)
                mean_e, m2_e, mean_o, m2_o = (stat[s][:, :, n] for n in (1, 2, 4, 5))
                nc.vector.tensor_tensor(mv[s][:, 0, :], mean_e, mean_o, ALU.add)
                nc.vector.tensor_tensor(mv[s][:, 1, :], m2_e, m2_o, ALU.add)
                nc.vector.tensor_tensor(mv[s][:, 2, :], mean_e, mean_o, ALU.subtract).then_inc(stats_ready[s], 1)
                dve.wait_ge(stats_ready[s], 3 * (NORMS * r + layer) + 2)
                nc.vector.tensor_scalar(mv[s][:, 0, :], mv[s][:, 0, :], 0.5, None, ALU.mult)
                nc.vector.scalar_tensor_tensor(out=mv[s][:, 2, :], in0=mv[s][:, 2, :], scalar=0.25, in1=mv[s][:, 2, :],
                                               op0=ALU.mult, op1=ALU.mult).then_inc(stats_ready[s], 1)
                dve.wait_ge(stats_ready[s], 3 * (NORMS * r + layer) + 3)
                nc.vector.scalar_tensor_tensor(out=mv[s][:, 1, :], in0=mv[s][:, 1, :], scalar=1.0 / D, in1=mv[s][:, 2, :],
                                               op0=ALU.mult, op1=ALU.add).then_inc(var_ready[s], 1)

            def norm(s, r, layer):
                dve.wait_ge(pool_done[s], POOLS * r + POOL[f"rstd{layer}"])
                for t in range(TILES):
                    last = nc.vector.tensor_scalar(X[s][:, t, :], X[s][:, t, :], mv[s][:, 0, t:t + 1], rstd[s][:, t:t + 1],
                                                   ALU.subtract, ALU.mult)
                last.then_inc(normed[s], 1)

            def stage_x0(s, r):
                turn(s, r, "x0")

            def stage_query(s, r):
                dve.wait_ge(gT_hi_ready[s], GTS * r + GT["query"])
                lo_part(gT_lo[s][:, :], psB[s][:, :], gT_hi[s][:, :]).then_inc(gT_lo_ready[s], 1)

            def scores(s, r, tiles):
                for t in tiles:
                    dve.wait_ge(exp_done[s], (TILES + 2) * r + t + 1)
                    nc.vector.tensor_tensor(E[s][:, t, :], E[s][:, t, :], adjT[:, t, :], ALU.mult).then_inc(edges_ready[s], 1)

            def stage_scores01(s, r):
                scores(s, r, (0, 1))

            def stage_scores23(s, r):
                scores(s, r, (2, 3))

            def stage_out0(s, r):
                dve.wait_ge(product[s], PRODUCTS * r + PRODUCT["sums0"])
                nc.vector.reciprocal(rsum[s][:, :], psB[s][:, 0:TILES]).then_inc(vector_done[s], 1)
                dve.wait_ge(vector_done[s], VECTORS * r + VECTOR["rsum"])
                dve.wait_ge(stored[s], 16 * (r + 1))
                for t in range(TILES):
                    last = nc.vector.scalar_tensor_tensor(out=X[s][:, t, :], in0=psA[s][:, t * D:(t + 1) * D],
                                                          scalar=rsum[s][:, t:t + 1], in1=xin[s][:, t, :],
                                                          op0=ALU.mult, op1=ALU.add)
                last.then_inc(residual[s], 1)
                spread(s, r, 0)

            def stage_x1(s, r):
                turn(s, r, "x1")

            def elu(s, r, n, ps, bias, dst):
                dve.wait_ge(exp_done[s], (TILES + 2) * r + TILES + n)
                nc.vector.tensor_scalar(U[s][:, :], U[s][:, :], 1.0, -1.0, ALU.min, ALU.add).then_inc(vector_done[s], 1)
                dve.wait_ge(vector_done[s], VECTORS * r + VECTOR[f"elu_low{n}"])
                nc.vector.scalar_tensor_tensor(out=dst, in0=ps, scalar=bias, in1=U[s][:, :],
                                               op0=ALU.add, op1=ALU.max).then_inc(vector_done[s], 1)

            def stage_xh(s, r):
                elu(s, r, 1, psB[s][:, :], bi_sb[:, :], H[s][:, :])

            def stage_gates(s, r):
                dve.wait_ge(product[s], PRODUCTS * r + PRODUCT["src"])
                nc.vector.tensor_scalar(src_bias[s][:, :], psB[s][:, 0:TILES], be_sb[:, :], 0.5,
                                        ALU.add, ALU.mult).then_inc(vector_done[s], 1)

            def stage_turn_xh(s, r):
                for t in range(TILES):
                    dve.wait_ge(gate_done[s], TILES * r + t + 1)
                    nc.vector.scalar_tensor_tensor(out=E[s][:, t, :], in0=E[s][:, t, :], scalar=1.0, in1=edge_mask[:, t, :],
                                                   op0=ALU.add, op1=ALU.mult).then_inc(edges_ready[s], 1)

            def stage_agg(s, r):
                dve.wait_ge(gT_hi_ready[s], GTS * r + GT["agg"])
                lo_part(gT_lo[s][:, :], psA[s][:, :], gT_hi[s][:, :]).then_inc(gT_lo_ready[s], 1)
                dve.wait_ge(product[s], PRODUCTS * r + PRODUCT["sums1"])
                nc.vector.tensor_tensor(S[s][:, 1, :], psB[s][:, :], H[s][:, :], ALU.mult).then_inc(vector_done[s], 1)

            def stage_recv(s, r):
                elu(s, r, 2, psA[s][:, :], bn_sb[:, :], U[s][:, :])

            def stage_out1(s, r):
                dve.wait_ge(product[s], PRODUCTS * r + PRODUCT["out1"])
                dve.wait_ge(pool_done[s], POOLS * r + POOL["bias1"])
                nc.vector.tensor_tensor(X[s], psB[s][:, :].rearrange("p (t d) -> p t d", t=TILES), X[s],
                                        ALU.add).then_inc(residual[s], 1)
                spread(s, r, 1)

            def stage_x2(s, r):
                turn(s, r, "x2")

            def cheb(s, r, tiles):
                i, o = s // 2, s % 2
                for t in tiles:
                    ps = (psA, psB)[t % 2][s]
                    dve.wait_ge(cheb_kept[s], TILES * r + t + 1)
                    nc.vector.scalar_tensor_tensor(out=nh_lo[i][:, t, o, :], in0=ps[:, 2 * D:3 * D], scalar=dinv[:, t:t + 1],
                                                   in1=nh_hi[i][:, t, o, :].bitcast(F32),
                                                   op0=ALU.mult, op1=ALU.subtract).then_inc(cheb_lo_ready[s], 1)

            def stage_cheb01(s, r):
                cheb(s, r, (0, 1))

            def stage_cheb23(s, r):
                cheb(s, r, (2, 3))

            def half_bank(ps, t):
                return ps[:, (t % 2) * 2 * D:(t % 2 + 1) * 2 * D].rearrange("p (o d) -> p o d", o=2)

            def stage_lap1(s, r):
                i = s // 2
                for t in range(TILES):
                    dve.wait_ge(lap_ready[i], 4 * r + t // 2 + 1)
                    keep = keep_pair[i][:, :, t, D:2 * D]
                    nc.vector.scalar_tensor_tensor(out=keep, in0=half_bank(psA[2 * i + t // 2], t), scalar=neg_dinv[:, t:t + 1],
                                                   in1=keep, op0=ALU.mult, op1=ALU.add).then_inc(lap_sum[i], 1)
                for t in range(TILES):
                    dve.wait_ge(lap_hi_ready[i], TILES * r + t + 1)
                    nc.vector.scalar_tensor_tensor(out=nh_lo[i][:, t, :, :], in0=keep_pair[i][:, :, t, D:2 * D],
                                                   scalar=dinv[:, t:t + 1], in1=nh_hi[i][:, t, :, :].bitcast(F32),
                                                   op0=ALU.mult, op1=ALU.subtract).then_inc(lap_lo_ready[i], 1)

            def stage_lap2(s, r):
                i = s // 2
                for s in (2 * i, 2 * i + 1):
                    dve.wait_ge(pool_done[s], POOLS * r + POOL["bias2"])
                for t in range(TILES):
                    dve.wait_ge(lap_ready[i], 4 * r + 2 + t // 2 + 1)
                    keep = keep_pair[i][:, :, t, 0:D]
                    nc.vector.scalar_tensor_tensor(out=keep, in0=half_bank(psB[2 * i + t // 2], t), scalar=neg_dinv[:, t:t + 1],
                                                   in1=keep, op0=ALU.mult, op1=ALU.add).then_inc(cheb_out[i], 1)
                for o in range(2):
                    s = 2 * i + o
                    dve.wait_ge(cheb_out[i], TILES * (r + 1))
                    nc.vector.scalar_tensor_tensor(out=X[s], in0=cheb_keep[s][:, :, 0:D], scalar=0.0,
                                                   in1=X[s], op0=ALU.max, op1=ALU.add).then_inc(residual[s], 1)
                for o in range(2):
                    spread(2 * i + o, r, 2)

            def stage_x3(s, r):
                i, o = s // 2, s % 2
                dve.wait_ge(normed[s], NORMS * r + 3)
                dve.wait_ge(nh_hi_ready[s], NHS * r + NH["x3"])
                lo_part(nh_lo[i][:, :, o, :], X[s], nh_hi[i][:, :, o, :]).then_inc(nh_lo_ready[s], 1)

            def stage_m(s, r, k):
                dve.wait_ge(gT_hi_ready[s], GTS * r + GT[f"m{k}"])
                lo_part(gT_lo[s][:, :], psA[s][:, :], gT_hi[s][:, :]).then_inc(gT_lo_ready[s], 1)

            def stage_r(s, r, k):
                dve.wait_ge(r_done[s], STEPS * r + k + 1)
                if k == 0:
                    dve.wait_ge(copied[s], 3 * r + 3)
                nc.vector.scalar_tensor_tensor(out=rh[s], in0=r_gate[s], scalar=1.0, in1=H[s][:, :],
                                               op0=ALU.add, op1=ALU.mult).then_inc(vector_done[s], 1)

            def stage_v(s, r, k):
                dve.wait_ge(hv_done[s], STEPS * r + k + 1)
                nc.vector.scalar_tensor_tensor(out=h_new[s], in0=z_gate[s], scalar=1.0, in1=h_new[s],
                                               op0=ALU.add, op1=ALU.mult).then_inc(vector_done[s], 1)
                dve.wait_ge(vector_done[s], VECTORS * r + VECTOR[f"update{k}"])
                dve.wait_ge(pool_done[s], POOLS * r + POOL[f"kept{k}"])
                nc.vector.scalar_tensor_tensor(out=H[s][:, :], in0=h_new[s], scalar=0.5, in1=kept[s],
                                               op0=ALU.mult, op1=ALU.add).then_inc(vector_done[s], 1)

            def stage_t(s, r, k):
                i, o = s // 2, s % 2
                dve.wait_ge(nh_hi_ready[s], NHS * r + NH[f"h{k}"])
                lo_part(nh_lo[i][:, :, o, :], psA[s][:, :].rearrange("p (t d) -> p t d", t=TILES),
                        nh_hi[i][:, :, o, :]).then_inc(nh_lo_ready[s], 1)

            def stage_last(s, r):
                dve.wait_ge(turned[s], TURNS * r + TURNED[f"h{STEPS - 1}"])
                nc.vector.tensor_tensor(X[s], psA[s][:, :].rearrange("p (t d) -> p t d", t=TILES), X[s],
                                        ALU.add).then_inc(residual[s], 1)
                spread(s, r, 3)

            stages = {"x0": stage_x0, "query": stage_query, "scores01": stage_scores01, "scores23": stage_scores23,
                      "out0": stage_out0, "x1": stage_x1, "xh": stage_xh, "gates": stage_gates, "turn_xh": stage_turn_xh,
                      "agg": stage_agg, "recv": stage_recv, "out1": stage_out1, "x2": stage_x2, "cheb01": stage_cheb01,
                      "cheb23": stage_cheb23, "lap1": stage_lap1, "lap2": stage_lap2, "x3": stage_x3, "last": stage_last}
            for n in range(NORMS):
                stages[f"norm{n}"] = lambda s, r, n=n: norm(s, r, n)
            for k in range(STEPS):
                stages[f"m{k}"] = lambda s, r, k=k: stage_m(s, r, k)
                stages[f"r{k}"] = lambda s, r, k=k: stage_r(s, r, k)
                stages[f"v{k}"] = lambda s, r, k=k: stage_v(s, r, k)
                if k < STEPS - 1:
                    stages[f"t{k}"] = lambda s, r, k=k: stage_t(s, r, k)
            run("vector", stages, 0, first=True)
            with dve.Fori(1, ROUNDS) as r:
                run("vector", stages, r)
            run("vector", stages, ROUNDS, last=True)

        @block.tensor
        def _(pe):
            def transpose_tiles(dst, src):
                for t in range(TILES):
                    last = nc.tensor.transpose(dst[:, t * P:(t + 1) * P], src(t), ident[:, :])
                return last

            def three_pass(dst, w_hi, w_lo, m_hi, m_lo, start=True, stop=True):
                nc.tensor.matmul(dst, w_hi, m_hi, start=start, stop=False)
                nc.tensor.matmul(dst, w_hi, m_lo, start=False, stop=False)
                return nc.tensor.matmul(dst, w_lo, m_hi, start=False, stop=stop)

            pe.wait_ge(s_ident, 1)
            pe.wait_ge(s_qk, 32)
            for g in range(2):
                last = nc.tensor.transpose(psA[0][:, g * D:(g + 1) * D], qk_in[:, g, :], ident[:, :])
            last.then_inc(s_setup_turned, 1)
            pe.wait_ge(s_sum, 1)
            for g in range(3):
                nc.tensor.transpose(psA[1][:, g * D:(g + 1) * D], w_sum[:, g, :], ident[:, :])
            pe.wait_ge(s_gru, 16 * 5)
            for g in range(2):
                last = nc.tensor.transpose(psA[2][:, g * D:(g + 1) * D], u_in[:, g, :], ident[:, :])
            last.then_inc(s_setup_turned, 1)
            pe.wait_ge(s_adj, 16)
            for m in range(TILES):
                transpose_tiles(psB[m], lambda t: adj_in[:, t, m:N:TILES]).then_inc(s_setup_turned, 1)
            pe.wait_ge(s_setup_qkT, 1)
            nc.tensor.matmul(psA[3][:, 0:D], qkT[:, 0, :], qkT[:, 1, :], start=True, stop=True).then_inc(s_setup_qk, 1)
            pe.wait_ge(s_flag_cols, 1)
            nc.tensor.matmul(psA[3][0:1, D:D + 1], flag_cols[:, :], ones[:, 0:1], start=True, stop=True).then_inc(s_flag_sum, 1)
            pe.wait_ge(s_small, 16 * 15)
            pe.wait_ge(s_setup, 1)
            pe.wait_ge(s_flag, 1)
            inexact = pe.value_load(flag[0:1, 0:1])

            def stage_x0(s, r):
                pe.wait_ge(loaded[s], 16 * r + 16)
                pe.wait_ge(residual[s], NORMS * r + 1)
                transpose_tiles(psA[s], lambda t: xin[s][:, t, :]).then_inc(turned[s], 1)

            def stage_query(s, r):
                pe.wait_ge(xT_lo_ready[s], XTS * r + XT["x0"])
                three_pass(psB[s][:, :], qk_hi[:, :], qk_lo[:, :], xT_hi[s][:, :], xT_lo[s][:, :]).then_inc(product[s], 1)

            def scores(s, r, tiles):
                for t in tiles:
                    c = slice(t * P, (t + 1) * P)
                    if t >= 2:
                        pe.wait_ge(tanh_done[s], TILES * r + t - 1)
                    three_pass((psA, psB)[t % 2][s][:, :], xT_hi[s][:, c], xT_lo[s][:, c],
                               gT_hi[s][:, :], gT_lo[s][:, :]).then_inc(scores_ready[s], 1)

            def stage_scores01(s, r):
                pe.wait_ge(gT_lo_ready[s], GTS * r + GT["query"])
                scores(s, r, (0, 1))

            def stage_scores23(s, r):
                scores(s, r, (2, 3))

            def stage_mix(s, r):
                pe.wait_ge(edges_ready[s], 2 * TILES * r + TILES)
                for t in range(TILES):
                    last = nc.tensor.matmul(psA[s][:, :], xin[s][:, t, :], E[s][:, t, :], start=(t == 0), stop=(t == TILES - 1))
                last.then_inc(product[s], 1)

            def stage_out0(s, r):
                pe.wait_ge(copied[s], 3 * r + 1)
                for t in range(TILES):
                    last = nc.tensor.matmul(psA[s][:, t * D:(t + 1) * D], U[s][:, t * P:(t + 1) * P], v_sb[:, :], start=True, stop=True)
                last.then_inc(product[s], 1)
                pe.wait_ge(pool_done[s], POOLS * r + POOL["edge_sum0"])
                for t in range(TILES):
                    last = nc.tensor.matmul(psB[s][:, t:t + 1], S[s][:, 0, t * P:(t + 1) * P], ones[:, 0:1], start=True, stop=True)
                last.then_inc(product[s], 1)

            def stage_x1(s, r):
                pe.wait_ge(normed[s], NORMS * r + 1)
                transpose_tiles(psA[s], lambda t: X[s][:, t, :]).then_inc(turned[s], 1)

            def stage_xh(s, r):
                pe.wait_ge(xT_lo_ready[s], XTS * r + XT["x1"])
                three_pass(psB[s][:, :], Wi_hi[:, :], Wi_lo[:, :], xT_hi[s][:, :], xT_lo[s][:, :]).then_inc(product[s], 1)

            def stage_gates(s, r):
                pe.wait_ge(vector_done[s], VECTORS * r + VECTOR["elu1"])
                for t in range(TILES):
                    last = nc.tensor.matmul(psB[s][:, t:t + 1], H[s][:, t * P:(t + 1) * P], We_sb[:, 0:1], start=True, stop=True)
                last.then_inc(product[s], 1)
                nc.tensor.matmul(psA[s][:, :], tgt_rows[:, :], H[s][:, :], start=True, stop=True).then_inc(product[s], 1)

            def stage_turn_xh(s, r):
                pe.wait_ge(vector_done[s], VECTORS * r + VECTOR["src_bias"])
                transpose_tiles(psB[s], lambda t: H[s][:, t * P:(t + 1) * P]).then_inc(turned[s], 1)

            def stage_agg(s, r):
                pe.wait_ge(copied[s], 3 * r + 2)
                pe.wait_ge(edges_ready[s], 2 * TILES * r + 2 * TILES)
                for t in range(TILES):
                    last = nc.tensor.matmul(psA[s][:, :], U[s][:, t * P:(t + 1) * P], E[s][:, t, :], start=(t == 0), stop=(t == TILES - 1))
                last.then_inc(product[s], 1)
                pe.wait_ge(pool_done[s], POOLS * r + POOL["edge_sum1"])
                nc.tensor.matmul(psB[s][:, :], ones[:, :], S[s][:, 0, :], start=True, stop=True).then_inc(product[s], 1)

            def stage_recv(s, r):
                pe.wait_ge(gT_lo_ready[s], GTS * r + GT["agg"])
                three_pass(psA[s][:, :], Wn_hi[:, :], Wn_lo[:, :], gT_hi[s][:, :], gT_lo[s][:, :], stop=False)
                pe.wait_ge(vector_done[s], VECTORS * r + VECTOR["self"])
                nc.tensor.matmul(psA[s][:, :], Wn2[:, :], S[s][:, 1, :], start=False, stop=True).then_inc(product[s], 1)

            def stage_out1(s, r):
                pe.wait_ge(vector_done[s], VECTORS * r + VECTOR["elu2"])
                for t in range(TILES):
                    dst, c = psB[s][:, t * D:(t + 1) * D], slice(t * P, (t + 1) * P)
                    nc.tensor.matmul(dst, U[s][:, c], Wm_sb[:, 0, :], start=True, stop=False)
                    last = nc.tensor.matmul(dst, H[s][:, c], Wm_sb[:, 1, :], start=False, stop=True)
                last.then_inc(product[s], 1)

            def stage_x2(s, r):
                pe.wait_ge(normed[s], NORMS * r + 2)
                transpose_tiles(psA[s], lambda t: X[s][:, t, :]).then_inc(turned[s], 1)

            def cheb(s, r, tiles):
                for t in tiles:
                    c = slice(t * P, (t + 1) * P)
                    if t >= 2:
                        pe.wait_ge(cheb_lo_ready[s], TILES * r + t - 1)
                    three_pass((psA, psB)[t % 2][s][:, 0:3 * D], xT_hi[s][:, c], xT_lo[s][:, c],
                               C_hi[:, :, :].rearrange("p g d -> p (g d)"), C_lo[:, :, :].rearrange("p g d -> p (g d)")).then_inc(cheb_ready[s], 1)

            def stage_cheb01(s, r):
                pe.wait_ge(xT_lo_ready[s], XTS * r + XT["x2"])
                cheb(s, r, (0, 1))

            def stage_cheb23(s, r):
                cheb(s, r, (2, 3))

            def lap(i, ps, exact):
                for t in range(TILES):
                    dst = ps[2 * i + t // 2][:, (t % 2) * 2 * D:(t % 2 + 1) * 2 * D]
                    c = slice(t * P, (t + 1) * P)
                    for m in range(TILES):
                        hi = nh_hi[i][:, m, :, :].rearrange("p o d -> p (o d)")
                        lo = nh_lo[i][:, m, :, :].rearrange("p o d -> p (o d)")
                        nc.tensor.matmul(dst, adjT_hi[:, m, c], hi, start=(m == 0), stop=False)
                        last = nc.tensor.matmul(dst, adjT_hi[:, m, c], lo, start=False, stop=(exact and m == TILES - 1))
                        if not exact:
                            last = nc.tensor.matmul(dst, adjT_lo[:, m, c], hi, start=False, stop=(m == TILES - 1))
                    if t % 2:
                        last.then_inc(lap_ready[i], 1)

            def stage_lap1(s, r, exact):
                pe.wait_ge(cheb_lo_ready[s - 1], TILES * (r + 1))
                pe.wait_ge(cheb_lo_ready[s], TILES * (r + 1))
                lap(s // 2, psA, exact)

            def stage_lap2(s, r, exact):
                pe.wait_ge(lap_lo_ready[s // 2], TILES * (r + 1))
                lap(s // 2, psB, exact)

            def stage_x3(s, r):
                pe.wait_ge(normed[s], NORMS * r + 3)
                transpose_tiles(psA[s], lambda t: X[s][:, t, :]).then_inc(turned[s], 1)

            def stage_m(s, r, k, exact):
                i, o = s // 2, s % 2
                pe.wait_ge(nh_lo_ready[s], NHS * r + NH["x3" if k == 0 else f"h{k - 1}"])
                if k == 0:
                    pe.wait_ge(copied[s], 3 * r + 3)
                for m in range(TILES):
                    hi, lo = nh_hi[i][:, m, o, :], nh_lo[i][:, m, o, :]
                    nc.tensor.matmul(psA[s][:, :], hi, adjT_hi[:, m, :], start=(m == 0), stop=False)
                    last = nc.tensor.matmul(psA[s][:, :], lo, adjT_hi[:, m, :], start=False, stop=(exact and m == TILES - 1))
                    if not exact:
                        last = nc.tensor.matmul(psA[s][:, :], hi, adjT_lo[:, m, :], start=False, stop=(m == TILES - 1))
                last.then_inc(product[s], 1)

            def stage_r(s, r, k):
                if k > 0:
                    pe.wait_ge(z_done[s], STEPS * r + k)
                nc.tensor.matmul(psB[s][:, :], U3[:, :], H[s][:, :], start=True, stop=False)
                pe.wait_ge(gT_lo_ready[s], GTS * r + GT[f"m{k}"])
                three_pass(psB[s][:, :], Gw_hi[:, G_R, :], Gw_lo[:, G_R, :], gT_hi[s][:, :], gT_lo[s][:, :], start=False).then_inc(product[s], 1)

            def stage_v(s, r, k):
                three_pass(psA[s][:, :], Gw_hi[:, G_HV, :], Gw_lo[:, G_HV, :], gT_hi[s][:, :], gT_lo[s][:, :], stop=False)
                pe.wait_ge(r_done[s], STEPS * r + k + 1)
                nc.tensor.matmul(psB[s][:, :], Gw_hi[:, G_ZR, :], gT_hi[s][:, :], start=False, stop=False, skip_group_check=True)
                nc.tensor.matmul(psB[s][:, :], Gw_hi[:, G_ZR, :], gT_lo[s][:, :], start=False, stop=False, skip_group_check=True)
                nc.tensor.matmul(psB[s][:, :], Gw_lo[:, G_ZR, :], gT_hi[s][:, :], start=False, stop=True,
                                 skip_group_check=True).then_inc(product[s], 1)
                pe.wait_ge(vector_done[s], VECTORS * r + VECTOR[f"rh{k}"])
                nc.tensor.matmul(psA[s][:, :], U5[:, :], rh[s], start=False, stop=True).then_inc(product[s], 1)

            def stage_t(s, r, k):
                pe.wait_ge(vector_done[s], VECTORS * r + VECTOR[f"h{k}"])
                transpose_tiles(psA[s], lambda t: H[s][:, t * P:(t + 1) * P]).then_inc(turned[s], 1)

            def rounds(exact):
                stages = {"x0": stage_x0, "query": stage_query, "scores01": stage_scores01, "scores23": stage_scores23,
                          "mix": stage_mix, "out0": stage_out0, "x1": stage_x1, "xh": stage_xh, "gates": stage_gates,
                          "turn_xh": stage_turn_xh, "agg": stage_agg, "recv": stage_recv, "out1": stage_out1, "x2": stage_x2,
                          "cheb01": stage_cheb01, "cheb23": stage_cheb23,
                          "lap1": lambda s, r: stage_lap1(s, r, exact), "lap2": lambda s, r: stage_lap2(s, r, exact), "x3": stage_x3}
                for k in range(STEPS):
                    stages[f"m{k}"] = lambda s, r, k=k: stage_m(s, r, k, exact)
                    stages[f"r{k}"] = lambda s, r, k=k: stage_r(s, r, k)
                    stages[f"v{k}"] = lambda s, r, k=k: stage_v(s, r, k)
                    stages[f"t{k}"] = lambda s, r, k=k: stage_t(s, r, k)
                run("tensor", stages, 0, first=True)
                with pe.Fori(1, ROUNDS) as r:
                    run("tensor", stages, r)
                run("tensor", stages, ROUNDS, last=True)

            with pe.If(inexact == 0):
                rounds(exact=True)
            with pe.Else():
                rounds(exact=False)


_INS = ["x", "adj", "L0_gnn_q", "L0_gnn_k", "L0_gnn_v", "L1_gnn_Wi", "L1_gnn_bi", "L1_gnn_We", "L1_gnn_be",
        "L1_gnn_Wn", "L1_gnn_bn", "L1_gnn_Wm", "L1_gnn_bm", "L2_gnn_weight", "L2_gnn_bias",
        "L3_gnn_w3_w", "L3_gnn_w3_b", "L3_gnn_u3_w", "L3_gnn_u3_b", "L3_gnn_w4_w", "L3_gnn_w4_b",
        "L3_gnn_w5_w", "L3_gnn_w5_b", "L3_gnn_u5_w", "L3_gnn_u5_b"]


def kernel(**inputs):
    import numpy as _np
    import concourse.bacc as _bacc
    from concourse import mybir as _mybir
    from concourse.bass_utils import run_bass_kernel_spmd as _run

    nc = _bacc.Bacc("TRN2", target_bir_lowering=False, num_devices=1)
    arrays, args = {}, []
    for name in _INS:
        a = _np.ascontiguousarray(inputs[name])
        arrays[f"in_{name}"] = a
        args.append(nc.dram_tensor(f"in_{name}", a.shape, _mybir.dt.from_np(a.dtype), kind="ExternalInput").ap())
    shape = _np.shape(inputs["x"])
    args.append(nc.dram_tensor("out_0", shape, _mybir.dt.float32, kind="ExternalOutput").ap())
    build(nc, *args)
    r = _run(nc, [arrays], core_ids=[0])
    return r.results[0]["out_0"]
```

```python
from contextlib import ExitStack

import concourse.bass as bass
from concourse import mybir

F32 = mybir.dt.float32
F32R = mybir.dt.float32r
ALU = mybir.AluOpType
ACT = mybir.ActivationFunctionType
AX = mybir.AxisListType

P = 128
SLOTS = 4
PAIRS = SLOTS // 2
STEPS = 5
ALPHA = 0.005
EPS = 1e-5

SCHEDULE = [
    ("load", 2.4, 0, 0, 0),
    ("x0", 5.3, 10.4, 13.26, 0),
    ("query", 4.5, 9.5, 12.6, 0),
    ("scores01", 4.1, 10.4, 12.8, 0),
    ("scores23", 5.5, 10.5, 11.4, 2.4),
    ("mix", 2.7, 8.5, 0, 0),
    ("out0", 0.77, 0, 0, 0),
    ("sums0", 1.6, 0, 10.4, 0),
    ("spread0", 1.9, 0, 11.7, 0),
    ("norm0", 6.3, 0, 13.2, 0),
    ("x1", 6.5, 7, 13.6, 0.1),
    ("xh", 5.4, 7, 12, 0),
    ("gates", 5.5, 0, 12.6, 0),
    ("turn_xh", 6.7, 7.5, 11.1, 5.6),
    ("agg", 8.37, 9.5, 13.5, 0),
    ("sums1", 2.33, 5.2, 11.3, 0.3),
    ("recv", 1.67, 0, 0, 0),
    ("self", 4.53, 10, 12.7, 0),
    ("out1", 5.5, 0, 10.9, 0),
    ("spread1", 2.63, 0, 8, 6.6),
    ("norm1", 5.8, 0, 8.6, 0),
    ("x2", 7, 10, 9.7, 0),
    ("cheb01", 11, 10, 14.3, 0),
    ("cheb23", 75.9, 10.3, 11, 3.4),
    ("lap1", 14.8, 7.6, 13.1, 0),
    ("lap_lo", 48.83, 0, 10.7, 0),
    ("lap2", 10.5, 0, 10, 0),
    ("spread2", 9.53, 0, 9.5, 2.9),
    ("norm2", 9.4, 0, 8.3, 0),
    ("x3", 12.5, 2.5, 10.5, 0),
    ("m0", 14.63, 10.3, 13.7, 0),
    ("uh0", 5.47, 0, 0, 0),
    ("r0", 8, 9, 13.69, 0),
    ("v0", 5.17, 11.7, 0, 5.5),
    ("rh0", 3.77, 8.8, 10.5, 0),
    ("split0", 3.1, 7.3, 0, 0),
    ("t0", 6.7, 8.9, 10.26, 0),
    ("m1", 3.43, 10.3, 13.7, 0),
    ("uh1", 5.07, 0, 0, 0),
    ("r1", 3.3, 9, 12.29, 0),
    ("v1", 5.77, 11.7, 0, 5.5),
    ("rh1", 6.67, 8.8, 10.5, 0),
    ("split1", 0.2, 7.3, 0, 0),
    ("t1", 5.1, 8.9, 9.76, 0),
    ("m2", 5.43, 10.3, 13.7, 0),
    ("uh2", 4.47, 0, 0, 0),
    ("r2", 7.7, 9, 11.5, 0),
    ("v2", 3.17, 11.7, 0, 5.5),
    ("rh2", 10.57, 8.8, 10.59, 0),
    ("split2", 0, 7.3, 0, 0),
    ("t2", 11.9, 8.9, 10.26, 0),
    ("m3", 20.53, 10.3, 13.7, 0),
    ("uh3", 6.87, 0, 0, 0),
    ("r3", 50.9, 9, 11.5, 0),
    ("v3", 6.17, 11.7, 0, 5.5),
    ("rh3", 7.17, 8.8, 10.59, 0),
    ("split3", 1.7, 7.3, 0, 0),
    ("t3", 8.7, 8.9, 9.7, 0),
    ("m4", 5.93, 10.3, 13.7, 0),
    ("uh4", 0.57, 0, 0, 0),
    ("r4", 2.5, 9, 13.19, 0),
    ("v4", 3.97, 11.7, 0, 5.5),
    ("rh4", 1.2, 8.8, 13.1, 0),
    ("split4", 3.16, 0, 0, 0),
    ("t4", 0, 0, 0, 0),
    ("last", 0, 0, 11.5, 0),
    ("spread3", 5.13, 0, 12.72, 4.8),
    ("norm3", 0.7, 0, 12.5, 0),
    ("store", 4.8, 0, 0, 0),
]
STAGES = [(name, length) for name, length, *_ in SCHEDULE]
LAGS = {"scalar": 2, "vector": 3, "gpsimd": 4}
SLOT_LAG = 7.30
PAIR_LAG = 14.28


def elag(engine, n):
    return SCHEDULE[n][LAGS[engine]] if engine in LAGS else 0.0


def body(engine):
    period = sum(length for _, length in STAGES) + SLOT_LAG
    at = []
    for s in range(SLOTS):
        time = (s // 2) * PAIR_LAG + (s % 2) * SLOT_LAG
        for n, (name, length) in enumerate(STAGES):
            if name == "lap1" and s % 2 == 0 or name == "spread2" and s % 2 == 1:
                time += SLOT_LAG
            if name not in ("lap1", "lap_lo", "lap2") or s % 2:
                t = time + elag(engine, n)
                at.append((t % period, s, n, name, int(t // period)))
            time += length
    assert all(behind in (0, 1) for *_, behind in at)
    return [(name, s, behind) for _, s, _, name, behind in sorted(at)]


def run(engine, stages, r, first=False, last=False):
    for name, s, behind in body(engine):
        if name in stages and not (first and behind) and not (last and not behind):
            stages[name](s, r - behind)


TURNED = {"x0": 1, "x1": 2, "xh": 3, "x2": 4, "x3": 5, **{f"h{k}": 6 + k for k in range(STEPS)}}
XT = {"x0": 1, "x1": 2, "x2": 3}
XT_HI = {"x0": 1, "x1": 2, "sum": 3, "x2": 4, "x3": 5, **{f"h{k}": 6 + k for k in range(STEPS - 1)}}
XT_HIS = len(XT_HI)
GT = {"query": 1, "agg": 2, **{f"m{k}": 3 + k for k in range(STEPS)}}
NH = {"x3": 1, **{f"h{k}": 2 + k for k in range(STEPS - 1)}}
PRODUCT = {name: n + 1 for n, name in enumerate(
    ["query", "mix", "out0", "sums0", "xh", "src", "tgt", "agg", "sums1", "recv", "out1"]
    + [f"{name}{k}" for k in range(STEPS) for name in ("m", "r", "z", "hv")])}
VECTOR = {name: n + 1 for n, name in enumerate(
    ["rsum", "elu_low1", "elu1", "src_bias", "self", "elu_low2", "elu2"]
    + [f"{name}{k}" for k in range(STEPS) for name in ("rh", "update", "h")])}
POOL = {name: n + 1 for n, name in enumerate(
    ["half_sum0", "edge_sum0", "std0", "rstd0", "bias1", "half_sum1", "edge_sum1", "sum_lo", "std1", "rstd1", "bias2",
     "std2", "rstd2"] + [f"{name}{k}" for k in range(STEPS) for name in ("h_lo", "kept")] + ["std3", "rstd3"])}
TURNS, XTS, GTS, NHS, PRODUCTS, VECTORS, POOLS = map(len, (TURNED, XT, GT, NH, PRODUCT, VECTOR, POOL))
NORMS = 4


def build(nc, x, adj, q, k, v, Wi, bi, We, be, Wn, bn, Wm, bm, cheb_w, cheb_b,
          w3_w, w3_b, u3_w, u3_b, w4_w, w4_b, w5_w, w5_b, u5_w, u5_b, out):
    B, N, D = x.shape
    TILES = N // P
    ROUNDS = B // SLOTS
    SCORE_SCALE = 1.0 / (float(D) ** 0.5 * 8.0)
    assert D == P and N == TILES * P and B == ROUNDS * SLOTS

    with ExitStack() as ctx:
        def sb(name, shape, dt=F32):
            return ctx.enter_context(nc.sbuf_tensor(name, shape, dt))

        def sem(name):
            return ctx.enter_context(nc.semaphore(name))

        def sems(name, n=SLOTS):
            return [sem(f"{name}{i}") for i in range(n)]

        ident = sb("ident", [P, P])
        ones = sb("ones", [P, P])
        ones_r = sb("ones_r", [P, P], F32R)
        neg_half = sb("neg_half", [P, TILES])
        eps_cols = sb("eps_cols", [P, TILES])
        adjT = sb("adjT", [P, TILES, N])
        adjT_hi = sb("adjT_hi", [P, TILES, N], F32R)
        adjT_lo = sb("adjT_lo", [P, TILES, N], F32R)
        edge_mask = sb("edge_mask", [P, TILES, N])
        degree = sb("degree", [P, TILES])
        dinv = sb("dinv", [P, TILES])
        neg_dinv = sb("neg_dinv", [P, TILES])
        v_sb = sb("v_sb", [P, D])
        qk_hi, qk_lo = sb("qk_hi", [P, D], F32R), sb("qk_lo", [P, D], F32R)
        Wi_hi, Wi_lo = sb("Wi_hi", [P, D], F32R), sb("Wi_lo", [P, D], F32R)
        We_sb = sb("We_sb", [P, 2])
        tgt_rows = sb("tgt_rows", [P, P])
        Wn_hi, Wn_lo = sb("Wn_hi", [P, D], F32R), sb("Wn_lo", [P, D], F32R)
        Wn2 = sb("Wn2", [P, D])
        Wm_sb = sb("Wm_sb", [P, 2, D])
        C_hi, C_lo = sb("C_hi", [P, 3, D], F32R), sb("C_lo", [P, 3, D], F32R)
        G_R, G_ZR, G_HV = range(3)
        Gw_hi, Gw_lo = sb("Gw_hi", [P, 3, D], F32R), sb("Gw_lo", [P, 3, D], F32R)
        U3_hi, U3_lo = sb("U3_hi", [P, D], F32R), sb("U3_lo", [P, D], F32R)
        U5 = sb("u5T", [P, D])
        flag_cols, flag = sb("flag_cols", [P, 1]), sb("flag", [1, 1], mybir.dt.int32)
        bi_sb, bn_sb, be_sb = sb("bi_sb", [P, 1]), sb("bn_sb", [P, 1]), sb("be_sb", [P, 1])
        bm_rows, cb_rows = sb("bm_rows", [P, D]), sb("cb_rows", [P, D])
        gate_bias = sb("gate_bias", [P, 5])
        z_bias, r_bias, hv_bias = sb("z_bias", [P, 1]), sb("r_bias", [P, 1]), sb("hv_bias", [P, 1])

        def per_slot(name, shape, dt=F32):
            return [sb(f"{name}{s}", shape, dt) for s in range(SLOTS)]

        xin = per_slot("xin", [P, TILES, D])
        X_pair = [sb(f"X{i}", [P, 2, TILES, D]) for i in range(PAIRS)]
        X = [X_pair[s // 2][:, s % 2] for s in range(SLOTS)]
        xT_hi, xT_lo = per_slot("xT_hi", [P, N], F32R), per_slot("xT_lo", [P, N], F32R)
        gT_hi, gT_lo = per_slot("gT_hi", [P, N], F32R), per_slot("gT_lo", [P, N], F32R)
        E_pair = [sb(f"E{i}", [P, 2, TILES, N]) for i in range(PAIRS)]
        E = [E_pair[s // 2][:, s % 2] for s in range(SLOTS)]
        S = per_slot("S", [P, 2, N])
        U = per_slot("U", [P, N])
        H = per_slot("H", [P, N])
        stat = per_slot("stat", [P, TILES, 6])
        mv = per_slot("mv", [P, 3, TILES])
        rstd = per_slot("rstd", [P, TILES])
        rsum = per_slot("rsum", [P, TILES])
        src_bias = per_slot("src_bias", [P, TILES])
        nh_hi = [sb(f"nh_hi{i}", [P, TILES, 2, D], F32R) for i in range(PAIRS)]
        nh_lo = [sb(f"nh_lo{i}", [P, TILES, 2, D], F32R) for i in range(PAIRS)]

        psA = [ctx.enter_context(nc.psum_tensor(f"psA{s}", [P, N], F32)) for s in range(SLOTS)]
        psB = [ctx.enter_context(nc.psum_tensor(f"psB{s}", [P, N], F32)) for s in range(SLOTS)]

        adj_in = E[0]
        stage_w3 = E[1][:, :, :].rearrange("p t n -> p (t n)")
        w_in = stage_w3[:, 0:6 * D].rearrange("p (g h d) -> p g h d", g=3, h=2)
        w_sum = stage_w3[:, 6 * D:9 * D].rearrange("p (g d) -> p g d", g=3)
        u_in = stage_w3[:, 9 * D:11 * D].rearrange("p (g d) -> p g d", g=2)
        qk_in = stage_w3[:, 11 * D:13 * D].rearrange("p (g d) -> p g d", g=2)
        qkT = stage_w3[:, 13 * D:15 * D].rearrange("p (g d) -> p g d", g=2)
        stage_c = E[2][:, :, :].rearrange("p t n -> p (t n)")
        c_in = stage_c[:, 0:3 * D].rearrange("p (g d) -> p g d", g=3)
        c_sum = stage_c[:, 3 * D:6 * D].rearrange("p (g d) -> p g d", g=3)
        Wi_in = stage_c[:, 6 * D:7 * D]
        Wn_in = stage_c[:, 7 * D:8 * D]
        five = stage_c[:, 10 * D:15 * D].rearrange("p (g d) -> p g d", g=5)

        keep_pair = [E_pair[i][:, :, 0:2, :].rearrange("p o a (t c) -> p o (a t) c", c=2 * D) for i in range(PAIRS)]
        cheb_keep = [keep_pair[s // 2][:, s % 2] for s in range(SLOTS)]
        r_gate = [E[s][:, 0, :] for s in range(SLOTS)]
        z_gate = [E[s][:, 1, :] for s in range(SLOTS)]
        h_new = [E[s][:, 2, :] for s in range(SLOTS)]
        rh = [E[s][:, 3, :] for s in range(SLOTS)]
        kept = [S[s][:, 1, :] for s in range(SLOTS)]

        s_adj, s_qk, s_gru, s_cheb, s_small = sem("s_adj"), sem("s_qk"), sem("s_gru"), sem("s_cheb"), sem("s_small")
        s_const, s_ident0, s_ident = sem("s_const"), sem("s_ident0"), sem("s_ident")
        s_mask = sem("s_mask")
        s_setup_turned, s_setup_qkT, s_setup_qk = sem("s_setup_turned"), sem("s_setup_qkT"), sem("s_setup_qk")
        s_flag_cols, s_flag_sum, s_flag = sem("s_flag_cols"), sem("s_flag_sum"), sem("s_flag")
        s_sum, s_degree, s_dinv, s_setup, dve_step = sem("s_sum"), sem("s_degree"), sem("s_dinv"), sem("s_setup"), sem("dve_step")
        loaded, stored = sems("loaded"), sems("stored")
        turned = sems("turned")
        scores_ready = sems("scores_ready")
        product = sems("product")
        cheb_ready = sems("cheb_ready")
        lap_ready = sems("lap_ready", PAIRS)
        xT_hi_ready, gT_hi_ready, nh_hi_ready = sems("xT_hi_ready"), sems("gT_hi_ready"), sems("nh_hi_ready")
        tanh_done = sems("tanh_done")
        exp_done = sems("exp_done")
        gate_done = sems("gate_done")
        copied = sems("copied")
        cheb_kept = sems("cheb_kept")
        lap_hi_ready = sems("lap_hi_ready", PAIRS)
        r_done, z_done, hv_done = sems("r_done"), sems("z_done"), sems("hv_done")
        keep_done = sems("keep_done")
        xT_lo_ready, gT_lo_ready, nh_lo_ready = sems("xT_lo_ready"), sems("gT_lo_ready"), sems("nh_lo_ready")
        cheb_lo_ready = sems("cheb_lo_ready")
        lap_lo_ready = sems("lap_lo_ready", PAIRS)
        edges_ready = sems("edges_ready")
        residual = sems("residual")
        var_ready = sems("var_ready")
        vector_done = sems("vector_done")
        normed = sems("normed")
        stats_ready = sems("stats_ready")
        lap_sum = sems("lap_sum", PAIRS)
        cheb_out = sems("cheb_out", PAIRS)
        pool_done = sems("pool_done")

        def col(w):
            return w.rearrange("(p a) -> p a", a=1)

        def rows(w):
            return w.rearrange("(a n) -> a n", a=1).partition_broadcast(P)

        xg = x.rearrange("b (p t) d -> b p t d", t=TILES)
        og = out.rearrange("b (p t) d -> b p t d", t=TILES)

        block = ctx.enter_context(nc.Block())

        @block.sync
        def _(sp):
            for s in range(SLOTS):
                sp.sem_inc(stored[s], 16)
                sp.sem_inc(residual[s], 1)
            sp.dma_start(adj_in[:, :, :], adj.rearrange("(p t) m -> p t m", t=TILES)).then_inc(s_adj, 16)
            sp.dma_start(qk_in[:, 0, :], q).then_inc(s_qk, 16)
            sp.dma_start(qk_in[:, 1, :], k).then_inc(s_qk, 16)
            for s in range(SLOTS):
                sp.dma_start(xin[s][:, :, :], xg[s]).then_inc(loaded[s], 16)
            for g, w in enumerate((w3_w, w4_w, w5_w)):
                sp.dma_start(w_in[:, g, :, :], w.rearrange("p (h d) -> p h d", h=2)).then_inc(s_gru, 16)
            sp.dma_start(u_in[:, 0, :], u3_w).then_inc(s_gru, 16)
            sp.dma_start(u_in[:, 1, :], u5_w).then_inc(s_gru, 16)
            sp.dma_start(c_in[:, :, :], cheb_w.rearrange("k a c d -> c (k a) d")).then_inc(s_cheb, 16)

            def stage_load(s, r):
                if isinstance(r, int):
                    return
                sp.wait_ge(residual[s], NORMS * (r - 1) + 2)
                sp.dma_start(xin[s][:, :, :], xg[bass.ds(r * SLOTS + s, 1)].rearrange("a p t d -> p (a t) d")).then_inc(loaded[s], 16)

            def stage_store(s, r):
                sp.wait_ge(normed[s], NORMS * (r + 1))
                sp.dma_start(og[bass.ds(r * SLOTS + s, 1)].rearrange("a p t d -> p (a t) d"), X[s]).then_inc(stored[s], 16)

            stages = {"load": stage_load, "store": stage_store}
            run("sync", stages, 0, first=True)
            with sp.Fori(1, ROUNDS) as r:
                run("sync", stages, r)
            run("sync", stages, ROUNDS, last=True)
            for s in range(SLOTS):
                sp.wait_ge(stored[s], 16 * (ROUNDS + 1))

        @block.gpsimd
        def _(pool):
            nc.gpsimd.memset(ident[:, :], 0.0).then_inc(s_ident0, 1)
            nc.gpsimd.memset(ones[:, :], 1.0).then_inc(s_const, 1)
            nc.gpsimd.memset(neg_half[:, :], -0.5).then_inc(s_const, 1)
            nc.gpsimd.memset(eps_cols[:, :], EPS).then_inc(s_const, 1)
            pool.wait_ge(s_ident0, 1)
            nc.gpsimd.affine_select(out=ident[:, :], in_=ident[:, :], compare_op=ALU.not_equal, fill=1.0,
                                    base=0, pattern=[[-1, P]], channel_multiplier=1).then_inc(s_ident, 1)
            pool.wait_ge(s_degree, 1)
            pool.wait_ge(s_const, 3)
            nc.gpsimd.tensor_tensor(dinv[:, :], degree[:, :], neg_half[:, :], ALU.pow).then_inc(s_dinv, 1)
            pool.wait_ge(s_flag_cols, 1)
            nc.gpsimd.tensor_scalar(edge_mask[:, :, :], adjT[:, :, :], 0.0, ALPHA, ALU.is_equal, ALU.mult).then_inc(s_mask, 1)
            pool.wait_ge(s_mask, 1)
            nc.gpsimd.tensor_tensor(edge_mask[:, :, :], adjT[:, :, :], edge_mask[:, :, :], ALU.add).then_inc(s_mask, 1)
            pool.wait_ge(s_small, 16 * 15)
            pool.wait_ge(s_setup, 1)

            def edge_sums(s, r, layer):
                pool.wait_ge(edges_ready[s], 2 * TILES * r + TILES * (layer + 1))
                if layer == 1:
                    pool.wait_ge(product[s], PRODUCTS * r + PRODUCT["sums0"])
                nc.gpsimd.tensor_tensor(S[s][:, :, :], E[s][:, 0:2, :], E[s][:, 2:4, :], ALU.add).then_inc(pool_done[s], 1)
                pool.wait_ge(pool_done[s], POOLS * r + POOL[f"half_sum{layer}"])
                nc.gpsimd.tensor_tensor(S[s][:, 0, :], S[s][:, 0, :], S[s][:, 1, :], ALU.add).then_inc(pool_done[s], 1)

            def norm(s, r, layer):
                pool.wait_ge(var_ready[s], NORMS * r + layer + 1)
                nc.gpsimd.tensor_tensor(rstd[s][:, :], mv[s][:, 1, :], eps_cols[:, :], ALU.add).then_inc(pool_done[s], 1)
                pool.wait_ge(pool_done[s], POOLS * r + POOL[f"std{layer}"])
                nc.gpsimd.tensor_tensor(rstd[s][:, :], rstd[s][:, :], neg_half[:, :], ALU.pow).then_inc(pool_done[s], 1)

            def stage_scores23(s, r):
                edge_sums(s, r, 0)

            def stage_x1(s, r):
                pool.wait_ge(normed[s], NORMS * r + 1)
                pool.wait_ge(turned[s], TURNS * r + TURNED["x1"])
                nc.gpsimd.tensor_tensor(X[s], X[s],
                                        bm_rows[:, :].unsqueeze(1).to_broadcast([P, TILES, D]), ALU.add).then_inc(pool_done[s], 1)

            def stage_turn_xh(s, r):
                edge_sums(s, r, 1)

            def stage_sums1(s, r):
                pool.wait_ge(xT_hi_ready[s], XT_HIS * r + XT_HI["sum"])
                nc.gpsimd.tensor_tensor(xT_lo[s][:, :], S[s][:, 0, :], xT_hi[s][:, :].bitcast(F32), ALU.subtract).then_inc(pool_done[s], 1)

            def stage_cheb23(s, r):
                pool.wait_ge(cheb_kept[s], TILES * (r + 1))
                nc.gpsimd.tensor_tensor(cheb_keep[s][:, :, 0:D], cheb_keep[s][:, :, 0:D],
                                        cb_rows[:, :].unsqueeze(1).to_broadcast([P, TILES, D]), ALU.add).then_inc(pool_done[s], 1)

            def stage_m(s, r, k):
                pool.wait_ge(xT_hi_ready[s], XT_HIS * r + XT_HI["x3" if k == 0 else f"h{k - 1}"])
                if k == 0:
                    pool.wait_ge(copied[s], 3 * r + 3)
                nc.gpsimd.tensor_tensor(xT_lo[s][:, :], H[s][:, :], xT_hi[s][:, :].bitcast(F32), ALU.subtract).then_inc(pool_done[s], 1)

            def stage_v(s, r, k):
                pool.wait_ge(keep_done[s], STEPS * r + k + 1)
                nc.gpsimd.tensor_tensor(kept[s], kept[s], H[s][:, :], ALU.mult).then_inc(pool_done[s], 1)

            stages = {"scores23": stage_scores23, "x1": stage_x1, "turn_xh": stage_turn_xh, "sums1": stage_sums1,
                      "cheb23": stage_cheb23}
            for n in range(NORMS):
                stages[f"spread{n}"] = lambda s, r, n=n: norm(s, r, n)
            for k in range(STEPS):
                stages[f"m{k}"] = lambda s, r, k=k: stage_m(s, r, k)
                stages[f"v{k}"] = lambda s, r, k=k: stage_v(s, r, k)
            run("gpsimd", stages, 0, first=True)
            with pool.Fori(1, ROUNDS) as r:
                run("gpsimd", stages, r)
            run("gpsimd", stages, ROUNDS, last=True)

        @block.scalar
        def _(act):
            for g, b in enumerate((w3_b, w4_b, w5_b, u3_b, u5_b)):
                act.dma_start(gate_bias[:, g:g + 1], col(b)).then_inc(s_small, 16)
            act.dma_start(bi_sb[:, :], col(bi)).then_inc(s_small, 16)
            act.dma_start(bn_sb[:, :], col(bn)).then_inc(s_small, 16)
            for h in range(2):
                act.dma_start(We_sb[:, h:h + 1], We[h * P:(h + 1) * P, :]).then_inc(s_small, 16)
            act.dma_start(be_sb[:, :], rows(be)).then_inc(s_small, 16)
            act.dma_start(bm_rows[:, :], rows(bm)).then_inc(s_small, 16)
            act.dma_start(cb_rows[:, :], cheb_b.rearrange("a b d -> (a b) d").partition_broadcast(P)).then_inc(s_small, 16)
            act.dma_start(v_sb[:, :], v).then_inc(s_small, 16)
            act.dma_start(Wm_sb[:, :, :], Wm.rearrange("(h p) d -> p h d", h=2)).then_inc(s_small, 16)
            act.dma_start(Wi_in, Wi).then_inc(s_cheb, 16)
            act.dma_start(Wn_in, Wn[0:P, :]).then_inc(s_cheb, 16)
            act.dma_start(Wn2[:, :], Wn[P:2 * P, :]).then_inc(s_small, 16)
            act.wait_ge(s_small, 16 * 15)
            act.wait_ge(s_setup, 1)

            def turn(s, r, name):
                act.wait_ge(turned[s], TURNS * r + TURNED[name])
                nc.scalar.copy(xT_hi[s][:, :], psA[s][:, :]).then_inc(xT_hi_ready[s], 1)

            def stage_x0(s, r):
                turn(s, r, "x0")

            def stage_query(s, r):
                act.wait_ge(product[s], PRODUCTS * r + PRODUCT["query"])
                nc.scalar.copy(gT_hi[s][:, :], psB[s][:, :]).then_inc(gT_hi_ready[s], 1)

            def scores(s, r, tiles):
                for t in tiles:
                    ps = (psA, psB)[t % 2][s]
                    act.wait_ge(scores_ready[s], TILES * r + t + 1)
                    nc.scalar.activation(E[s][:, t, :], ps[:, :], ACT.Tanh, scale=SCORE_SCALE).then_inc(tanh_done[s], 1)
                for t in tiles:
                    act.wait_ge(tanh_done[s], TILES * r + t + 1)
                    nc.scalar.activation(E[s][:, t, :], E[s][:, t, :], ACT.Exp, scale=8.0).then_inc(exp_done[s], 1)

            def stage_scores01(s, r):
                scores(s, r, (0, 1))

            def stage_scores23(s, r):
                scores(s, r, (2, 3))

            def stage_mix(s, r):
                act.wait_ge(product[s], PRODUCTS * r + PRODUCT["mix"])
                nc.scalar.copy(U[s][:, :], psA[s][:, :]).then_inc(copied[s], 1)

            def stage_x1(s, r):
                turn(s, r, "x1")

            def stage_xh(s, r):
                act.wait_ge(product[s], PRODUCTS * r + PRODUCT["xh"])
                nc.scalar.activation(U[s][:, :], psB[s][:, :], ACT.Exp, bias=bi_sb[:, :]).then_inc(exp_done[s], 1)

            def stage_turn_xh(s, r):
                act.wait_ge(vector_done[s], VECTORS * r + VECTOR["src_bias"])
                act.wait_ge(product[s], PRODUCTS * r + PRODUCT["tgt"])
                for t in range(TILES):
                    nc.scalar.activation(E[s][:, t, :], psA[s][:, :], ACT.Tanh, scale=0.5,
                                         bias=src_bias[s][:, t:t + 1]).then_inc(gate_done[s], 1)
                act.wait_ge(turned[s], TURNS * r + TURNED["xh"])
                nc.scalar.copy(U[s][:, :], psB[s][:, :]).then_inc(copied[s], 1)

            def stage_sums1(s, r):
                act.wait_ge(pool_done[s], POOLS * r + POOL["edge_sum1"])
                nc.scalar.copy(xT_hi[s][:, :], S[s][:, 0, :]).then_inc(xT_hi_ready[s], 1)

            def stage_agg(s, r):
                act.wait_ge(product[s], PRODUCTS * r + PRODUCT["agg"])
                nc.scalar.copy(gT_hi[s][:, :], psA[s][:, :]).then_inc(gT_hi_ready[s], 1)

            def stage_self(s, r):
                act.wait_ge(product[s], PRODUCTS * r + PRODUCT["recv"])
                nc.scalar.activation(U[s][:, :], psA[s][:, :], ACT.Exp, bias=bn_sb[:, :]).then_inc(exp_done[s], 1)

            def stage_x2(s, r):
                turn(s, r, "x2")

            def cheb(s, r, tiles):
                i, o = s // 2, s % 2
                for t in tiles:
                    ps = (psA, psB)[t % 2][s]
                    act.wait_ge(cheb_ready[s], TILES * r + t + 1)
                    nc.scalar.activation(nh_hi[i][:, t, o, :], ps[:, 2 * D:3 * D], ACT.Copy,
                                         scale=dinv[:, t:t + 1])
                    nc.scalar.copy(cheb_keep[s][:, t, :], ps[:, 0:2 * D]).then_inc(cheb_kept[s], 1)

            def stage_cheb01(s, r):
                cheb(s, r, (0, 1))

            def stage_cheb23(s, r):
                cheb(s, r, (2, 3))

            def stage_lap1(s, r):
                i = s // 2
                act.wait_ge(lap_ready[i], 4 * r + 2)
                for t in range(TILES):
                    act.wait_ge(lap_sum[i], TILES * r + t + 1)
                    nc.scalar.activation(nh_hi[i][:, t, :, :], keep_pair[i][:, :, t, D:2 * D], ACT.Copy,
                                         scale=dinv[:, t:t + 1]).then_inc(lap_hi_ready[i], 1)

            def stage_x3(s, r):
                i, o = s // 2, s % 2
                act.wait_ge(normed[s], NORMS * r + 3)
                nc.scalar.copy(nh_hi[i][:, :, o, :], X[s]).then_inc(nh_hi_ready[s], 1)
                act.wait_ge(turned[s], TURNS * r + TURNED["x3"])
                nc.scalar.copy(xT_hi[s][:, :], psA[s][:, :]).then_inc(xT_hi_ready[s], 1)
                nc.scalar.copy(H[s][:, :], psA[s][:, :]).then_inc(copied[s], 1)

            def stage_m(s, r, k):
                act.wait_ge(product[s], PRODUCTS * r + PRODUCT[f"m{k}"])
                nc.scalar.copy(gT_hi[s][:, :], psA[s][:, :]).then_inc(gT_hi_ready[s], 1)

            def stage_r(s, r, k):
                act.wait_ge(product[s], PRODUCTS * r + PRODUCT[f"r{k}"])
                nc.scalar.activation(r_gate[s], psB[s][:, :], ACT.Tanh, scale=0.5, bias=r_bias[:, :]).then_inc(r_done[s], 1)

            def stage_v(s, r, k):
                act.wait_ge(product[s], PRODUCTS * r + PRODUCT[f"z{k}"])
                nc.scalar.activation(z_gate[s], psB[s][:, :], ACT.Tanh, scale=0.5, bias=z_bias[:, :]).then_inc(z_done[s], 1)
                act.wait_ge(z_done[s], STEPS * r + k + 1)
                nc.scalar.activation(kept[s], z_gate[s], ACT.Copy, scale=-0.5, bias=0.5).then_inc(keep_done[s], 1)

            def stage_rh(s, r, k):
                act.wait_ge(product[s], PRODUCTS * r + PRODUCT[f"hv{k}"])
                nc.scalar.activation(h_new[s], psA[s][:, :], ACT.Tanh, bias=hv_bias[:, :]).then_inc(hv_done[s], 1)

            def stage_split(s, r, k):
                act.wait_ge(vector_done[s], VECTORS * r + VECTOR[f"h{k}"])
                nc.scalar.copy(xT_hi[s][:, :], H[s][:, :]).then_inc(xT_hi_ready[s], 1)

            def stage_t(s, r, k):
                i, o = s // 2, s % 2
                act.wait_ge(turned[s], TURNS * r + TURNED[f"h{k}"])
                nc.scalar.copy(nh_hi[i][:, :, o, :], psA[s][:, :].rearrange("p (t d) -> p t d", t=TILES)).then_inc(nh_hi_ready[s], 1)

            stages = {"x0": stage_x0, "query": stage_query, "scores01": stage_scores01, "scores23": stage_scores23,
                      "mix": stage_mix, "x1": stage_x1, "xh": stage_xh, "turn_xh": stage_turn_xh, "agg": stage_agg,
                      "sums1": stage_sums1, "self": stage_self, "x2": stage_x2, "cheb01": stage_cheb01, "cheb23": stage_cheb23,
                      "lap1": stage_lap1, "x3": stage_x3}
            for k in range(STEPS):
                stages[f"m{k}"] = lambda s, r, k=k: stage_m(s, r, k)
                stages[f"r{k}"] = lambda s, r, k=k: stage_r(s, r, k)
                stages[f"v{k}"] = lambda s, r, k=k: stage_v(s, r, k)
                stages[f"rh{k}"] = lambda s, r, k=k: stage_rh(s, r, k)
                if k < STEPS - 1:
                    stages[f"split{k}"] = lambda s, r, k=k: stage_split(s, r, k)
                    stages[f"t{k}"] = lambda s, r, k=k: stage_t(s, r, k)
            run("scalar", stages, 0, first=True)
            with act.Fori(1, ROUNDS) as r:
                run("scalar", stages, r)
            run("scalar", stages, ROUNDS, last=True)

        @block.vector
        def _(dve):
            steps = [0]

            def link(instruction):
                steps[0] += 1
                instruction.then_inc(dve_step, 1)
                dve.wait_ge(dve_step, steps[0])

            def split_const(hi, lo, src):
                link(nc.vector.tensor_copy(hi, src))
                nc.vector.tensor_tensor(lo, src, hi.bitcast(F32), ALU.subtract)

            dve.wait_ge(s_adj, 16)
            nc.vector.tensor_reduce(degree[:, :], adj_in, AX.X, ALU.add).then_inc(s_degree, 1)
            dve.wait_ge(s_setup_turned, 1)
            nc.vector.tensor_copy(qkT, psA[0][:, 0:2 * D].rearrange("p (g d) -> p g d", g=2)).then_inc(s_setup_qkT, 1)
            for t in range(TILES):
                dve.wait_ge(s_setup_turned, 2 + t)
                last = nc.vector.tensor_copy(adjT[:, t, :], psB[t][:, :])
            link(last)
            link(nc.vector.tensor_copy(adjT_hi[:, :, :], adjT[:, :, :]))
            link(nc.vector.tensor_tensor(adjT_lo[:, :, :], adjT[:, :, :], adjT_hi[:, :, :].bitcast(F32), ALU.subtract))
            link(nc.vector.tensor_scalar(edge_mask[:, :, :], adjT_lo[:, :, :].bitcast(F32), 0.0, None, ALU.not_equal))
            nc.vector.tensor_reduce(flag_cols[:, :], edge_mask[:, :, :], AX.XY, ALU.max).then_inc(s_flag_cols, 1)
            dve.wait_ge(s_flag_cols, 1)
            dve.wait_ge(s_gru, 16 * 5)
            nc.vector.tensor_tensor(w_sum, w_in[:, :, 0, :], w_in[:, :, 1, :], ALU.add).then_inc(s_sum, 1)
            dve.wait_ge(s_setup_turned, 2 + TILES)
            nc.vector.tensor_copy(five[:, 3, :], psA[1][:, 0:D])
            nc.vector.tensor_copy(five[:, G_R, :], psA[1][:, D:2 * D])
            link(nc.vector.tensor_copy(five[:, G_HV, :], psA[1][:, 2 * D:3 * D]))
            nc.vector.tensor_copy(five[:, 4, :], psA[2][:, 0:D])
            nc.vector.tensor_scalar(U5[:, :], psA[2][:, D:2 * D], 0.5, None, ALU.mult)
            link(nc.vector.tensor_tensor(five[:, G_ZR, :], five[:, 3, :], five[:, G_R, :], ALU.subtract))
            split_const(Gw_hi[:, :, :], Gw_lo[:, :, :], five[:, 0:3, :])
            split_const(U3_hi[:, :], U3_lo[:, :], five[:, 4, :])
            dve.wait_ge(s_cheb, 16 * 3)
            nc.vector.tensor_tensor(c_sum[:, 0, :], c_in[:, 0, :], c_in[:, 1, :], ALU.add)
            nc.vector.scalar_tensor_tensor(out=c_sum[:, 1, :], in0=c_in[:, 2, :], scalar=4.0, in1=c_in[:, 1, :],
                                           op0=ALU.mult, op1=ALU.add)
            link(nc.vector.tensor_scalar(c_sum[:, 2, :], c_in[:, 2, :], 2.0, None, ALU.mult))
            link(nc.vector.tensor_tensor(c_sum[:, 0, :], c_sum[:, 0, :], c_in[:, 2, :], ALU.add))
            split_const(C_hi[:, :, :], C_lo[:, :, :], c_sum)
            split_const(Wi_hi[:, :], Wi_lo[:, :], Wi_in)
            link(nc.vector.tensor_scalar(Wn_in, Wn_in, 0.5, None, ALU.mult))
            split_const(Wn_hi[:, :], Wn_lo[:, :], Wn_in)
            dve.wait_ge(s_small, 16 * 15)
            dve.wait_ge(s_const, 3)
            nc.vector.tensor_scalar(Wn2[:, :], Wn2[:, :], 0.5, None, ALU.mult)
            nc.vector.tensor_copy(ones_r[:, :], ones[:, :])
            nc.vector.tensor_scalar(tgt_rows[:, :], ones[:, :], We_sb[:, 1:2], None, ALU.mult)
            nc.vector.tensor_tensor(hv_bias[:, :], gate_bias[:, 2:3], gate_bias[:, 4:5], ALU.add)
            nc.vector.tensor_tensor(z_bias[:, :], gate_bias[:, 0:1], gate_bias[:, 3:4], ALU.add)
            link(nc.vector.tensor_tensor(r_bias[:, :], gate_bias[:, 1:2], gate_bias[:, 3:4], ALU.add))
            nc.vector.tensor_scalar(z_bias[:, :], z_bias[:, :], 0.5, None, ALU.mult)
            nc.vector.tensor_scalar(r_bias[:, :], r_bias[:, :], 0.5, None, ALU.mult)
            dve.wait_ge(s_dinv, 1)
            nc.vector.tensor_scalar(neg_dinv[:, :], dinv[:, :], -1.0, None, ALU.mult)
            dve.wait_ge(s_flag_sum, 1)
            nc.vector.tensor_copy(flag[:, :], psA[3][0:1, D:D + 1]).then_inc(s_flag, 1)
            dve.wait_ge(s_setup_qk, 1)
            link(nc.vector.tensor_copy(five[:, 0, :], psA[3][:, 0:D]))
            link(nc.vector.tensor_copy(qk_hi[:, :], five[:, 0, :]))
            nc.vector.tensor_tensor(qk_lo[:, :], five[:, 0, :], qk_hi[:, :].bitcast(F32), ALU.subtract).then_inc(s_setup, 1)
            dve.wait_ge(s_setup, 1)

            def lo_part(lo, src, hi):
                return nc.vector.tensor_tensor(lo, src, hi.bitcast(F32), ALU.subtract)

            def turn(s, r, name):
                dve.wait_ge(xT_hi_ready[s], XT_HIS * r + XT_HI[name])
                lo_part(xT_lo[s][:, :], psA[s][:, :], xT_hi[s][:, :]).then_inc(xT_lo_ready[s], 1)

            def spread(s, r, layer):
                dve.wait_ge(residual[s], NORMS * r + layer + 2)
                for t in range(TILES):
                    last = nc.vector.bn_stats(out=stat[s][:, t, :], in_=X[s][:, t, :])
                last.then_inc(stats_ready[s], 1)
                dve.wait_ge(stats_ready[s], 3 * (NORMS * r + layer) + 1)
                mean_e, m2_e, mean_o, m2_o = (stat[s][:, :, n] for n in (1, 2, 4, 5))
                nc.vector.tensor_tensor(mv[s][:, 0, :], mean_e, mean_o, ALU.add)
                nc.vector.tensor_tensor(mv[s][:, 1, :], m2_e, m2_o, ALU.add)
                nc.vector.tensor_tensor(mv[s][:, 2, :], mean_e, mean_o, ALU.subtract).then_inc(stats_ready[s], 1)
                dve.wait_ge(stats_ready[s], 3 * (NORMS * r + layer) + 2)
                nc.vector.tensor_scalar(mv[s][:, 0, :], mv[s][:, 0, :], 0.5, None, ALU.mult)
                nc.vector.scalar_tensor_tensor(out=mv[s][:, 2, :], in0=mv[s][:, 2, :], scalar=0.25, in1=mv[s][:, 2, :],
                                               op0=ALU.mult, op1=ALU.mult).then_inc(stats_ready[s], 1)
                dve.wait_ge(stats_ready[s], 3 * (NORMS * r + layer) + 3)
                nc.vector.scalar_tensor_tensor(out=mv[s][:, 1, :], in0=mv[s][:, 1, :], scalar=1.0 / D, in1=mv[s][:, 2, :],
                                               op0=ALU.mult, op1=ALU.add).then_inc(var_ready[s], 1)

            def norm(s, r, layer):
                dve.wait_ge(pool_done[s], POOLS * r + POOL[f"rstd{layer}"])
                for t in range(TILES):
                    last = nc.vector.tensor_scalar(X[s][:, t, :], X[s][:, t, :], mv[s][:, 0, t:t + 1], rstd[s][:, t:t + 1],
                                                   ALU.subtract, ALU.mult)
                last.then_inc(normed[s], 1)

            def stage_x0(s, r):
                turn(s, r, "x0")

            def stage_query(s, r):
                dve.wait_ge(gT_hi_ready[s], GTS * r + GT["query"])
                lo_part(gT_lo[s][:, :], psB[s][:, :], gT_hi[s][:, :]).then_inc(gT_lo_ready[s], 1)

            def scores(s, r, tiles):
                for t in tiles:
                    dve.wait_ge(exp_done[s], (TILES + 2) * r + t + 1)
                    nc.vector.tensor_tensor(E[s][:, t, :], E[s][:, t, :], adjT[:, t, :], ALU.mult).then_inc(edges_ready[s], 1)

            def stage_scores01(s, r):
                scores(s, r, (0, 1))

            def stage_scores23(s, r):
                scores(s, r, (2, 3))

            def stage_sums0(s, r):
                dve.wait_ge(product[s], PRODUCTS * r + PRODUCT["sums0"])
                nc.vector.reciprocal(rsum[s][:, :], psB[s][:, 0:TILES]).then_inc(vector_done[s], 1)
                dve.wait_ge(vector_done[s], VECTORS * r + VECTOR["rsum"])
                dve.wait_ge(stored[s], 16 * (r + 1))
                for t in range(TILES):
                    last = nc.vector.scalar_tensor_tensor(out=X[s][:, t, :], in0=psA[s][:, t * D:(t + 1) * D],
                                                          scalar=rsum[s][:, t:t + 1], in1=xin[s][:, t, :],
                                                          op0=ALU.mult, op1=ALU.add)
                last.then_inc(residual[s], 1)

            def stage_x1(s, r):
                turn(s, r, "x1")

            def elu(s, r, n, ps, bias, dst):
                dve.wait_ge(exp_done[s], (TILES + 2) * r + TILES + n)
                nc.vector.tensor_scalar(U[s][:, :], U[s][:, :], 1.0, -1.0, ALU.min, ALU.add).then_inc(vector_done[s], 1)
                dve.wait_ge(vector_done[s], VECTORS * r + VECTOR[f"elu_low{n}"])
                nc.vector.scalar_tensor_tensor(out=dst, in0=ps, scalar=bias, in1=U[s][:, :],
                                               op0=ALU.add, op1=ALU.max).then_inc(vector_done[s], 1)

            def stage_xh(s, r):
                elu(s, r, 1, psB[s][:, :], bi_sb[:, :], H[s][:, :])

            def stage_gates(s, r):
                dve.wait_ge(product[s], PRODUCTS * r + PRODUCT["src"])
                nc.vector.tensor_scalar(src_bias[s][:, :], psB[s][:, 0:TILES], be_sb[:, :], 0.5,
                                        ALU.add, ALU.mult).then_inc(vector_done[s], 1)

            def stage_turn_xh(s, r):
                dve.wait_ge(s_mask, 2)
                for t in range(TILES):
                    dve.wait_ge(gate_done[s], TILES * r + t + 1)
                    nc.vector.scalar_tensor_tensor(out=E[s][:, t, :], in0=E[s][:, t, :], scalar=1.0, in1=edge_mask[:, t, :],
                                                   op0=ALU.add, op1=ALU.mult).then_inc(edges_ready[s], 1)

            def stage_agg(s, r):
                dve.wait_ge(gT_hi_ready[s], GTS * r + GT["agg"])
                lo_part(gT_lo[s][:, :], psA[s][:, :], gT_hi[s][:, :]).then_inc(gT_lo_ready[s], 1)

            def stage_sums1(s, r):
                dve.wait_ge(product[s], PRODUCTS * r + PRODUCT["sums1"])
                nc.vector.tensor_tensor(S[s][:, 1, :], psB[s][:, :], H[s][:, :], ALU.mult).then_inc(vector_done[s], 1)

            def stage_self(s, r):
                elu(s, r, 2, psA[s][:, :], bn_sb[:, :], U[s][:, :])

            def stage_out1(s, r):
                dve.wait_ge(product[s], PRODUCTS * r + PRODUCT["out1"])
                dve.wait_ge(pool_done[s], POOLS * r + POOL["bias1"])
                nc.vector.tensor_tensor(X[s], psB[s][:, :].rearrange("p (t d) -> p t d", t=TILES), X[s],
                                        ALU.add).then_inc(residual[s], 1)

            def stage_x2(s, r):
                turn(s, r, "x2")

            def cheb(s, r, tiles):
                i, o = s // 2, s % 2
                for t in tiles:
                    ps = (psA, psB)[t % 2][s]
                    dve.wait_ge(cheb_kept[s], TILES * r + t + 1)
                    nc.vector.scalar_tensor_tensor(out=nh_lo[i][:, t, o, :], in0=ps[:, 2 * D:3 * D], scalar=dinv[:, t:t + 1],
                                                   in1=nh_hi[i][:, t, o, :].bitcast(F32),
                                                   op0=ALU.mult, op1=ALU.subtract).then_inc(cheb_lo_ready[s], 1)

            def stage_cheb01(s, r):
                cheb(s, r, (0, 1))

            def stage_cheb23(s, r):
                cheb(s, r, (2, 3))

            def half_bank(ps, t):
                return ps[:, (t % 2) * 2 * D:(t % 2 + 1) * 2 * D].rearrange("p (o d) -> p o d", o=2)

            def stage_lap1(s, r):
                i = s // 2
                for t in range(TILES):
                    dve.wait_ge(lap_ready[i], 4 * r + t // 2 + 1)
                    keep = keep_pair[i][:, :, t, D:2 * D]
                    nc.vector.scalar_tensor_tensor(out=keep, in0=half_bank(psA[2 * i + t // 2], t), scalar=neg_dinv[:, t:t + 1],
                                                   in1=keep, op0=ALU.mult, op1=ALU.add).then_inc(lap_sum[i], 1)

            def stage_lap_lo(s, r):
                i = s // 2
                for t in range(TILES):
                    dve.wait_ge(lap_hi_ready[i], TILES * r + t + 1)
                    nc.vector.scalar_tensor_tensor(out=nh_lo[i][:, t, :, :], in0=keep_pair[i][:, :, t, D:2 * D],
                                                   scalar=dinv[:, t:t + 1], in1=nh_hi[i][:, t, :, :].bitcast(F32),
                                                   op0=ALU.mult, op1=ALU.subtract).then_inc(lap_lo_ready[i], 1)

            def stage_lap2(s, r):
                i = s // 2
                for s in (2 * i, 2 * i + 1):
                    dve.wait_ge(pool_done[s], POOLS * r + POOL["bias2"])
                for t in range(TILES):
                    dve.wait_ge(lap_ready[i], 4 * r + 2 + t // 2 + 1)
                    keep = keep_pair[i][:, :, t, 0:D]
                    nc.vector.scalar_tensor_tensor(out=keep, in0=half_bank(psB[2 * i + t // 2], t), scalar=neg_dinv[:, t:t + 1],
                                                   in1=keep, op0=ALU.mult, op1=ALU.add).then_inc(cheb_out[i], 1)
                for o in range(2):
                    s = 2 * i + o
                    dve.wait_ge(cheb_out[i], TILES * (r + 1))
                    nc.vector.scalar_tensor_tensor(out=X[s], in0=cheb_keep[s][:, :, 0:D], scalar=0.0,
                                                   in1=X[s], op0=ALU.max, op1=ALU.add).then_inc(residual[s], 1)

            def stage_x3(s, r):
                i, o = s // 2, s % 2
                dve.wait_ge(normed[s], NORMS * r + 3)
                dve.wait_ge(nh_hi_ready[s], NHS * r + NH["x3"])
                lo_part(nh_lo[i][:, :, o, :], X[s], nh_hi[i][:, :, o, :]).then_inc(nh_lo_ready[s], 1)

            def stage_m(s, r, k):
                dve.wait_ge(gT_hi_ready[s], GTS * r + GT[f"m{k}"])
                lo_part(gT_lo[s][:, :], psA[s][:, :], gT_hi[s][:, :]).then_inc(gT_lo_ready[s], 1)

            def stage_r(s, r, k):
                dve.wait_ge(r_done[s], STEPS * r + k + 1)
                if k == 0:
                    dve.wait_ge(copied[s], 3 * r + 3)
                nc.vector.scalar_tensor_tensor(out=rh[s], in0=r_gate[s], scalar=1.0, in1=H[s][:, :],
                                               op0=ALU.add, op1=ALU.mult).then_inc(vector_done[s], 1)

            def stage_rh(s, r, k):
                dve.wait_ge(hv_done[s], STEPS * r + k + 1)
                nc.vector.scalar_tensor_tensor(out=h_new[s], in0=z_gate[s], scalar=1.0, in1=h_new[s],
                                               op0=ALU.add, op1=ALU.mult).then_inc(vector_done[s], 1)
                dve.wait_ge(vector_done[s], VECTORS * r + VECTOR[f"update{k}"])
                dve.wait_ge(pool_done[s], POOLS * r + POOL[f"kept{k}"])
                nc.vector.scalar_tensor_tensor(out=H[s][:, :], in0=h_new[s], scalar=0.5, in1=kept[s],
                                               op0=ALU.mult, op1=ALU.add).then_inc(vector_done[s], 1)

            def stage_t(s, r, k):
                i, o = s // 2, s % 2
                dve.wait_ge(nh_hi_ready[s], NHS * r + NH[f"h{k}"])
                lo_part(nh_lo[i][:, :, o, :], psA[s][:, :].rearrange("p (t d) -> p t d", t=TILES),
                        nh_hi[i][:, :, o, :]).then_inc(nh_lo_ready[s], 1)

            def stage_last(s, r):
                dve.wait_ge(turned[s], TURNS * r + TURNED[f"h{STEPS - 1}"])
                nc.vector.tensor_tensor(X[s], psA[s][:, :].rearrange("p (t d) -> p t d", t=TILES), X[s],
                                        ALU.add).then_inc(residual[s], 1)

            stages = {"x0": stage_x0, "query": stage_query, "scores01": stage_scores01, "scores23": stage_scores23,
                      "sums0": stage_sums0, "x1": stage_x1, "xh": stage_xh, "gates": stage_gates, "turn_xh": stage_turn_xh,
                      "agg": stage_agg, "sums1": stage_sums1, "self": stage_self, "out1": stage_out1, "x2": stage_x2, "cheb01": stage_cheb01,
                      "cheb23": stage_cheb23, "lap1": stage_lap1, "lap_lo": stage_lap_lo, "lap2": stage_lap2, "x3": stage_x3, "last": stage_last}
            for n in range(NORMS):
                stages[f"spread{n}"] = lambda s, r, n=n: spread(s, r, n)
                stages[f"norm{n}"] = lambda s, r, n=n: norm(s, r, n)
            for k in range(STEPS):
                stages[f"m{k}"] = lambda s, r, k=k: stage_m(s, r, k)
                stages[f"r{k}"] = lambda s, r, k=k: stage_r(s, r, k)
                stages[f"rh{k}"] = lambda s, r, k=k: stage_rh(s, r, k)
                if k < STEPS - 1:
                    stages[f"t{k}"] = lambda s, r, k=k: stage_t(s, r, k)
            run("vector", stages, 0, first=True)
            with dve.Fori(1, ROUNDS) as r:
                run("vector", stages, r)
            run("vector", stages, ROUNDS, last=True)

        @block.tensor
        def _(pe):
            def transpose_tiles(dst, src):
                for t in range(TILES):
                    last = nc.tensor.transpose(dst[:, t * P:(t + 1) * P], src(t), ident[:, :])
                return last

            def three_pass(dst, w_hi, w_lo, m_hi, m_lo, start=True, stop=True):
                nc.tensor.matmul(dst, w_hi, m_hi, start=start, stop=False)
                nc.tensor.matmul(dst, w_hi, m_lo, start=False, stop=False)
                return nc.tensor.matmul(dst, w_lo, m_hi, start=False, stop=stop)

            pe.wait_ge(s_ident, 1)
            pe.wait_ge(s_qk, 32)
            for g in range(2):
                last = nc.tensor.transpose(psA[0][:, g * D:(g + 1) * D], qk_in[:, g, :], ident[:, :])
            last.then_inc(s_setup_turned, 1)
            pe.wait_ge(s_adj, 16)
            for m in range(TILES):
                transpose_tiles(psB[m], lambda t: adj_in[:, t, m:N:TILES]).then_inc(s_setup_turned, 1)
            pe.wait_ge(s_setup_qkT, 1)
            nc.tensor.matmul(psA[3][:, 0:D], qkT[:, 0, :], qkT[:, 1, :], start=True, stop=True).then_inc(s_setup_qk, 1)
            pe.wait_ge(s_sum, 1)
            for g in range(3):
                nc.tensor.transpose(psA[1][:, g * D:(g + 1) * D], w_sum[:, g, :], ident[:, :])
            pe.wait_ge(s_gru, 16 * 5)
            for g in range(2):
                last = nc.tensor.transpose(psA[2][:, g * D:(g + 1) * D], u_in[:, g, :], ident[:, :])
            last.then_inc(s_setup_turned, 1)
            pe.wait_ge(s_flag_cols, 1)
            nc.tensor.matmul(psA[3][0:1, D:D + 1], flag_cols[:, :], ones[:, 0:1], start=True, stop=True).then_inc(s_flag_sum, 1)
            pe.wait_ge(s_small, 16 * 15)
            pe.wait_ge(s_setup, 1)
            pe.wait_ge(s_flag, 1)
            inexact = pe.value_load(flag[0:1, 0:1])

            def stage_x0(s, r):
                pe.wait_ge(loaded[s], 16 * r + 16)
                pe.wait_ge(residual[s], NORMS * r + 1)
                transpose_tiles(psA[s], lambda t: xin[s][:, t, :]).then_inc(turned[s], 1)

            def stage_query(s, r):
                pe.wait_ge(xT_lo_ready[s], XTS * r + XT["x0"])
                three_pass(psB[s][:, :], qk_hi[:, :], qk_lo[:, :], xT_hi[s][:, :], xT_lo[s][:, :]).then_inc(product[s], 1)

            def scores(s, r, tiles):
                for t in tiles:
                    c = slice(t * P, (t + 1) * P)
                    if t >= 2:
                        pe.wait_ge(tanh_done[s], TILES * r + t - 1)
                    three_pass((psA, psB)[t % 2][s][:, :], xT_hi[s][:, c], xT_lo[s][:, c],
                               gT_hi[s][:, :], gT_lo[s][:, :]).then_inc(scores_ready[s], 1)

            def stage_scores01(s, r):
                pe.wait_ge(gT_lo_ready[s], GTS * r + GT["query"])
                scores(s, r, (0, 1))

            def stage_scores23(s, r):
                scores(s, r, (2, 3))

            def stage_mix(s, r):
                pe.wait_ge(edges_ready[s], 2 * TILES * r + TILES)
                for t in range(TILES):
                    last = nc.tensor.matmul(psA[s][:, :], xin[s][:, t, :], E[s][:, t, :], start=(t == 0), stop=(t == TILES - 1))
                last.then_inc(product[s], 1)

            def stage_out0(s, r):
                pe.wait_ge(copied[s], 3 * r + 1)
                for t in range(TILES):
                    last = nc.tensor.matmul(psA[s][:, t * D:(t + 1) * D], U[s][:, t * P:(t + 1) * P], v_sb[:, :], start=True, stop=True)
                last.then_inc(product[s], 1)

            def stage_sums0(s, r):
                pe.wait_ge(pool_done[s], POOLS * r + POOL["edge_sum0"])
                for t in range(TILES):
                    last = nc.tensor.matmul(psB[s][:, t:t + 1], S[s][:, 0, t * P:(t + 1) * P], ones[:, 0:1], start=True, stop=True)
                last.then_inc(product[s], 1)

            def stage_x1(s, r):
                pe.wait_ge(normed[s], NORMS * r + 1)
                transpose_tiles(psA[s], lambda t: X[s][:, t, :]).then_inc(turned[s], 1)

            def stage_xh(s, r):
                pe.wait_ge(xT_lo_ready[s], XTS * r + XT["x1"])
                three_pass(psB[s][:, :], Wi_hi[:, :], Wi_lo[:, :], xT_hi[s][:, :], xT_lo[s][:, :]).then_inc(product[s], 1)

            def stage_gates(s, r):
                pe.wait_ge(vector_done[s], VECTORS * r + VECTOR["elu1"])
                for t in range(TILES):
                    last = nc.tensor.matmul(psB[s][:, t:t + 1], H[s][:, t * P:(t + 1) * P], We_sb[:, 0:1], start=True, stop=True)
                last.then_inc(product[s], 1)
                nc.tensor.matmul(psA[s][:, :], tgt_rows[:, :], H[s][:, :], start=True, stop=True).then_inc(product[s], 1)

            def stage_turn_xh(s, r):
                pe.wait_ge(vector_done[s], VECTORS * r + VECTOR["src_bias"])
                transpose_tiles(psB[s], lambda t: H[s][:, t * P:(t + 1) * P]).then_inc(turned[s], 1)

            def stage_agg(s, r):
                pe.wait_ge(copied[s], 3 * r + 2)
                pe.wait_ge(edges_ready[s], 2 * TILES * r + 2 * TILES)
                for t in range(TILES):
                    last = nc.tensor.matmul(psA[s][:, :], U[s][:, t * P:(t + 1) * P], E[s][:, t, :], start=(t == 0), stop=(t == TILES - 1))
                last.then_inc(product[s], 1)

            def stage_sums1(s, r):
                pe.wait_ge(pool_done[s], POOLS * r + POOL["sum_lo"])
                nc.tensor.matmul(psB[s][:, :], ones_r[:, :], xT_hi[s][:, :], start=True, stop=False)
                nc.tensor.matmul(psB[s][:, :], ones_r[:, :], xT_lo[s][:, :], start=False, stop=True).then_inc(product[s], 1)

            def stage_recv(s, r):
                pe.wait_ge(gT_lo_ready[s], GTS * r + GT["agg"])
                three_pass(psA[s][:, :], Wn_hi[:, :], Wn_lo[:, :], gT_hi[s][:, :], gT_lo[s][:, :], stop=False)

            def stage_self(s, r):
                pe.wait_ge(vector_done[s], VECTORS * r + VECTOR["self"])
                nc.tensor.matmul(psA[s][:, :], Wn2[:, :], S[s][:, 1, :], start=False, stop=True).then_inc(product[s], 1)

            def stage_out1(s, r):
                pe.wait_ge(vector_done[s], VECTORS * r + VECTOR["elu2"])
                for t in range(TILES):
                    dst, c = psB[s][:, t * D:(t + 1) * D], slice(t * P, (t + 1) * P)
                    nc.tensor.matmul(dst, U[s][:, c], Wm_sb[:, 0, :], start=True, stop=False)
                    last = nc.tensor.matmul(dst, H[s][:, c], Wm_sb[:, 1, :], start=False, stop=True)
                last.then_inc(product[s], 1)

            def stage_x2(s, r):
                pe.wait_ge(normed[s], NORMS * r + 2)
                transpose_tiles(psA[s], lambda t: X[s][:, t, :]).then_inc(turned[s], 1)

            def cheb(s, r, tiles):
                for t in tiles:
                    c = slice(t * P, (t + 1) * P)
                    if t >= 2:
                        pe.wait_ge(cheb_lo_ready[s], TILES * r + t - 1)
                    three_pass((psA, psB)[t % 2][s][:, 0:3 * D], xT_hi[s][:, c], xT_lo[s][:, c],
                               C_hi[:, :, :].rearrange("p g d -> p (g d)"), C_lo[:, :, :].rearrange("p g d -> p (g d)")).then_inc(cheb_ready[s], 1)

            def stage_cheb01(s, r):
                pe.wait_ge(xT_lo_ready[s], XTS * r + XT["x2"])
                cheb(s, r, (0, 1))

            def stage_cheb23(s, r):
                cheb(s, r, (2, 3))

            def lap(i, ps, exact):
                for t in range(TILES):
                    dst = ps[2 * i + t // 2][:, (t % 2) * 2 * D:(t % 2 + 1) * 2 * D]
                    c = slice(t * P, (t + 1) * P)
                    for m in range(TILES):
                        hi = nh_hi[i][:, m, :, :].rearrange("p o d -> p (o d)")
                        lo = nh_lo[i][:, m, :, :].rearrange("p o d -> p (o d)")
                        nc.tensor.matmul(dst, adjT_hi[:, m, c], hi, start=(m == 0), stop=False)
                        last = nc.tensor.matmul(dst, adjT_hi[:, m, c], lo, start=False, stop=(exact and m == TILES - 1))
                        if not exact:
                            last = nc.tensor.matmul(dst, adjT_lo[:, m, c], hi, start=False, stop=(m == TILES - 1))
                    if t % 2:
                        last.then_inc(lap_ready[i], 1)

            def stage_lap1(s, r, exact):
                pe.wait_ge(cheb_lo_ready[s - 1], TILES * (r + 1))
                pe.wait_ge(cheb_lo_ready[s], TILES * (r + 1))
                lap(s // 2, psA, exact)

            def stage_lap2(s, r, exact):
                pe.wait_ge(lap_lo_ready[s // 2], TILES * (r + 1))
                lap(s // 2, psB, exact)

            def stage_x3(s, r):
                pe.wait_ge(normed[s], NORMS * r + 3)
                transpose_tiles(psA[s], lambda t: X[s][:, t, :]).then_inc(turned[s], 1)

            def stage_m(s, r, k, exact):
                i, o = s // 2, s % 2
                pe.wait_ge(nh_lo_ready[s], NHS * r + NH["x3" if k == 0 else f"h{k - 1}"])
                if k == 0:
                    pe.wait_ge(copied[s], 3 * r + 3)
                for m in range(TILES):
                    hi, lo = nh_hi[i][:, m, o, :], nh_lo[i][:, m, o, :]
                    nc.tensor.matmul(psA[s][:, :], hi, adjT_hi[:, m, :], start=(m == 0), stop=False)
                    last = nc.tensor.matmul(psA[s][:, :], lo, adjT_hi[:, m, :], start=False, stop=(exact and m == TILES - 1))
                    if not exact:
                        last = nc.tensor.matmul(psA[s][:, :], hi, adjT_lo[:, m, :], start=False, stop=(m == TILES - 1))
                last.then_inc(product[s], 1)

            def stage_uh(s, r, k):
                if k > 0:
                    pe.wait_ge(z_done[s], STEPS * r + k)
                pe.wait_ge(pool_done[s], POOLS * r + POOL[f"h_lo{k}"])
                three_pass(psB[s][:, :], U3_hi[:, :], U3_lo[:, :], xT_hi[s][:, :], xT_lo[s][:, :], stop=False)

            def stage_r(s, r, k):
                pe.wait_ge(gT_lo_ready[s], GTS * r + GT[f"m{k}"])
                three_pass(psB[s][:, :], Gw_hi[:, G_R, :], Gw_lo[:, G_R, :], gT_hi[s][:, :], gT_lo[s][:, :], start=False).then_inc(product[s], 1)

            def stage_v(s, r, k):
                three_pass(psA[s][:, :], Gw_hi[:, G_HV, :], Gw_lo[:, G_HV, :], gT_hi[s][:, :], gT_lo[s][:, :], stop=False)
                pe.wait_ge(r_done[s], STEPS * r + k + 1)
                nc.tensor.matmul(psB[s][:, :], Gw_hi[:, G_ZR, :], gT_hi[s][:, :], start=False, stop=False, skip_group_check=True)
                nc.tensor.matmul(psB[s][:, :], Gw_hi[:, G_ZR, :], gT_lo[s][:, :], start=False, stop=False, skip_group_check=True)
                nc.tensor.matmul(psB[s][:, :], Gw_lo[:, G_ZR, :], gT_hi[s][:, :], start=False, stop=True,
                                 skip_group_check=True).then_inc(product[s], 1)

            def stage_rh(s, r, k):
                pe.wait_ge(vector_done[s], VECTORS * r + VECTOR[f"rh{k}"])
                nc.tensor.matmul(psA[s][:, :], U5[:, :], rh[s], start=False, stop=True).then_inc(product[s], 1)

            def stage_t(s, r, k):
                pe.wait_ge(vector_done[s], VECTORS * r + VECTOR[f"h{k}"])
                transpose_tiles(psA[s], lambda t: H[s][:, t * P:(t + 1) * P]).then_inc(turned[s], 1)

            def rounds(exact):
                stages = {"x0": stage_x0, "query": stage_query, "scores01": stage_scores01, "scores23": stage_scores23,
                          "mix": stage_mix, "out0": stage_out0, "sums0": stage_sums0, "x1": stage_x1, "xh": stage_xh, "gates": stage_gates,
                          "turn_xh": stage_turn_xh, "agg": stage_agg, "sums1": stage_sums1, "recv": stage_recv, "self": stage_self, "out1": stage_out1, "x2": stage_x2,
                          "cheb01": stage_cheb01, "cheb23": stage_cheb23,
                          "lap1": lambda s, r: stage_lap1(s, r, exact), "lap2": lambda s, r: stage_lap2(s, r, exact), "x3": stage_x3}
                for k in range(STEPS):
                    stages[f"m{k}"] = lambda s, r, k=k: stage_m(s, r, k, exact)
                    stages[f"uh{k}"] = lambda s, r, k=k: stage_uh(s, r, k)
                    stages[f"r{k}"] = lambda s, r, k=k: stage_r(s, r, k)
                    stages[f"rh{k}"] = lambda s, r, k=k: stage_rh(s, r, k)
                    stages[f"v{k}"] = lambda s, r, k=k: stage_v(s, r, k)
                    stages[f"t{k}"] = lambda s, r, k=k: stage_t(s, r, k)
                run("tensor", stages, 0, first=True)
                with pe.Fori(1, ROUNDS) as r:
                    run("tensor", stages, r)
                run("tensor", stages, ROUNDS, last=True)

            with pe.If(inexact == 0):
                rounds(exact=True)
            with pe.Else():
                rounds(exact=False)


_INS = ["x", "adj", "L0_gnn_q", "L0_gnn_k", "L0_gnn_v", "L1_gnn_Wi", "L1_gnn_bi", "L1_gnn_We", "L1_gnn_be",
        "L1_gnn_Wn", "L1_gnn_bn", "L1_gnn_Wm", "L1_gnn_bm", "L2_gnn_weight", "L2_gnn_bias",
        "L3_gnn_w3_w", "L3_gnn_w3_b", "L3_gnn_u3_w", "L3_gnn_u3_b", "L3_gnn_w4_w", "L3_gnn_w4_b",
        "L3_gnn_w5_w", "L3_gnn_w5_b", "L3_gnn_u5_w", "L3_gnn_u5_b"]


def kernel(**inputs):
    import numpy as _np
    import concourse.bacc as _bacc
    from concourse import mybir as _mybir
    from concourse.bass_utils import run_bass_kernel_spmd as _run

    nc = _bacc.Bacc("TRN2", target_bir_lowering=False, num_devices=1)
    arrays, args = {}, []
    for name in _INS:
        a = _np.ascontiguousarray(inputs[name])
        arrays[f"in_{name}"] = a
        args.append(nc.dram_tensor(f"in_{name}", a.shape, _mybir.dt.from_np(a.dtype), kind="ExternalInput").ap())
    shape = _np.shape(inputs["x"])
    args.append(nc.dram_tensor("out_0", shape, _mybir.dt.float32, kind="ExternalOutput").ap())
    build(nc, *args)
    r = _run(nc, [arrays], core_ids=[0])
    return r.results[0]["out_0"]
```
